# Optimizing a Trainium2 kernel written in Bass

```python
import numpy as np
import jax
import jax.numpy as jnp

def _softmax(x, axis=-1):
    return jax.nn.softmax(x, axis=axis)

def _gelu(x):
    return jax.nn.gelu(x, approximate=True)

def _silu(x):
    return jax.nn.silu(x)

def _sigmoid(x):
    return jax.nn.sigmoid(x)

def _layernorm(x, axis=-1, eps=1e-05):
    m = jnp.mean(x, axis=axis, keepdims=True)
    v = jnp.var(x, axis=axis, keepdims=True)
    return (x - m) / jnp.sqrt(v + eps)

def _scatter_add(tgt, idx, src, axis=0):
    return tgt.at[idx].add(src)

def _segment_sum(src, seg, n):
    return jax.ops.segment_sum(src, seg, n)
kernel_name = 'mk_adaln_d2_jaxref_r8_a2eda2'

def setup_inputs(seed: int=0):
    np.random.seed(seed)
    _w = jnp.asarray

    def _L0_attn_setup():
        import jax, jax.numpy as jnp
        import numpy as np
        B, N, D = (2, 256, 128)
        H, QH, DH = (8, 16, 64)
        SOFTCLAMP = 50.0

        def _rmsnorm(x, w):
            eps = jnp.finfo(x.dtype).eps
            return x * jax.lax.rsqrt(jnp.mean(x * x, axis=-1, keepdims=True) + eps) * w

        def _l2norm(x):
            n = jnp.maximum(jnp.linalg.norm(x, axis=-1, keepdims=True), 1e-12)
            return x / n

        def _mh_rmsnorm(x, gamma):
            scale = (gamma + 1.0) * np.sqrt(x.shape[-1]).astype(np.float32)
            return _l2norm(x) * scale[None, :, None, :]
        key = jax.random.key(seed)
        ks = jax.random.split(key, 7)
        return {'tokens': jax.random.normal(ks[0], (B, N, D), jnp.float32), 'norm_w': jnp.ones((D,), jnp.float32) + 0.02 * jax.random.normal(ks[1], (D,), jnp.float32), 'Wq': 0.02 * jax.random.normal(ks[2], (D, QH * DH), jnp.float32), 'Wkv': 0.02 * jax.random.normal(ks[3], (D, 2 * H * DH), jnp.float32), 'Wout': 0.02 * jax.random.normal(ks[4], (H * DH, D), jnp.float32), 'q_gamma': 0.02 * jax.random.normal(ks[5], (QH, DH), jnp.float32), 'k_gamma': 0.02 * jax.random.normal(ks[6], (H, DH), jnp.float32)}
    _L0_attn_in = _L0_attn_setup()

    def _L0_ffn_setup():
        import jax, jax.numpy as jnp
        import numpy as np
        DIM = 128
        N_EXPERTS = 16
        TOP_K = 4
        N_GROUP = 4
        TOPK_GROUP = 2
        MOE_INTER = 64
        SHARED_INTER = 256
        ROUTED_SCALE = 2.5

        def relu2(x):
            return jnp.square(jax.nn.relu(x))

        def _router(x2, gate_w, bias_e):
            T = x2.shape[0]
            logits = x2 @ gate_w.T
            scores = jax.nn.sigmoid(logits)
            sc = jax.lax.stop_gradient(scores + bias_e[None, :])
            grp = sc.reshape(T, N_GROUP, N_EXPERTS // N_GROUP)
            top2, _ = jax.lax.top_k(grp, 2)
            group_scores = top2.sum(-1)
            _, gidx = jax.lax.top_k(group_scores, TOPK_GROUP)
            rows = jnp.arange(T)[:, None]
            gmask = jnp.zeros((T, N_GROUP), dtype=sc.dtype).at[rows, gidx].set(1.0)
            smask = jnp.repeat(gmask, N_EXPERTS // N_GROUP, axis=1)
            masked = jnp.where(smask > 0, sc, 0.0)
            _, topk_idx = jax.lax.top_k(masked, TOP_K)
            topk_w = jnp.take_along_axis(scores, topk_idx, axis=1)
            topk_w = topk_w / (topk_w.sum(-1, keepdims=True) + 1e-20)
            topk_w = topk_w * ROUTED_SCALE
            return (topk_idx, topk_w)
        key = jax.random.key(seed)
        ks = jax.random.split(key, 6)
        hidden_states = jax.random.normal(ks[0], (2, 256, DIM), dtype=jnp.float32)
        gate_w = jax.random.normal(ks[1], (N_EXPERTS, DIM), dtype=jnp.float32) * 0.02
        bias_e = jnp.zeros((N_EXPERTS,), dtype=jnp.float32)
        up_w = jax.random.normal(ks[2], (N_EXPERTS, MOE_INTER, DIM), dtype=jnp.float32) * 0.02
        down_w = jax.random.normal(ks[3], (N_EXPERTS, DIM, MOE_INTER), dtype=jnp.float32) * 0.02
        shared_up = jax.random.normal(ks[4], (SHARED_INTER, DIM), dtype=jnp.float32) * 0.02
        shared_down = jax.random.normal(ks[5], (DIM, SHARED_INTER), dtype=jnp.float32) * 0.02
        return {'hidden_states': hidden_states, 'gate_w': gate_w, 'bias_e': bias_e, 'up_w': up_w, 'down_w': down_w, 'shared_up': shared_up, 'shared_down': shared_down}
    _L0_ffn_in = _L0_ffn_setup()
    _L0_c = _w((lambda *s: np.random.randn(*s).astype(np.float32) * 0.05)(32, 128))
    _L0_wmod = _w((lambda *s: np.random.randn(*s).astype(np.float32) * 0.05)(128, 6 * 128) * 128 ** (-0.5))

    def _L1_attn_setup():
        import jax, jax.numpy as jnp
        import numpy as np
        D_MODEL, N_HEADS = (128, 16)
        D_H = D_MODEL // N_HEADS
        D_HR = D_H // 2
        D_LATENT = 32
        THETA = 10000.0

        def rope(x, theta=THETA):
            S, d = (x.shape[-2], x.shape[-1])
            inv = theta ** (-jnp.arange(0, d, 2, dtype=jnp.float32) / d)
            ang = jnp.arange(S, dtype=jnp.float32)[:, None] * inv
            cos, sin = (jnp.cos(ang), jnp.sin(ang))
            x1, x2 = (x[..., 0::2], x[..., 1::2])
            r1 = x1 * cos - x2 * sin
            r2 = x1 * sin + x2 * cos
            return jnp.stack([r1, r2], axis=-1).reshape(x.shape)
        key = jax.random.key(seed)
        ks = jax.random.split(key, 9)
        s = lambda fan_in: 1.0 / np.sqrt(fan_in)
        return {'x': jax.random.normal(ks[0], (4, 256, D_MODEL), jnp.float32), 'W_DQ': jax.random.normal(ks[1], (D_MODEL, D_LATENT), jnp.float32) * s(D_MODEL), 'W_UQ': jax.random.normal(ks[2], (D_LATENT, N_HEADS * D_H), jnp.float32) * s(D_LATENT), 'W_QR': jax.random.normal(ks[3], (D_LATENT, N_HEADS * D_HR), jnp.float32) * s(D_LATENT), 'W_DKV': jax.random.normal(ks[4], (D_MODEL, D_LATENT), jnp.float32) * s(D_MODEL), 'W_UK': jax.random.normal(ks[5], (D_LATENT, N_HEADS * D_H), jnp.float32) * s(D_LATENT), 'W_UV': jax.random.normal(ks[6], (D_LATENT, N_HEADS * D_H), jnp.float32) * s(D_LATENT), 'W_KR': jax.random.normal(ks[7], (D_MODEL, D_HR), jnp.float32) * s(D_MODEL), 'W_O': jax.random.normal(ks[8], (N_HEADS * D_H, D_MODEL), jnp.float32) * s(N_HEADS * D_H)}
    _L1_attn_in = _L1_attn_setup()

    def _L1_ffn_setup():
        import jax, jax.numpy as jnp
        import numpy as np
        D_IN, D_HID = (128, 512)

        def _ternary(key, shape):
            return jax.random.randint(key, shape, -1, 2).astype(jnp.float32)

        def _tlin(x, w, s):
            return jnp.einsum('bsi,oi->bso', x, w) * s
        key = jax.random.key(seed)
        ks = jax.random.split(key, 12)
        inv = lambda fan: 1.0 / np.sqrt(fan).astype(np.float32)
        return {'x': jax.random.normal(ks[0], (4, 256, D_IN), dtype=jnp.float32), 'w1_w': _ternary(ks[1], (D_HID, D_IN)), 'w1_s': jax.random.uniform(ks[2], (D_HID,), dtype=jnp.float32) * inv(D_IN), 'w2_w': _ternary(ks[3], (D_HID, D_IN)), 'w2_s': jax.random.uniform(ks[4], (D_HID,), dtype=jnp.float32) * inv(D_IN), 'h1_w': _ternary(ks[5], (D_HID, D_HID)), 'h1_s': jax.random.uniform(ks[6], (D_HID,), dtype=jnp.float32) * inv(D_HID), 'h2_w': _ternary(ks[7], (D_HID, D_HID)), 'h2_s': jax.random.uniform(ks[8], (D_HID,), dtype=jnp.float32) * inv(D_HID), 'w3_w': _ternary(ks[9], (D_IN, D_HID)), 'w3_s': jax.random.uniform(ks[10], (D_IN,), dtype=jnp.float32) * inv(D_HID)}
    _L1_ffn_in = _L1_ffn_setup()
    _L1_c = _w((lambda *s: np.random.randn(*s).astype(np.float32) * 0.05)(32, 128))
    _L1_wmod = _w((lambda *s: np.random.randn(*s).astype(np.float32) * 0.05)(128, 6 * 128) * 128 ** (-0.5))
    _d = {'L0_attn_tokens': _L0_attn_in['tokens'], 'L0_attn_norm_w': _L0_attn_in['norm_w'], 'L0_attn_Wq': _L0_attn_in['Wq'], 'L0_attn_Wkv': _L0_attn_in['Wkv'], 'L0_attn_Wout': _L0_attn_in['Wout'], 'L0_attn_q_gamma': _L0_attn_in['q_gamma'], 'L0_attn_k_gamma': _L0_attn_in['k_gamma'], 'L0_ffn_gate_w': _L0_ffn_in['gate_w'], 'L0_ffn_bias_e': _L0_ffn_in['bias_e'], 'L0_ffn_up_w': _L0_ffn_in['up_w'], 'L0_ffn_down_w': _L0_ffn_in['down_w'], 'L0_ffn_shared_up': _L0_ffn_in['shared_up'], 'L0_ffn_shared_down': _L0_ffn_in['shared_down'], 'L0_c': _L0_c, 'L0_wmod': _L0_wmod, 'L1_attn_W_DQ': _L1_attn_in['W_DQ'], 'L1_attn_W_UQ': _L1_attn_in['W_UQ'], 'L1_attn_W_QR': _L1_attn_in['W_QR'], 'L1_attn_W_DKV': _L1_attn_in['W_DKV'], 'L1_attn_W_UK': _L1_attn_in['W_UK'], 'L1_attn_W_UV': _L1_attn_in['W_UV'], 'L1_attn_W_KR': _L1_attn_in['W_KR'], 'L1_attn_W_O': _L1_attn_in['W_O'], 'L1_ffn_w1_w': _L1_ffn_in['w1_w'], 'L1_ffn_w1_s': _L1_ffn_in['w1_s'], 'L1_ffn_w2_w': _L1_ffn_in['w2_w'], 'L1_ffn_w2_s': _L1_ffn_in['w2_s'], 'L1_ffn_h1_w': _L1_ffn_in['h1_w'], 'L1_ffn_h1_s': _L1_ffn_in['h1_s'], 'L1_ffn_h2_w': _L1_ffn_in['h2_w'], 'L1_ffn_h2_s': _L1_ffn_in['h2_s'], 'L1_ffn_w3_w': _L1_ffn_in['w3_w'], 'L1_ffn_w3_s': _L1_ffn_in['w3_s'], 'L1_c': _L1_c, 'L1_wmod': _L1_wmod}
    _x0 = _d['L0_attn_tokens']
    _d['L0_attn_tokens'] = jax.random.normal(jax.random.fold_in(jax.random.key(seed), 1), (32, 256, 128), dtype=_x0.dtype)
    del _x0
    return _d

def reference(L0_attn_tokens, L0_attn_norm_w, L0_attn_Wq, L0_attn_Wkv, L0_attn_Wout, L0_attn_q_gamma, L0_attn_k_gamma, L0_ffn_gate_w, L0_ffn_bias_e, L0_ffn_up_w, L0_ffn_down_w, L0_ffn_shared_up, L0_ffn_shared_down, L0_c, L0_wmod, L1_attn_W_DQ, L1_attn_W_UQ, L1_attn_W_QR, L1_attn_W_DKV, L1_attn_W_UK, L1_attn_W_UV, L1_attn_W_KR, L1_attn_W_O, L1_ffn_w1_w, L1_ffn_w1_s, L1_ffn_w2_w, L1_ffn_w2_s, L1_ffn_h1_w, L1_ffn_h1_s, L1_ffn_h2_w, L1_ffn_h2_s, L1_ffn_w3_w, L1_ffn_w3_s, L1_c, L1_wmod):

    def _L0_attn_ref(tokens, norm_w, Wq, Wkv, Wout, q_gamma, k_gamma):
        import jax, jax.numpy as jnp
        import numpy as np
        B, N, D = (2, 256, 128)
        H, QH, DH = (8, 16, 64)
        SOFTCLAMP = 50.0

        def _rmsnorm(x, w):
            eps = jnp.finfo(x.dtype).eps
            return x * jax.lax.rsqrt(jnp.mean(x * x, axis=-1, keepdims=True) + eps) * w

        def _l2norm(x):
            n = jnp.maximum(jnp.linalg.norm(x, axis=-1, keepdims=True), 1e-12)
            return x / n

        def _mh_rmsnorm(x, gamma):
            scale = (gamma + 1.0) * np.sqrt(x.shape[-1]).astype(np.float32)
            return _l2norm(x) * scale[None, :, None, :]
        b, n, d = tokens.shape
        x = _rmsnorm(tokens, norm_w)
        q = (x @ Wq).reshape(b, n, QH, DH).transpose(0, 2, 1, 3)
        kv = x @ Wkv
        k = kv[..., :H * DH].reshape(b, n, H, DH).transpose(0, 2, 1, 3)
        v = kv[..., H * DH:].reshape(b, n, H, DH).transpose(0, 2, 1, 3)
        q = _mh_rmsnorm(q, q_gamma)
        k = _mh_rmsnorm(k, k_gamma)
        g = QH // H
        q = q.reshape(b, H, g, n, DH)
        sim = jnp.einsum('bhgid,bhjd->bhgij', q, k)
        sim = jnp.tanh(sim / SOFTCLAMP) * SOFTCLAMP
        sim = sim * DH ** (-0.5)
        neg = -jnp.finfo(sim.dtype).max
        causal = jnp.triu(jnp.ones((n, n), dtype=bool), 1)
        sim = jnp.where(causal, neg, sim)
        attn = jax.nn.softmax(sim, axis=-1)
        out = jnp.einsum('bhgij,bhjd->bhid', attn, v)
        out = out.transpose(0, 2, 1, 3).reshape(b, n, H * DH)
        return out @ Wout

    def _L0_ffn_ref(hidden_states, gate_w, bias_e, up_w, down_w, shared_up, shared_down):
        import jax, jax.numpy as jnp
        import numpy as np
        DIM = 128
        N_EXPERTS = 16
        TOP_K = 4
        N_GROUP = 4
        TOPK_GROUP = 2
        MOE_INTER = 64
        SHARED_INTER = 256
        ROUTED_SCALE = 2.5

        def relu2(x):
            return jnp.square(jax.nn.relu(x))

        def _router(x2, gate_w, bias_e):
            T = x2.shape[0]
            logits = x2 @ gate_w.T
            scores = jax.nn.sigmoid(logits)
            sc = jax.lax.stop_gradient(scores + bias_e[None, :])
            grp = sc.reshape(T, N_GROUP, N_EXPERTS // N_GROUP)
            top2, _ = jax.lax.top_k(grp, 2)
            group_scores = top2.sum(-1)
            _, gidx = jax.lax.top_k(group_scores, TOPK_GROUP)
            rows = jnp.arange(T)[:, None]
            gmask = jnp.zeros((T, N_GROUP), dtype=sc.dtype).at[rows, gidx].set(1.0)
            smask = jnp.repeat(gmask, N_EXPERTS // N_GROUP, axis=1)
            masked = jnp.where(smask > 0, sc, 0.0)
            _, topk_idx = jax.lax.top_k(masked, TOP_K)
            topk_w = jnp.take_along_axis(scores, topk_idx, axis=1)
            topk_w = topk_w / (topk_w.sum(-1, keepdims=True) + 1e-20)
            topk_w = topk_w * ROUTED_SCALE
            return (topk_idx, topk_w)
        B, S, D = hidden_states.shape
        x2 = hidden_states.reshape(-1, D)
        T = x2.shape[0]
        topk_idx, topk_w = _router(x2, gate_w, bias_e)
        rows = jnp.arange(T)[:, None]
        combine = jnp.zeros((T, N_EXPERTS), dtype=topk_w.dtype).at[rows, topk_idx].add(topk_w)

        def body(acc, inp):
            wu, wd, cw = inp
            y = relu2(x2 @ wu.T) @ wd.T
            return (acc + cw[:, None] * y, None)
        routed, _ = jax.lax.scan(body, jnp.zeros_like(x2), (up_w, down_w, combine.T))
        shared = relu2(x2 @ shared_up.T) @ shared_down.T
        out = routed + shared
        return out.reshape(B, S, D)

    def _L1_attn_ref(x, W_DQ, W_UQ, W_QR, W_DKV, W_UK, W_UV, W_KR, W_O):
        import jax, jax.numpy as jnp
        import numpy as np
        D_MODEL, N_HEADS = (128, 16)
        D_H = D_MODEL // N_HEADS
        D_HR = D_H // 2
        D_LATENT = 32
        THETA = 10000.0

        def rope(x, theta=THETA):
            S, d = (x.shape[-2], x.shape[-1])
            inv = theta ** (-jnp.arange(0, d, 2, dtype=jnp.float32) / d)
            ang = jnp.arange(S, dtype=jnp.float32)[:, None] * inv
            cos, sin = (jnp.cos(ang), jnp.sin(ang))
            x1, x2 = (x[..., 0::2], x[..., 1::2])
            r1 = x1 * cos - x2 * sin
            r2 = x1 * sin + x2 * cos
            return jnp.stack([r1, r2], axis=-1).reshape(x.shape)
        B, S, _ = x.shape
        d_qk = D_H + D_HR
        c_q = x @ W_DQ
        Qc = (c_q @ W_UQ).reshape(B, S, N_HEADS, D_H).transpose(0, 2, 1, 3)
        Qr = (c_q @ W_QR).reshape(B, S, N_HEADS, D_HR).transpose(0, 2, 1, 3)
        Qr = rope(Qr)
        c_kv = x @ W_DKV
        Kc = (c_kv @ W_UK).reshape(B, S, N_HEADS, D_H).transpose(0, 2, 1, 3)
        Kr = rope((x @ W_KR)[:, None, :, :])
        Kr = jnp.broadcast_to(Kr, (B, N_HEADS, S, D_HR))
        V = (c_kv @ W_UV).reshape(B, S, N_HEADS, D_H).transpose(0, 2, 1, 3)
        Q = jnp.concatenate([Qc, Qr], axis=-1)
        K = jnp.concatenate([Kc, Kr], axis=-1)
        scores = jnp.einsum('bhqd,bhkd->bhqk', Q, K)
        scores = jnp.clip(scores, -80.0, 80.0)
        causal = jnp.tril(jnp.ones((S, S), dtype=bool))
        scores = jnp.where(causal, scores, -jnp.inf)
        weights = jax.nn.softmax(scores / jnp.sqrt(jnp.float32(d_qk)), axis=-1)
        attn = jnp.einsum('bhqk,bhkd->bhqd', weights, V)
        attn = attn.transpose(0, 2, 1, 3).reshape(B, S, N_HEADS * D_H)
        return attn @ W_O

    def _L1_ffn_ref(x, w1_w, w1_s, w2_w, w2_s, h1_w, h1_s, h2_w, h2_s, w3_w, w3_s):
        import jax, jax.numpy as jnp
        import numpy as np
        D_IN, D_HID = (128, 512)

        def _ternary(key, shape):
            return jax.random.randint(key, shape, -1, 2).astype(jnp.float32)

        def _tlin(x, w, s):
            return jnp.einsum('bsi,oi->bso', x, w) * s
        h = jax.nn.silu(_tlin(x, w1_w, w1_s)) * _tlin(x, w2_w, w2_s)
        h = jax.nn.gelu(_tlin(h, h1_w, h1_s), approximate=False)
        h = jax.nn.gelu(_tlin(h, h2_w, h2_s), approximate=False)
        return _tlin(h, w3_w, w3_s)
    x = L0_attn_tokens
    mod = (_silu(L0_c) @ L0_wmod).reshape(L0_c.shape[0], 6, 1, -1)
    sa, ca, ga, sb, cb, gb = (mod[:, 0], mod[:, 1], mod[:, 2], mod[:, 3], mod[:, 4], mod[:, 5])
    ga = (2 * (ga >= 0) - 1) * jnp.maximum(jnp.abs(ga), 0.25)
    gb = (2 * (gb >= 0) - 1) * jnp.maximum(jnp.abs(gb), 0.25)
    h = _layernorm(x, axis=-1) * (1 + ca) + sa
    x = x + ga * _L0_attn_ref(h, L0_attn_norm_w, L0_attn_Wq, L0_attn_Wkv, L0_attn_Wout, L0_attn_q_gamma, L0_attn_k_gamma)
    h = _layernorm(x, axis=-1) * (1 + cb) + sb
    x = x + gb * _L0_ffn_ref(h, L0_ffn_gate_w, L0_ffn_bias_e, L0_ffn_up_w, L0_ffn_down_w, L0_ffn_shared_up, L0_ffn_shared_down)
    mod = (_silu(L1_c) @ L1_wmod).reshape(L1_c.shape[0], 6, 1, -1)
    sa, ca, ga, sb, cb, gb = (mod[:, 0], mod[:, 1], mod[:, 2], mod[:, 3], mod[:, 4], mod[:, 5])
    ga = (2 * (ga >= 0) - 1) * jnp.maximum(jnp.abs(ga), 0.25)
    gb = (2 * (gb >= 0) - 1) * jnp.maximum(jnp.abs(gb), 0.25)
    h = _layernorm(x, axis=-1) * (1 + ca) + sa
    x = x + ga * _L1_attn_ref(h, L1_attn_W_DQ, L1_attn_W_UQ, L1_attn_W_QR, L1_attn_W_DKV, L1_attn_W_UK, L1_attn_W_UV, L1_attn_W_KR, L1_attn_W_O)
    h = _layernorm(x, axis=-1) * (1 + cb) + sb
    x = x + gb * _L1_ffn_ref(h, L1_ffn_w1_w, L1_ffn_w1_s, L1_ffn_w2_w, L1_ffn_w2_s, L1_ffn_h1_w, L1_ffn_h1_s, L1_ffn_h2_w, L1_ffn_h2_s, L1_ffn_w3_w, L1_ffn_w3_s)
    return x

_drawn_inputs = setup_inputs


def setup_inputs(seed=0):
    import zlib

    import numpy as np

    out = dict(_drawn_inputs(seed))
    spreads = {'L0_ffn_bias_e': (0.0, 0.1)}
    factors = {}
    for name, (base, spread) in spreads.items():
        noise = np.random.default_rng([zlib.crc32(name.encode()), seed]).standard_normal(out[name].shape)
        drawn = base * np.exp(spread * noise) if base else spread * noise
        out[name] = jnp.asarray(drawn.astype(out[name].dtype))
    for name, factor in factors.items():
        out[name] = (out[name] * factor).astype(out[name].dtype)
    return out
```

```python
from contextlib import ExitStack

import numpy as np

import concourse.bass as bass
from concourse import mybir

F32 = mybir.dt.float32
F16 = mybir.dt.float16
I32 = mybir.dt.int32
ALU = mybir.AluOpType
ACT = mybir.ActivationFunctionType
AX = mybir.AxisListType

P = 128
B, N, D = 32, 256, 128
TT = N // P
TILES = B * TT
LN_EPS = 1e-5
QH, KH, DH = 16, 8, 64
G2 = QH // KH
HPG = 4
GROUPS = QH // HPG
QW, KW = QH * DH, KH * DH
VC = 96
RMS_EPS = float(np.finfo(np.float32).eps)
SOFTCLAMP = 50.0
E, EI, SI = 16, 64, 256
NG, EG = 4, 4
TOPG, TOPK, ROUTED = 2, 4, 2.5
H1, DC, DR, LAT = 16, 8, 4, 32
DQ = DC + DR
CLIP = 80.0
HID = 512
BANK = 512


class Signal:

    def __init__(self, nc, ctx, name, per=1):
        self.sem, self.per, self.name = ctx.enter_context(nc.semaphore(name)), per, name

    def up(self, instruction, by=1):
        instruction.then_inc(self.sem, by)

    def wait(self, engine, n, k=None):
        value = n * self.per + (self.per if k is None else k)
        if isinstance(value, int) and value <= 0:
            return
        engine.wait_ge(self.sem, value)

    def wait_apart(self, engine, n, k=None):
        self.wait(engine, n, k)
        engine.nop(nofuse=True)


class Chain:

    def __init__(self, nc, ctx, name, per):
        self.raised, self.k = Signal(nc, ctx, name, per), 0

    def begin(self, engine, n):
        self.engine, self.n, self.k = engine, n, 0

    def step(self, instruction):
        self.k += 1
        self.raised.up(instruction)
        self.raised.wait(self.engine, self.n, self.k)

    def end(self):
        assert self.k == self.raised.per, (self.raised.name, self.k)


class Steps:

    def __init__(self, nc, ctx, name):
        self.sem, self.k = ctx.enter_context(nc.semaphore(name)), 0

    def on(self, engine):
        def step(instruction):
            self.k += 1
            instruction.then_inc(self.sem, 1)
            engine.wait_ge(self.sem, self.k)
        return step


RSQRT_STEPS = 12


def rsqrt(step, dve, y, v, tmp, half):
    step(dve.tensor_scalar(tmp.bitcast(I32), v.bitcast(I32), 1, None, ALU.logical_shift_right))
    step(dve.tensor_scalar(y.bitcast(I32), tmp.bitcast(I32), -1.0, float(0x5F3759DF), ALU.mult, ALU.add))
    step(dve.tensor_scalar(half, v, -0.5, None, ALU.mult))
    for _ in range(3):
        step(dve.tensor_tensor(tmp, y, y, ALU.mult))
        step(dve.tensor_tensor(tmp, tmp, half, ALU.mult))
        step(dve.scalar_tensor_tensor(y, tmp, 1.5, y, ALU.add, ALU.mult))


class Core:

    def __init__(self, nc, ctx):
        def sb(name, shape, dt=F32):
            return ctx.enter_context(nc.sbuf_tensor(name, shape, dt))
        self.x = sb("x", [P, TILES, D])
        self.mv = sb("mv", [P, TILES, 2])
        self.rs = sb("rs", [P, TILES])
        self.var = sb("var", [P, TILES])
        self.tmp = sb("ln_tmp", [P, TILES])
        self.half = sb("ln_half", [P, TILES])
        self.stat = sb("stat", [P, TT * TT, 6])
        self.agg = sb("agg", [P, TT * TT, 2])
        self.mod = sb("mod", [P, 2, 6, B])
        self.id32 = sb("id32", [P, P])
        self.id16 = sb("id16", [P, P], F16)


LN_STEPS = 1 + RSQRT_STEPS


def ln_scales(step, dve, c):
    step(dve.tensor_scalar(c.var[:, :], c.mv[:, :, 1], LN_EPS, None, ALU.add))
    rsqrt(step, dve, c.rs[:, :], c.var[:, :], c.tmp[:, :], c.half[:, :])


def normalise(dve, c, out, tile):
    return dve.tensor_scalar(out, c.x[:, bass.ds(tile, 1), :].rearrange("p a d -> p (a d)"),
                             c.mv[:, bass.ds(tile, 1), 0], c.rs[:, bass.ds(tile, 1)],
                             ALU.subtract, ALU.mult)


def x_tiles(c, tile, count):
    return c.x[:, bass.ds(tile, count), :]


ADD_STEPS = 4


def add_and_measure(dve, c, s_st, n, tiles, out):
    xt = x_tiles(c, n * tiles, tiles)
    s_st.up(dve.tensor_tensor(xt, xt, out.rearrange("p (t d) -> p t d", t=tiles), ALU.add))
    s_st.wait_apart(dve, n, 1)
    for t in range(tiles):
        last = dve.bn_stats(c.stat[:, t, :], x_tiles(c, n * tiles + t, 1).rearrange("p a d -> p (a d)"))
    s_st.up(last)
    s_st.wait_apart(dve, n, 2)
    for t in range(tiles):
        last = dve.bn_aggr(c.agg[:, t, :], c.stat[:, t, :])
    s_st.up(last)
    s_st.wait(dve, n, 3)
    s_st.up(dve.tensor_copy(c.mv[:, bass.ds(n * tiles, tiles), :], c.agg[:, 0:tiles, :]))


def setup(nc, c, ins):
    with ExitStack() as ctx:
        def sb(name, shape, dt=F32):
            return ctx.enter_context(nc.sbuf_tensor(name, shape, dt))
        CH = 8
        TC = TILES // CH
        cin = [sb(f"cin{l}", [B, D]) for l in range(2)]
        sg = [sb(f"sg{l}", [B, D]) for l in range(2)]
        wmod = [sb(f"wmod{l}", [D, 6 * D]) for l in range(2)]
        cT = sb("cT", [D, 2, B])
        sgn, mag = sb("sgn", [P, B]), sb("mag", [P, B])
        st = sb("st", [P, TILES, 6])
        psc = ctx.enter_context(nc.psum_tensor("psc", [D, BANK], F32))
        psm = [ctx.enter_context(nc.psum_tensor(f"psm{l}", [D, BANK], F32)) for l in range(2)]
        s_c = [Signal(nc, ctx, f"su_c{l}", 32) for l in range(2)]
        s_x = [Signal(nc, ctx, f"su_x{k}", 16) for k in range(CH)]
        s_id = Signal(nc, ctx, "su_id", 4)
        s_exp = Signal(nc, ctx, "su_exp", 2)
        s_silu = Signal(nc, ctx, "su_silu", 1)
        s_cT = Signal(nc, ctx, "su_cT", 1)
        s_cTs = Signal(nc, ctx, "su_cTs", 1)
        s_mod = Signal(nc, ctx, "su_mod", 1)
        s_st = Signal(nc, ctx, "su_st", 1)
        steps = Steps(nc, ctx, "su_dve")
        x_dram = ins["L0_attn_tokens"].rearrange("b (t p) d -> p (b t) d", p=P)
        block = ctx.enter_context(nc.Block())

        @block.sync
        def _(sp):
            for l in range(2):
                s_c[l].up(sp.dma_start(cin[l][:, :], ins[f"L{l}_c"]), 16)
                s_c[l].up(sp.dma_start(wmod[l][:, :], ins[f"L{l}_wmod"]), 16)
            for k in range(CH):
                s_x[k].up(sp.dma_start(c.x[:, k * TC:(k + 1) * TC, :], x_dram[:, k * TC:(k + 1) * TC, :]), 16)

        @block.gpsimd
        def _(gp):
            s_id.up(gp.memset(c.id32[:, :], 0.0))
            s_id.up(gp.memset(c.id16[:, :], 0.0))
            s_id.wait(gp, 0, 2)
            for m in (c.id32, c.id16):
                s_id.up(gp.affine_select(out=m[:, :], in_=m[:, :], compare_op=ALU.not_equal, fill=1.0,
                                         base=0, pattern=[[-1, P]], channel_multiplier=1))

        @block.scalar
        def _(act):
            for l in range(2):
                s_c[l].wait(act, 0)
                s_exp.up(act.activation(sg[l][:, :], cin[l][:, :], ACT.Exp, scale=-1.0))

        @block.tensor
        def _(pe):
            s_id.wait(pe, 0)
            s_silu.wait(pe, 0)
            for l in range(2):
                last = pe.transpose(psc[:, l * B:(l + 1) * B], sg[l][:, :], c.id32[0:B, 0:B])
            s_cT.up(last)
            s_cTs.wait(pe, 0)
            for l in range(2):
                s_c[l].wait(pe, 0)
                for j in range(6):
                    last = pe.matmul(psm[l][:, j * B:(j + 1) * B], wmod[l][:, j * D:(j + 1) * D],
                                     cT[:, l, :], start=True, stop=True)
            s_mod.up(last)

        @block.vector
        def _(dve):
            step = steps.on(dve)
            for l in range(2):
                s_exp.wait(dve, 0, l + 1)
                step(dve.tensor_scalar(sg[l][:, :], sg[l][:, :], 1.0, None, ALU.add))
                step(dve.reciprocal(sg[l][:, :], sg[l][:, :]))
                last = dve.tensor_tensor(sg[l][:, :], sg[l][:, :], cin[l][:, :], ALU.mult)
                if l == 0:
                    step(last)
            s_silu.up(last)
            s_cT.wait(dve, 0)
            s_cTs.up(dve.tensor_copy(cT[:, :, :].rearrange("p l b -> p (l b)"), psc[:, 0:2 * B]))
            s_mod.wait(dve, 0)
            for l in range(2):
                out, got = c.mod[:, l, :, :], psm[l][:, 0:6 * B].rearrange("p (j b) -> p j b", j=6)
                for j in (0, 3):
                    step(dve.tensor_copy(out[:, j, :], got[:, j, :]))
                    step(dve.tensor_scalar(out[:, j + 1, :], got[:, j + 1, :], 1.0, None, ALU.add))
                    step(dve.tensor_scalar(sgn[:, :], got[:, j + 2, :], 0.0, 2.0, ALU.is_ge, ALU.mult))
                    step(dve.tensor_copy(mag[:, :], got[:, j + 2, :]))
                    step(dve.scalar_tensor_tensor(mag[:, :], mag[:, :], -1.0, mag[:, :], ALU.mult, ALU.max))
                    step(dve.tensor_scalar(mag[:, :], mag[:, :], 0.25, None, ALU.max))
                    step(dve.scalar_tensor_tensor(out[:, j + 2, :], sgn[:, :], -1.0, mag[:, :], ALU.add, ALU.mult))
            for t in range(TILES):
                if t % TC == 0:
                    s_x[t // TC].wait(dve, 0)
                last = dve.bn_stats(st[:, t, :], c.x[:, t, :])
            s_st.up(last)
            s_st.wait(dve, 0)
            for t in range(TILES):
                last = dve.bn_aggr(c.mv[:, t, :], st[:, t, :])
            step(last)
            ln_scales(step, dve, c)


def attention0(nc, c, ins):
    with ExitStack() as ctx:
        def sb(name, shape, dt=F32):
            return ctx.enter_context(nc.sbuf_tensor(name, shape, dt))

        def sig(name, per=1):
            return Signal(nc, ctx, "a_" + name, per)
        wq, wkv = sb("wq", [D, QW]), sb("wkv", [D, 2 * KW])
        wo = sb("wo", [P, KW // P, D])
        nw = sb("nw", [D, 1])
        gam = sb("gam", [P, QW + KW])
        gk = sb("gk", [P, KW])
        ones = sb("ones", [P, 1])
        xn, hT, hsq = sb("xn", [P, TT, D]), sb("hT", [D, N]), sb("hsq", [D, N])
        sq = sb("sq", [P, QW + KW])
        qg = sb("qg", [P, TT, QW + KW])
        heads = QH + KH
        ss = sb("ss", [P, TT * heads + TT])
        rr, rtmp, rhalf = (sb(x, [P, TT * heads + TT]) for x in ("rr", "rtmp", "rhalf"))
        rlim = sb("rlim", [P, TT])
        rv = sb("rv", [P, TT])
        qp = sb("qp", [P, TT, QH, 2 * DH], F16)
        kp = sb("kp", [P, TT, KH, 3 * DH], F16)
        qs = sb("qs", [P, QH, N], F16)
        k1, k2 = sb("k1", [P, KH, N], F16), sb("k2", [P, KH, N], F16)
        va = sb("va", [P, TT, KH, VC])
        SC = HPG * (N + P)
        th = sb("th", [P, SC])
        pr = [sb(f"pr{k}", [P, SC]) for k in range(2)]
        rl = sb("rl", [P, TT, HPG])
        on = [sb(f"on{k}", [P, TT, HPG, DH]) for k in range(2)]
        as_ = sb("as", [P, TT, KW])
        at = sb("at", [P, KW // P, N])
        og = sb("og", [D, N])
        pS = ctx.enter_context(nc.psum_tensor("a_pS", [P, 3 * BANK], F32))
        pO = ctx.enter_context(nc.psum_tensor("a_pO", [P, TT, BANK], F32))
        pW = ctx.enter_context(nc.psum_tensor("a_pW", [P, 3, BANK], F32))

        s_w = Signal(nc, ctx, "a_w", 16 * 6)
        s_ones = sig("ones")
        s_prep = sig("prep")
        steps = Steps(nc, ctx, "a_steps")
        s_aT, s_at, s_o, s_og, s_oT, s_x, s_st = (
            sig(x, p) for x, p in (("aT", 2), ("at", 2), ("o", 1), ("og", 1), ("oT", 1), ("x", 1), ("st", ADD_STEPS)))
        s_sc, s_th, s_pr, s_mk, s_pv, s_rl, s_on, s_as = (
            sig(x, GROUPS) for x in ("sc", "th", "pr", "mk", "pv", "rl", "on", "as"))
        s_xn, s_xT, s_hT, s_hsq, s_ms, s_msv = (sig(x) for x in ("xn", "xT", "hT", "hsq", "ms", "msv"))
        s_qk, s_sq, s_qg, s_ss, s_qn, s_hi = (sig(x, TT) for x in ("qk", "sq", "qg", "ss", "qn", "hi"))
        s_lo = sig("lo", TT)
        s_tr, s_trv = sig("tr", 8), sig("trv", 4)
        s_trk = sig("trk", 4)
        s_v, s_va = sig("v", TT), sig("va", TT)
        chain = Chain(nc, ctx, "a_rs", RSQRT_STEPS + 1 + TT)

        block = ctx.enter_context(nc.Block())

        @block.sync
        def _(sp):
            for to, of in ((wq[:, :], ins["L0_attn_Wq"]), (wkv[:, :], ins["L0_attn_Wkv"]),
                           (wo[:, :, :], ins["L0_attn_Wout"].rearrange("(j p) n -> p j n", p=P)),
                           (nw[:, :], ins["L0_attn_norm_w"].rearrange("(p a) -> p a", a=1)),
                           (gam[:, 0:QW], ins["L0_attn_q_gamma"].rearrange("h d -> (h d)").partition_broadcast(P)),
                           (gk[:, :], ins["L0_attn_k_gamma"].rearrange("h d -> (h d)").partition_broadcast(P))):
                s_w.up(sp.dma_start(to, of), 16)

        def pe_transpose_x(pe, n):
            s_xn.wait(pe, n)
            s_va.wait(pe, n - 1)
            for t in range(TT):
                last = pe.transpose(pW[:, 0, t * P:(t + 1) * P], xn[:, t, :], c.id32[:, :])
            s_xT.up(last)

        def pe_mean_square(pe, n):
            s_hsq.wait(pe, n)
            s_hT.wait(pe, n)
            for t in range(TT):
                last = pe.matmul(pW[:, 0, t:t + 1], hsq[:, t * P:(t + 1) * P], ones[:, :], start=True, stop=True)
            s_ms.up(last)

        def pe_project_qk(pe, n, t):
            if t == 0:
                s_hT.wait(pe, n)
                s_msv.wait(pe, n)
                s_at.wait(pe, n - 2, 2)
            else:
                s_qg.wait(pe, n, t)
            h = hT[:, t * P:(t + 1) * P]
            for j in range(2):
                pe.matmul(pW[:, j, :], h, wq[:, j * BANK:(j + 1) * BANK], start=True, stop=True)
            s_qk.up(pe.matmul(pW[:, 2, :], h, wkv[:, 0:KW], start=True, stop=True))

        def pe_split_transposes(pe, n):
            for t in range(TT):
                s_hi.wait(pe, n, t + 1)
                s_lo.wait(pe, n, t + 1)
                for u in range(4):
                    m = 4 * t + u
                    if m < 3:
                        (s_og if m == 0 else s_st).wait(pe, n - 2, 1)
                        s_qg.wait(pe, n)
                    else:
                        b = m - 3
                        if b % 4 < 2:
                            s_trv.wait(pe, n, 2 * (b // 4) + b % 4 + 1)
                        else:
                            s_trk.wait(pe, n, 2 * (b // 4) + b % 4 - 1)
                    bank = pW[:, m % 3, :].bitcast(F16)
                    for j in range(8):
                        src = (qp[:, t, 8 * u + j, :] if u < 2 else
                               kp[:, t, j, (u - 2) * DH:(u - 2) * DH + 2 * DH])
                        last = pe.transpose(bank[:, j * P:(j + 1) * P], src, c.id16[:, :])
                    s_tr.up(last)

        def pe_values(pe, n):
            s_trk.wait(pe, n, 4)
            s_trv.wait(pe, n, 4)
            for t in range(TT):
                s_v.up(pe.matmul(pW[:, 2 - 2 * t, :], hT[:, t * P:(t + 1) * P], wkv[:, KW:2 * KW],
                                 start=True, stop=True))

        def pe_scores(pe, n, g):
            if g == 0:
                s_trv.wait(pe, n)
                s_trk.wait(pe, n)
            s_th.wait(pe, n - 1 if g == 0 else n, GROUPS if g == 0 else g)
            for hh in range(HPG):
                h = g * HPG + hh
                for out, keys, i0 in ((pS[:, hh * N:(hh + 1) * N], 0, 0),
                                      (pS[:, HPG * N + hh * P:HPG * N + (hh + 1) * P], 1, P)):
                    for first, k in ((True, k1), (False, k2)):
                        last = pe.matmul(out, k[:, h // G2, keys * P:(keys + 1) * P], qs[:, h, i0:N],
                                         start=first, stop=not first)
            s_sc.up(last)

        def pe_weighted_values(pe, n, g):
            if g == 0:
                s_va.wait(pe, n)
            s_mk.wait(pe, n, g + 1)
            s_on.wait(pe, n - 1 if g == 0 else n, GROUPS if g == 0 else g)
            p = pr[g % 2]
            for hh in range(HPG):
                v = (g * HPG + hh) // G2
                for t in range(TT):
                    out = pO[:, t, hh * VC:(hh + 1) * VC]
                    pe.matmul(out, p[:, hh * N + t * P:hh * N + (t + 1) * P], va[:, 0, v, :],
                              start=True, stop=t == 0)
                last = pe.matmul(out, p[:, HPG * N + hh * P:HPG * N + (hh + 1) * P], va[:, 1, v, :],
                                 start=False, stop=True)
            s_pv.up(last)

        def pe_out_transposes(pe, n, last_run=False):
            s_as.wait(pe, n)
            if last_run:
                s_st.wait(pe, n - 1, 1)
            else:
                s_va.wait(pe, n + 1)
            for t in range(TT):
                for j in range(KW // P):
                    last = pe.transpose(pW[:, 1 + t, j * P:(j + 1) * P], as_[:, t, j * P:(j + 1) * P], c.id32[:, :])
                s_aT.up(last)

        def pe_out_project(pe, n, last_run):
            s_at.wait(pe, n)
            if not last_run:
                s_qg.wait(pe, n + 2)
            for j in range(KW // P):
                last = pe.matmul(pW[:, 0, 0:N], wo[:, j, :], at[:, j, :], start=j == 0, stop=j == KW // P - 1)
            s_o.up(last)

        def pe_out_back(pe, n):
            s_og.wait(pe, n)
            for t in range(TT):
                last = pe.transpose(pW[:, 1, t * P:(t + 1) * P], og[:, t * P:(t + 1) * P], c.id32[:, :])
            s_oT.up(last)

        def pe_run(pe, n, tail=True, front=True):
            pe_scores(pe, n, 0)
            if front:
                pe_transpose_x(pe, n + 1)
            if tail:
                pe_out_transposes(pe, n - 1)
            if front:
                pe_mean_square(pe, n + 1)
            pe_scores(pe, n, 1)
            if front:
                pe_project_qk(pe, n + 1, 0)
            pe_weighted_values(pe, n, 0)
            if front:
                pe_project_qk(pe, n + 1, 1)
            pe_scores(pe, n, 2)
            pe_weighted_values(pe, n, 1)
            if tail:
                pe_out_project(pe, n - 1, not front)
            pe_scores(pe, n, 3)
            pe_weighted_values(pe, n, 2)
            if tail:
                pe_out_back(pe, n - 1)
            pe_weighted_values(pe, n, 3)
            if front:
                pe_split_transposes(pe, n + 1)
                pe_values(pe, n + 1)

        @block.tensor
        def _(pe):
            s_prep.wait(pe, 0)
            pe_transpose_x(pe, 0)
            pe_mean_square(pe, 0)
            pe_project_qk(pe, 0, 0)
            pe_project_qk(pe, 0, 1)
            pe_split_transposes(pe, 0)
            pe_values(pe, 0)
            pe_run(pe, 0, tail=False)
            with pe.Fori(1, B - 1) as n:
                pe_run(pe, n)
            pe_run(pe, B - 1, front=False)
            pe_out_transposes(pe, B - 1, True)
            pe_out_project(pe, B - 1, True)
            pe_out_back(pe, B - 1)

        def dve_modulate(dve, n):
            s_xT.wait(dve, n - 1)
            for t in range(TT):
                last = normalise(dve, c, xn[:, t, :], n * TT + t)
            s_xn.up(last)
            s_xT.wait(dve, n)
            s_v.wait(dve, n - 1)
            s_hT.up(dve.tensor_scalar(hT[:, :], pW[:, 0, 0:N], c.mod[:, 0, 1, bass.ds(n, 1)],
                                      c.mod[:, 0, 0, bass.ds(n, 1)], ALU.mult, ALU.add))

        def dve_mean_square(dve, n):
            s_ms.wait(dve, n)
            chain.raised.wait(dve, n - 1)
            s_msv.up(dve.tensor_scalar(ss[:, TT * heads:], pW[:, 0, 0:TT], RMS_EPS, None, ALU.add))

        def dve_gains(dve, n, t):
            s_sq.wait(dve, n, t + 1)
            s_hi.wait(dve, n - 1)
            s_lo.wait(dve, n - 1)
            s_qg.up(dve.tensor_tensor(qg[:, t, :], pW[:, :, :].rearrange("p b w -> p (b w)"), gam[:, :], ALU.mult))
            s_ss.up(dve.tensor_reduce(ss[:, t * heads:(t + 1) * heads],
                                      sq[:, :].rearrange("p (h d) -> p h d", d=DH), AX.X, ALU.add))

        def dve_norms(dve, n):
            chain.begin(dve, n)
            s_ss.wait(dve, n)
            s_msv.wait(dve, n)
            s_va.wait(dve, n - 1)
            s_qn.wait(dve, n - 1)
            rsqrt(chain.step, dve, rr[:, :], ss[:, :], rtmp[:, :], rhalf[:, :])
            dve.tensor_copy(rv[:, :], rr[:, TT * heads:])
            chain.step(dve.tensor_scalar(rlim[:, :], rr[:, TT * heads:], 1e12, None, ALU.mult))
            for t in range(TT):
                r = rr[:, t * heads:(t + 1) * heads]
                chain.step(dve.tensor_scalar(r, r, rlim[:, t:t + 1], None, ALU.min))
            chain.end()
            s_qg.wait(dve, n)
            for t in range(TT):
                r = rr[:, t * heads:(t + 1) * heads].unsqueeze(2).broadcast_to((P, heads, DH))
                q = qg[:, t, :].rearrange("p (h d) -> p h d", d=DH)
                s_qn.up(dve.tensor_tensor(q, q, r, ALU.mult))

        def dve_outputs(dve, n, g):
            s_pv.wait(dve, n, g + 1)
            s_as.wait(dve, n - 1 if g < 2 else n, GROUPS + g - 1 if g < 2 else g - 1)
            o = pO[:, :, 0:HPG * VC].rearrange("p t (h w) -> p t h w", w=VC)
            s_rl.up(dve.reciprocal(rl[:, :, :], o[:, :, :, DH]))
            s_rl.wait(dve, n, g + 1)
            for t in range(TT):
                last = dve.tensor_tensor(on[g % 2][:, t, :, :], o[:, t, :, 0:DH],
                                         rl[:, t, :].unsqueeze(2).broadcast_to((P, HPG, DH)), ALU.mult)
            s_on.up(last)

        def dve_take_q(dve, n):
            s_sc.wait(dve, n - 1)
            for t in range(TT):
                for u in range(2):
                    m = 4 * t + u
                    s_tr.wait(dve, n, m + 1)
                    s_trv.up(dve.tensor_copy(qs[:, 8 * u:8 * u + 8, t * P:(t + 1) * P],
                                             pW[:, m % 3, :].bitcast(F16).rearrange("p (h i) -> p h i", i=P)))

        def dve_gate(dve, n):
            s_o.wait(dve, n)
            s_oT.wait(dve, n - 1)
            s_og.up(dve.tensor_scalar(og[:, :], pW[:, 0, 0:N], c.mod[:, 0, 2, bass.ds(n, 1)], None, ALU.mult))

        def dve_add(dve, n):
            s_oT.wait(dve, n)
            add_and_measure(dve, c, s_st, n, TT, pW[:, 1, 0:N])

        def dve_run(dve, n, tail=True, front=True):
            if front:
                dve_modulate(dve, n + 1)
                dve_mean_square(dve, n + 1)
                dve_gains(dve, n + 1, 0)
            dve_outputs(dve, n, 0)
            if front:
                dve_gains(dve, n + 1, 1)
                dve_norms(dve, n + 1)
            dve_outputs(dve, n, 1)
            if tail:
                dve_gate(dve, n - 1)
            dve_outputs(dve, n, 2)
            if tail:
                dve_add(dve, n - 1)
            dve_outputs(dve, n, 3)
            if front:
                dve_take_q(dve, n + 1)

        @block.vector
        def _(dve):
            step = steps.on(dve)
            s_w.wait(dve, 0)
            step(dve.tensor_scalar(wq[:, :], wq[:, :], nw[:, 0:1], None, ALU.mult))
            step(dve.tensor_scalar(wkv[:, :], wkv[:, :], nw[:, 0:1], None, ALU.mult))
            step(dve.tensor_scalar(gam[:, 0:QW], gam[:, 0:QW], 1.0, float(DH) ** 0.5, ALU.add, ALU.mult))
            step(dve.tensor_scalar(gk[:, :], gk[:, :], 1.0, None, ALU.add))
            gq = gam[:, 0:QW].rearrange("p (h g d) -> p h g d", g=G2, d=DH)
            for g in range(G2):
                step(dve.tensor_tensor(gq[:, :, g, :], gq[:, :, g, :],
                                       gk[:, :].rearrange("p (h d) -> p h d", d=DH), ALU.mult))
            step(dve.memset(gam[:, QW:], float(DH) ** 0.5))
            step(dve.memset(ones[:, :], 1.0 / D))
            s_prep.up(dve.memset(va[:, :, :, DH:VC], 1.0))
            dve_modulate(dve, 0)
            dve_mean_square(dve, 0)
            dve_gains(dve, 0, 0)
            dve_gains(dve, 0, 1)
            dve_norms(dve, 0)
            dve_take_q(dve, 0)
            dve_run(dve, 0, tail=False)
            with dve.Fori(1, B - 1) as n:
                dve_run(dve, n)
            dve_run(dve, B - 1, front=False)
            dve_gate(dve, B - 1)
            dve_add(dve, B - 1)
            s_st.wait(dve, B - 1)
            ln_scales(step, dve, c)

        def act_square_h(act, n):
            s_hT.wait(act, n)
            s_ms.wait(act, n - 1)
            s_hsq.up(act.activation(hsq[:, :], hT[:, :], ACT.Square))

        def act_square_qk(act, n, t):
            s_qk.wait(act, n, t + 1)
            s_ss.wait(act, n - 1 if t == 0 else n, TT if t == 0 else t)
            s_sq.up(act.activation(sq[:, :], pW[:, :, :].rearrange("p b w -> p (b w)"), ACT.Square))

        def act_hi(act, n, t):
            s_qn.wait(act, n, t + 1)
            s_tr.wait(act, n - 1)
            act.activation(qp[:, t, :, 0:DH], qg[:, t, 0:QW].rearrange("p (h d) -> p h d", d=DH), ACT.Copy)
            k = qg[:, t, QW:].rearrange("p (h d) -> p h d", d=DH)
            act.activation(kp[:, t, :, 0:DH], k, ACT.Copy)
            s_hi.up(act.activation(kp[:, t, :, 2 * DH:3 * DH], k, ACT.Copy))

        def act_softmax(act, n, g):
            s_sc.wait(act, n, g + 1)
            s_pr.wait(act, n - 1 if g == 0 else n, GROUPS if g == 0 else g)
            s_th.up(act.activation(th[:, :], pS[:, :], ACT.Tanh, scale=1.0 / SOFTCLAMP))
            s_th.wait(act, n, g + 1)
            s_pv.wait(act, n - 1 if g < 2 else n, GROUPS + g - 1 if g < 2 else g - 1)
            s_pr.up(act.activation(pr[g % 2][:, :], th[:, :], ACT.Exp, scale=SOFTCLAMP * DH ** -0.5))

        def act_take_heads(act, n):
            s_o.wait(act, n - 1)
            for t in range(TT):
                s_aT.wait(act, n, t + 1)
                s_at.up(act.activation(at[:, :, t * P:(t + 1) * P],
                                       pW[:, 1 + t, :].rearrange("p (j i) -> p j i", i=P), ACT.Copy))

        def act_take_k(act, n):
            s_sc.wait(act, n - 1)
            for t in range(TT):
                for u in range(2):
                    m = 4 * t + 2 + u
                    s_tr.wait(act, n, m + 1)
                    s_trk.up(act.activation((k1, k2)[u][:, :, t * P:(t + 1) * P],
                                            pW[:, m % 3, :].bitcast(F16).rearrange("p (h i) -> p h i", i=P), ACT.Copy))

        def act_take_values(act, n):
            s_pv.wait(act, n - 1)
            chain.raised.wait(act, n, RSQRT_STEPS + 1)
            for t in range(TT):
                s_v.wait(act, n, t + 1)
                s_va.up(act.activation(va[:, t, :, 0:DH], pW[:, 2 - 2 * t, :].rearrange("p (h d) -> p h d", d=DH),
                                       ACT.Copy, scale=rv[:, t:t + 1]))

        def act_run(act, n, tail=True, front=True):
            act_softmax(act, n, 0)
            if front:
                act_square_h(act, n + 1)
            if tail:
                act_take_heads(act, n - 1)
            act_softmax(act, n, 1)
            if front:
                act_square_qk(act, n + 1, 0)
                act_square_qk(act, n + 1, 1)
            act_softmax(act, n, 2)
            if front:
                act_hi(act, n + 1, 0)
                act_hi(act, n + 1, 1)
            act_softmax(act, n, 3)
            if front:
                act_take_k(act, n + 1)
                act_take_values(act, n + 1)

        @block.scalar
        def _(act):
            act_square_h(act, 0)
            act_square_qk(act, 0, 0)
            act_square_qk(act, 0, 1)
            act_hi(act, 0, 0)
            act_hi(act, 0, 1)
            act_take_k(act, 0)
            act_take_values(act, 0)
            act_run(act, 0, tail=False)
            with act.Fori(1, B - 1) as n:
                act_run(act, n)
            act_run(act, B - 1, front=False)
            act_take_heads(act, B - 1)

        def gp_lo(gp, n, t):
            s_hi.wait(gp, n, t + 1)
            gp.tensor_tensor(qp[:, t, :, DH:2 * DH], qg[:, t, 0:QW].rearrange("p (h d) -> p h d", d=DH),
                             qp[:, t, :, 0:DH], ALU.subtract)
            s_lo.up(gp.tensor_tensor(kp[:, t, :, DH:2 * DH], qg[:, t, QW:].rearrange("p (h d) -> p h d", d=DH),
                                     kp[:, t, :, 0:DH], ALU.subtract))

        def gp_mask(gp, n, g):
            s_pr.wait_apart(gp, n, g + 1)
            p = pr[g % 2]
            for part in (p[:, 0:HPG * N].rearrange("p (h i) -> p h i", i=N)[:, :, 0:P],
                         p[:, HPG * N:].rearrange("p (h i) -> p h i", i=P)):
                last = gp.affine_select(out=part, in_=part, compare_op=ALU.is_ge, fill=0.0, base=0,
                                        pattern=[[0, HPG], [1, P]], channel_multiplier=-1)
            s_mk.up(last)

        def gp_sum(gp, n, g):
            s_on.wait(gp, n, g + 1)
            if g == 0:
                s_aT.wait(gp, n - 1)
            o = on[g % 2][:, :, :, :].rearrange("p t (h g) d -> p t h g d", g=G2)
            w = HPG // G2 * DH
            for t in range(TT):
                last = gp.tensor_tensor(as_[:, t, g * w:(g + 1) * w].rearrange("p (h d) -> p h d", d=DH),
                                        o[:, t, :, 0, :], o[:, t, :, 1, :], ALU.add)
            s_as.up(last)

        def gp_run(gp, n, front=True):
            gp_mask(gp, n, 0)
            gp_mask(gp, n, 1)
            gp_sum(gp, n, 0)
            gp_mask(gp, n, 2)
            gp_sum(gp, n, 1)
            if front:
                gp_lo(gp, n + 1, 0)
            gp_mask(gp, n, 3)
            if front:
                gp_lo(gp, n + 1, 1)
            gp_sum(gp, n, 2)
            gp_sum(gp, n, 3)

        @block.gpsimd
        def _(gp):
            gp_lo(gp, 0, 0)
            gp_lo(gp, 0, 1)
            gp_run(gp, 0)
            with gp.Fori(1, B - 1) as n:
                gp_run(gp, n)
            gp_run(gp, B - 1, front=False)


class Turner:

    def __init__(self, nc, ctx, c, name, banks):
        self.c, self.banks, self.groups = c, banks, []
        self.turned = Signal(nc, ctx, name + "_turned", 1)
        self.taken = Signal(nc, ctx, name + "_taken", 1)

    def add(self, out, blocks):
        self.groups.append((out, blocks))

    def tensor(self, pe):
        nb = len(self.banks)
        for m, (_, blocks) in enumerate(self.groups):
            self.taken.wait(pe, m - nb)
            at = 0
            for b in blocks:
                rows, cols = b.shape
                last = pe.transpose(self.banks[m % nb][0:cols, at:at + rows], b, self.c.id32[0:rows, 0:rows])
                at += rows
            self.turned.up(last)

    def vector(self, dve):
        for m, (out, blocks) in enumerate(self.groups):
            self.turned.wait(dve, m)
            rows, cols = sum(b.shape[0] for b in blocks), blocks[0].shape[1]
            self.taken.up(dve.tensor_copy(out, self.banks[m % len(self.banks)][0:cols, 0:rows]))

    def wait(self, engine):
        self.taken.wait(engine, len(self.groups) - 1)


def moe(nc, c, ins):
    with ExitStack() as ctx:
        def sb(name, shape, dt=F32):
            return ctx.enter_context(nc.sbuf_tensor("b_" + name, shape, dt))

        def sig(name, per=1):
            return Signal(nc, ctx, "b_" + name, per)
        S2 = 2
        RUNS = B // S2
        T4, W = S2 * TT, S2 * N
        RT, ST = E * EI // P, SI // P
        IT = RT + ST
        DEPTH = 3
        un, dn, gn = sb("un", [P, IT, D]), sb("dn", [D, IT * P]), sb("gn", [E, D])
        uT, dT, gT = sb("uT", [D, IT * P]), sb("dT", [P, IT * D]), sb("gT", [D, E])
        bias = sb("bias", [P, E])
        sel = sb("sel", [2 * E, RT, P], F16)
        lt4, lt16 = sb("lt4", [P, NG, NG]), sb("lt16", [P, E, E])
        xn = sb("xn", [P, T4, D])
        hT = [sb(f"hT{k}", [D, W]) for k in range(2)]
        s, sc, mk, cw, rank = (sb(x, [P, T4, E]) for x in ("s", "sc", "mk", "cw", "rank"))
        pm, qm = sb("pm", [P, T4 * NG, 2]), sb("qm", [P, T4 * NG, 2])
        m1, m2, m3, gs, gr = (sb(x, [P, T4 * NG]) for x in ("m1", "m2", "m3", "gs", "gr"))
        gt4, eq4 = sb("gt4", [P, T4, NG, NG]), sb("eq4", [P, T4, NG, NG])
        gt16, eq16 = sb("gt16", [P, T4, E, E]), sb("eq16", [P, T4, E, E])
        tot = sb("tot", [P, T4])
        cwp = sb("cwp", [P, T4, 2 * E], F16)
        cwT = [sb(f"cwT{k}", [2 * E, W], F16) for k in range(2)]
        r = [sb(f"r{k}", [P, W]) for k in range(3)]
        rc = [sb(f"rc{k}", [P, W]) for k in range(3)]
        a = [sb(f"a{k}", [P, W]) for k in range(4)]
        og = sb("og", [D, W])
        pX, pR, pD, pB = (ctx.enter_context(nc.psum_tensor("b_p" + x, [P, BANK], F32)) for x in "XRDB")
        pU = [ctx.enter_context(nc.psum_tensor(f"b_pU{k}", [P, BANK], F32)) for k in range(2)]
        pC = [ctx.enter_context(nc.psum_tensor(f"b_pC{k}", [P, BANK], F32)) for k in range(2)]

        s_w, s_k, s_km = Signal(nc, ctx, "b_w", 16 * 6), sig("k", 5), sig("km")
        steps = Steps(nc, ctx, "b_steps")
        turner = Turner(nc, ctx, c, "b", [pU[0], pU[1], pC[0], pC[1]])
        s_xn, s_xT, s_hT, s_lg, s_ex, s_cT, s_cw = (
            sig(x, p) for x, p in (("xn", 1), ("xT", 1), ("hT", 1), ("lg", 1), ("ex", 1), ("cT", 1), ("cw", 1)))
        s_up, s_r, s_dn, s_a = (sig(x, IT) for x in ("up", "r", "dn", "a"))
        s_cb, s_rc = sig("cb", RT), sig("rc", RT)
        s_og, s_oT, s_st = sig("og"), sig("oT"), sig("st", ADD_STEPS)
        for lo in range(0, IT, 4):
            hi = min(lo + 4, IT)
            turner.add(uT[:, lo * P:hi * P], [un[:, t, :] for t in range(lo, hi)])
        for lo in range(0, IT, 4):
            hi = min(lo + 4, IT)
            turner.add(dT[:, lo * D:hi * D], [dn[:, t * P:(t + 1) * P] for t in range(lo, hi)])
        turner.add(gT[:, :], [gn[:, :]])

        block = ctx.enter_context(nc.Block())

        @block.sync
        def _(sp):
            for to, of in ((un[:, 0:RT, :], ins["L0_ffn_up_w"].rearrange("e i d -> (e i) d").rearrange("(t p) d -> p t d", p=P)),
                           (un[:, RT:IT, :], ins["L0_ffn_shared_up"].rearrange("(t p) d -> p t d", p=P)),
                           (dn[:, 0:RT * P].rearrange("p (e i) -> p e i", i=EI), ins["L0_ffn_down_w"].rearrange("e d i -> d e i")),
                           (dn[:, RT * P:], ins["L0_ffn_shared_down"]),
                           (gn[:, :], ins["L0_ffn_gate_w"]),
                           (bias[:, :], ins["L0_ffn_bias_e"].partition_broadcast(P))):
                s_w.up(sp.dma_start(to, of), 16)

        def pe_front(pe, n):
            s_xn.wait(pe, n)
            s_hT.wait(pe, n - 1)
            for t in range(T4):
                last = pe.transpose(pX[:, t * P:(t + 1) * P], xn[:, t, :], c.id32[:, :])
            s_xT.up(last)

        def pe_route(pe, n, k):
            s_hT.wait(pe, n)
            s_cw.wait(pe, n - 1)
            for t in range(T4):
                last = pe.matmul(pR[:, t * E:(t + 1) * E], hT[k][:, t * P:(t + 1) * P], gT[:, :], start=True, stop=True)
            s_lg.up(last)

        def pe_turn_weights(pe, n):
            chain.raised.wait(pe, n)
            out = pR[0:2 * E, BANK // 2:BANK].bitcast(F16)
            for t in range(T4):
                last = pe.transpose(out[:, t * P:(t + 1) * P], cwp[:, t, :], c.id16[:, :])
            s_cT.up(last)

        def pe_up(pe, n, t, k):
            before = n * IT + t - 2
            pe_at(pe, s_r, before)
            s_up.up(pe.matmul(pU[t % 2][:, :], uT[:, t * P:(t + 1) * P], hT[k][:, :], start=True, stop=True))
            if t < RT:
                pe_at(pe, s_rc, n * RT + t - 2)
                if t == 0:
                    s_cw.wait(pe, n)
                s_cb.up(pe.matmul(pC[t % 2][:, :], sel[:, t, :], cwT[k][:, :], start=True, stop=True))

        def pe_at(engine, signal, count):
            if isinstance(count, int) and count < 0:
                return
            engine.wait_ge(signal.sem, count + 1)

        def pe_down(pe, n, t):
            s_a.wait(pe, n, t + 1)
            if t == 0:
                s_og.wait(pe, n - 1)
            s_dn.up(pe.matmul(pD[:, :], dT[:, t * D:(t + 1) * D], a[t % 4][:, :], start=t == 0, stop=t == IT - 1))

        def pe_back(pe, n):
            s_og.wait(pe, n)
            for t in range(T4):
                last = pe.transpose(pB[:, t * P:(t + 1) * P], og[:, t * P:(t + 1) * P], c.id32[:, :])
            s_oT.up(last)

        def pe_run(pe, n, k, tail=True, front=True):
            for t in range(IT + DEPTH):
                if t < IT:
                    pe_up(pe, n, t, k)
                if t == 0 and front:
                    pe_front(pe, n + 1)
                if t == 1 and front:
                    pe_route(pe, n + 1, 1 - k)
                if t == 2 and tail:
                    pe_back(pe, n - 1)
                if t == IT + 1 and front:
                    pe_turn_weights(pe, n + 1)
                if t >= DEPTH:
                    pe_down(pe, n, t - DEPTH)

        chain = Chain(nc, ctx, "b_rt", 29)

        def runs(engine, run):
            run(engine, 0, 0, tail=False)
            with engine.Fori(0, (RUNS - 2) // 2) as i:
                run(engine, i * 2 + 1, 1)
                run(engine, i * 2 + 2, 0)
            run(engine, RUNS - 1, 1, front=False)

        @block.tensor
        def _(pe):
            s_w.wait(pe, 0)
            turner.tensor(pe)
            turner.wait(pe)
            s_k.wait(pe, 0)
            s_km.wait(pe, 0)
            pe_front(pe, 0)
            pe_route(pe, 0, 0)
            pe_turn_weights(pe, 0)
            runs(pe, pe_run)
            pe_back(pe, RUNS - 1)

        def dve_front(dve, n, k):
            s_xT.wait(dve, n - 1)
            for t in range(T4):
                last = normalise(dve, c, xn[:, t, :], n * T4 + t)
            s_xn.up(last)

        def dve_modulate(dve, n, k):
            s_xT.wait(dve, n)
            for m in range(S2):
                last = dve.tensor_scalar(hT[k][:, m * N:(m + 1) * N], pX[:, m * N:(m + 1) * N],
                                         c.mod[:, 0, 4, bass.ds(n * S2 + m, 1)], c.mod[:, 0, 3, bass.ds(n * S2 + m, 1)],
                                         ALU.mult, ALU.add)
            s_hT.up(last)

        def dve_routing(dve, n):
            tt, ts, stt = dve.tensor_tensor, dve.tensor_scalar, dve.scalar_tensor_tensor

            def rows(x):
                return x[:, :, :].rearrange("p t (g e) -> p (t g) e", e=EG)
            pairs = rows(sc).rearrange("p a (x y) -> p a x y", y=2)
            g3 = gs[:, :].rearrange("p (t g) -> p t g", g=NG)
            s4, s16 = (P, T4, NG, NG), (P, T4, E, E)
            a4, b4 = g3.unsqueeze(2).broadcast_to(s4), g3.unsqueeze(3).broadcast_to(s4)
            a16, b16 = mk[:, :, :].unsqueeze(2).broadcast_to(s16), mk[:, :, :].unsqueeze(3).broadcast_to(s16)
            return [
                lambda: (s_ex.wait(dve, n), ts(s[:, :, :], s[:, :, :], 1.0, None, ALU.add))[1],
                lambda: dve.reciprocal(s[:, :, :], s[:, :, :]),
                lambda: tt(sc[:, :, :], s[:, :, :], bias[:, :].unsqueeze(1).broadcast_to((P, T4, E)), ALU.add),
                lambda: tt(pm[:, :, :], pairs[:, :, :, 0], pairs[:, :, :, 1], ALU.max),
                lambda: tt(qm[:, :, :], pairs[:, :, :, 0], pairs[:, :, :, 1], ALU.min),
                lambda: tt(m1[:, :], pm[:, :, 0], pm[:, :, 1], ALU.max),
                lambda: tt(m2[:, :], pm[:, :, 0], pm[:, :, 1], ALU.min),
                lambda: tt(m3[:, :], qm[:, :, 0], qm[:, :, 1], ALU.max),
                lambda: tt(m2[:, :], m2[:, :], m3[:, :], ALU.max),
                lambda: tt(gs[:, :], m1[:, :], m2[:, :], ALU.add),
                lambda: tt(gt4[:, :, :, :], a4, b4, ALU.is_gt),
                lambda: tt(eq4[:, :, :, :], a4, b4, ALU.is_equal),
                lambda: tt(eq4[:, :, :, :], eq4[:, :, :, :], lt4[:, :, :].unsqueeze(1).broadcast_to(s4), ALU.mult),
                lambda: tt(gt4[:, :, :, :], gt4[:, :, :, :], eq4[:, :, :, :], ALU.add),
                lambda: dve.tensor_reduce(gr[:, :], gt4[:, :, :, :].rearrange("p t a b -> p (t a) b"), AX.X, ALU.add),
                lambda: ts(gr[:, :], gr[:, :], float(TOPG), None, ALU.is_lt),
                lambda: tt(rows(mk), rows(sc), gr[:, :].unsqueeze(2).broadcast_to((P, T4 * NG, EG)), ALU.mult),
                lambda: tt(gt16[:, :, :, :], a16, b16, ALU.is_gt),
                lambda: tt(eq16[:, :, :, :], a16, b16, ALU.is_equal),
                lambda: tt(eq16[:, :, :, :], eq16[:, :, :, :], lt16[:, :, :].unsqueeze(1).broadcast_to(s16), ALU.mult),
                lambda: tt(gt16[:, :, :, :], gt16[:, :, :, :], eq16[:, :, :, :], ALU.add),
                lambda: dve.tensor_reduce(rank[:, :, :], gt16[:, :, :, :], AX.X, ALU.add),
                lambda: stt(cw[:, :, :], rank[:, :, :], float(TOPK), s[:, :, :], ALU.is_lt, ALU.mult),
                lambda: dve.tensor_reduce(tot[:, :], cw[:, :, :], AX.X, ALU.add),
                lambda: ts(tot[:, :], tot[:, :], 1e-20, None, ALU.add),
                lambda: dve.reciprocal(tot[:, :], tot[:, :]),
                lambda: stt(cw[:, :, :], cw[:, :, :], ROUTED, tot[:, :].unsqueeze(2).broadcast_to((P, T4, E)), ALU.mult, ALU.mult),
                lambda: (s_cT.wait(dve, n - 1), dve.tensor_copy(cwp[:, :, 0:E], cw[:, :, :]))[1],
                lambda: tt(cwp[:, :, E:2 * E], cw[:, :, :], cwp[:, :, 0:E], ALU.subtract),
            ]

        def dve_take_weights(dve, n, k):
            s_cT.wait(dve, n)
            s_cw.up(dve.tensor_copy(cwT[k][:, :], pR[0:2 * E, BANK // 2:BANK].bitcast(F16)))

        def dve_weigh(dve, n, t):
            s_r.wait(dve, n, t + 1)
            s_cb.wait(dve, n, t + 1)
            pe_at(dve, s_a, n * IT + t - 3)
            s_rc.up(dve.tensor_tensor(rc[t % 3][:, :], r[t % 3][:, :], pC[t % 2][:, :], ALU.mult))

        def dve_gate(dve, n):
            s_dn.wait(dve, n)
            s_oT.wait(dve, n - 1)
            for m in range(S2):
                last = dve.tensor_scalar(og[:, m * N:(m + 1) * N], pD[:, m * N:(m + 1) * N],
                                         c.mod[:, 0, 5, bass.ds(n * S2 + m, 1)], None, ALU.mult)
            s_og.up(last)

        def dve_add(dve, n):
            s_oT.wait(dve, n)
            add_and_measure(dve, c, s_st, n, T4, pB[:, :])

        def dve_run(dve, n, k, tail=True, front=True):
            todo = []
            if front:
                dve_front(dve, n + 1, 1 - k)
                chain.begin(dve, n + 1)
                chain.raised.wait(dve, n)
                todo = dve_routing(dve, n + 1)
            if tail:
                dve_gate(dve, n - 1)
            if front:
                dve_modulate(dve, n + 1, 1 - k)
            for t in range(RT):
                dve_weigh(dve, n, t)
                for step in todo[:4]:
                    chain.step(step())
                todo = todo[4:]
                if t == 2 and tail:
                    dve_add(dve, n - 1)
            if front:
                chain.end()
                dve_take_weights(dve, n + 1, 1 - k)

        @block.vector
        def _(dve):
            turner.vector(dve)
            dve_front(dve, 0, 0)
            dve_modulate(dve, 0, 0)
            s_km.wait(dve, 0)
            chain.begin(dve, 0)
            for step in dve_routing(dve, 0):
                chain.step(step())
            chain.end()
            dve_take_weights(dve, 0, 0)
            runs(dve, dve_run)
            dve_gate(dve, RUNS - 1)
            dve_add(dve, RUNS - 1)
            s_st.wait(dve, RUNS - 1)
            ln_scales(steps.on(dve), dve, c)

        def act_exp(act, n):
            s_lg.wait(act, n)
            chain.raised.wait(act, n - 1, 23)
            s_ex.up(act.activation(s[:, :, :].rearrange("p t e -> p (t e)"), pR[:, 0:T4 * E], ACT.Exp, scale=-1.0))

        def act_relu(act, n, t):
            s_up.wait(act, n, t + 1)
            pe_at(act, s_a, n * IT + t - 3)
            s_r.up(act.activation(r[(t) % 3][:, :], pU[t % 2][:, :], ACT.Relu))

        def act_run(act, n, k, tail=True, front=True):
            for t in range(IT):
                act_relu(act, n, t)
                if t == 2 and front:
                    act_exp(act, n + 1)

        @block.scalar
        def _(act):
            act_exp(act, 0)
            runs(act, act_run)

        def gp_square(gp, n, t):
            if t < RT:
                s_rc.wait(gp, n, t + 1)
            else:
                s_r.wait(gp, n, t + 1)
            pe_at(gp, s_dn, n * IT + t - 4)
            other = rc[t % 3] if t < RT else r[t % 3]
            s_a.up(gp.tensor_tensor(a[t % 4][:, :], r[t % 3][:, :], other[:, :], ALU.mult))

        def gp_run(gp, n, k, tail=True, front=True):
            for t in range(IT):
                gp_square(gp, n, t)

        @block.gpsimd
        def _(gp):
            s_k.up(gp.memset(sel[:, :, :], 0.0))
            s_k.up(gp.memset(lt4[:, :, :], 1.0))
            s_k.up(gp.memset(lt16[:, :, :], 1.0))
            for k in range(2):
                s_k.wait(gp, 0, 3 + k)
                m = sel[:, :, :].rearrange("r t (x i) -> r t x i", i=EI)
                s_k.up(gp.affine_select(out=m, in_=m, compare_op=ALU.not_equal, fill=1.0, base=k * E,
                                        pattern=[[2, RT], [1, 2], [0, EI]], channel_multiplier=-1))
            for m, w in ((lt4, NG), (lt16, E)):
                last = gp.affine_select(out=m[:, :, :], in_=m[:, :, :], compare_op=ALU.is_gt, fill=0.0, base=0,
                                        pattern=[[1, w], [-1, w]], channel_multiplier=0)
            s_km.up(last)
            runs(gp, gp_run)


def rope_tables():
    inverse = np.float32(10000.0) ** (-np.arange(0, DR, 2, dtype=np.float32) / np.float32(DR))
    angle = np.arange(N, dtype=np.float32)[:, None] * inverse
    both = [f(angle).astype(np.float32).reshape(TT, P, DR // 2).transpose(1, 0, 2) for f in (np.cos, np.sin)]
    return np.ascontiguousarray(np.stack(both, axis=1))


def attention1(nc, c, ins):
    with ExitStack() as ctx:
        def sb(name, shape, dt=F32):
            return ctx.enter_context(nc.sbuf_tensor("c_" + name, shape, dt))

        def sig(name, per=1):
            return Signal(nc, ctx, "c_" + name, per)
        HD = H1 * DC
        QA = (H1 + 1) * DQ
        KA, VA_ = QA, QA + HD
        COLS = VA_ + HD
        SW = 64
        VW = 32
        SC = HPG * (N + P)
        groups = H1 // HPG
        lim = float(CLIP / np.sqrt(np.float32(DQ)))
        most, least = float(np.float32(np.exp(lim))), float(np.float32(np.exp(-lim)))
        dq_, dkv = sb("dq", [D, LAT]), sb("dkv", [D, LAT])
        up = sb("up", [LAT, 3 * HD + H1 * DR])
        dT = sb("dT", [LAT, 2, D])
        wa = sb("wa", [D, COLS])
        kr = sb("kr", [D, DR])
        wo = sb("wo", [HD, D])
        tab = sb("tab", [P, 2, TT, DR // 2])
        xn, hT = sb("xn", [P, TT, D]), sb("hT", [D, N])
        rt = [sb(f"rt{k}", [P, TT, H1 + 1, DR // 2]) for k in range(4)]
        qf, kf = sb("qf", [P, TT, H1 + 1, DQ]), sb("kf", [P, TT, H1, DQ])
        qp, kp = sb("qp", [P, TT, H1, SW], F16), sb("kp", [P, TT, H1, SW], F16)
        qs, ks = sb("qs", [P, H1 // 2, N], F16), sb("ks", [P, H1, N], F16)
        vs = sb("vs", [P, TT, HD])
        va = sb("va", [P, TT, H1, VW])
        pr = [sb(f"pr{k}", [P, SC]) for k in range(2)]
        vu = sb("vu", [P, groups, N])
        rl = sb("rl", [P, TT, H1])
        an, at, og = sb("an", [P, TT, H1, DC]), sb("at", [HD, N]), sb("og", [D, N])
        pS = ctx.enter_context(nc.psum_tensor("c_pS", [P, 3 * BANK], F32))
        pV = [ctx.enter_context(nc.psum_tensor(f"c_pV{k}", [P, BANK], F32)) for k in range(2)]
        pW = ctx.enter_context(nc.psum_tensor("c_pW", [P, 3, BANK], F32))

        s_w = Signal(nc, ctx, "c_w", 16 * 9)
        s_wm, s_wr, s_z = sig("wm"), sig("wr"), sig("z", 2)
        steps = Steps(nc, ctx, "c_steps")
        turner = Turner(nc, ctx, c, "c", [pV[0], pV[1]])
        turner.add(dT[:, 0, :], [dq_[:, :]])
        turner.add(dT[:, 1, :], [dkv[:, :]])
        s_sc, s_ex, s_cl, s_mk, s_pv, s_vu = (sig(x, groups) for x in ("sc", "ex", "cl", "mk", "pv", "vu"))
        s_xn, s_xT, s_hT = sig("xn"), sig("xT"), sig("hT")
        s_pj, s_f, s_rd = sig("pj"), sig("f"), sig("rd")
        s_va = sig("va")
        s_hi, s_lo = sig("hi", TT), sig("lo", TT)
        s_tr, s_ev = sig("tr", 2 * TT), sig("ev", 2 * TT)
        s_aT, s_nm, s_bT, s_at, s_o, s_og, s_oT, s_st = (
            sig(x, p) for x, p in (("aT", TT), ("nm", TT), ("bT", 1), ("at", 1), ("o", 1), ("og", 1), ("oT", 1), ("st", ADD_STEPS)))
        chain = Chain(nc, ctx, "c_rl", TT)
        block = ctx.enter_context(nc.Block())

        @block.sync
        def _(sp):
            for to, of in ((dq_[:, :], ins["L1_attn_W_DQ"]), (dkv[:, :], ins["L1_attn_W_DKV"]),
                           (up[:, 0:HD], ins["L1_attn_W_UQ"]), (up[:, HD:2 * HD], ins["L1_attn_W_UK"]),
                           (up[:, 2 * HD:3 * HD], ins["L1_attn_W_UV"]), (up[:, 3 * HD:], ins["L1_attn_W_QR"]),
                           (kr[:, :], ins["L1_attn_W_KR"]), (wo[:, :], ins["L1_attn_W_O"]),
                           (tab[:, :, :, :], ins["rope"])):
                s_w.up(sp.dma_start(to, of), 16)

        def pe_front(pe, n):
            s_xn.wait(pe, n)
            s_ev.wait(pe, n - 1)
            for t in range(TT):
                last = pe.transpose(pW[:, 0, t * P:(t + 1) * P], xn[:, t, :], c.id32[:, :])
            s_xT.up(last)

        def pe_project(pe, n):
            s_hT.wait(pe, n)
            s_nm.wait(pe, n - 2, 1)
            for t in range(TT):
                last = pe.matmul(pW[:, t, 0:COLS], hT[:, t * P:(t + 1) * P], wa[:, :], start=True, stop=True)
            s_pj.up(last)

        def pe_stacks(pe, n):
            for t in range(TT):
                s_hi.wait(pe, n, t + 1)
                s_lo.wait(pe, n, t + 1)
                for u, src in enumerate((qp, kp)):
                    m = 2 * t + u
                    if m == 2:
                        s_st.wait(pe, n - 2, 1)
                    elif m == 3:
                        s_ev.wait(pe, n, 1)
                    else:
                        s_rd.wait(pe, n)
                    bank = pW[:, m % 3, :].bitcast(F16)
                    for j in range(H1 // 2):
                        last = pe.transpose(bank[:, j * P:(j + 1) * P],
                                            src[:, t, 2 * j:2 * j + 2, :].rearrange("p h w -> p (h w)"), c.id16[:, :])
                    s_tr.up(last)

        def pe_scores(pe, n, g):
            if g == 0:
                s_ev.wait(pe, n)
            s_ex.wait(pe, n - 1 if g == 0 else n, groups if g == 0 else g)
            for hh in range(HPG):
                h = g * HPG + hh
                pe.matmul(pS[:, hh * N:(hh + 1) * N], ks[:, h, 0:P], qs[:, h // 2, :], start=True, stop=True)
                last = pe.matmul(pS[:, HPG * N + hh * P:HPG * N + (hh + 1) * P], ks[:, h, P:N], qs[:, h // 2, P:N],
                                 start=True, stop=True)
            s_sc.up(last)

        def pe_weighted_values(pe, n, g):
            if g == 0:
                s_va.wait(pe, n)
            s_mk.wait(pe, n, g + 1)
            s_vu.wait(pe, n - 1 if g < 2 else n, groups + g - 1 if g < 2 else g - 1)
            for keys in range(TT):
                for hh in range(HPG):
                    rows = slice(hh * VW, (hh + 1) * VW)
                    rhs = (pr[(g) % 2][:, hh * N:(hh + 1) * N] if keys == 0 else
                           pr[(g) % 2][:, HPG * N + hh * P:HPG * N + (hh + 1) * P])
                    last = pe.matmul(pV[g % 2][rows, keys * P:N], va[:, keys, g * HPG + hh, :], rhs,
                                     start=keys == 0, stop=keys == TT - 1, skip_group_check=True)
            s_pv.up(last)

        def pe_heads_back(pe, n, last_run=False):
            s_vu.wait(pe, n)
            if last_run:
                s_st.wait(pe, n - 1, 1)
            else:
                s_ev.wait(pe, n + 1)
            for t in range(TT):
                for g in range(groups):
                    last = pe.transpose(pW[:, 1 + t, g * P:(g + 1) * P], vu[:, g, t * P:(t + 1) * P], c.id32[:, :])
                s_aT.up(last)

        def pe_heads_turned(pe, n):
            s_nm.wait(pe, n)
            for t in range(TT):
                last = pe.transpose(pW[:, 2, t * P:(t + 1) * P], an[:, t, :, :].rearrange("p h d -> p (h d)"), c.id32[:, :])
            s_bT.up(last)

        def pe_out_project(pe, n):
            s_at.wait(pe, n)
            s_o.up(pe.matmul(pW[:, 2, 0:N], wo[:, :], at[:, :], start=True, stop=True))

        def pe_out_back(pe, n):
            s_og.wait(pe, n)
            for t in range(TT):
                last = pe.transpose(pW[:, 2, t * P:(t + 1) * P], og[:, t * P:(t + 1) * P], c.id32[:, :])
            s_oT.up(last)

        def pe_run(pe, n, tail=True, front=True):
            pe_scores(pe, n, 0)
            if front:
                pe_front(pe, n + 1)
            if tail:
                pe_heads_back(pe, n - 1)
            pe_scores(pe, n, 1)
            pe_weighted_values(pe, n, 0)
            if front:
                pe_project(pe, n + 1)
            if tail:
                pe_heads_turned(pe, n - 1)
            pe_scores(pe, n, 2)
            pe_weighted_values(pe, n, 1)
            if tail:
                pe_out_project(pe, n - 1)
            pe_scores(pe, n, 3)
            pe_weighted_values(pe, n, 2)
            if tail:
                pe_out_back(pe, n - 1)
            pe_weighted_values(pe, n, 3)
            if front:
                pe_stacks(pe, n + 1)

        @block.tensor
        def _(pe):
            s_w.wait(pe, 0)
            turner.tensor(pe)
            turner.wait(pe)
            for j, (a, u) in enumerate(((0, 0), (1, 1), (1, 2), (0, 3))):
                w = HD if j < 3 else H1 * DR
                last = pe.matmul(pW[:, 0, j * HD:j * HD + w], dT[:, a, :], up[:, u * HD:u * HD + w], start=True, stop=True)
            s_wm.up(last)
            s_wr.wait(pe, 0)
            pe_front(pe, 0)
            pe_project(pe, 0)
            pe_stacks(pe, 0)
            s_z.wait(pe, 0)
            pe_run(pe, 0, tail=False)
            with pe.Fori(1, B - 1) as n:
                pe_run(pe, n)
            pe_run(pe, B - 1, front=False)
            for stage in (lambda pe, n: pe_heads_back(pe, n, True), pe_heads_turned, pe_out_project, pe_out_back):
                stage(pe, B - 1)

        def dve_front(dve, n):
            s_xT.wait(dve, n - 1)
            for t in range(TT):
                last = normalise(dve, c, xn[:, t, :], n * TT + t)
            s_xn.up(last)

        def dve_modulate(dve, n):
            s_xT.wait(dve, n)
            s_pj.wait(dve, n - 1)
            s_hT.up(dve.tensor_scalar(hT[:, :], pW[:, 0, 0:N], c.mod[:, 1, 1, bass.ds(n, 1)],
                                      c.mod[:, 1, 0, bass.ds(n, 1)], ALU.mult, ALU.add))

        def dve_heads(dve, n):
            s_pj.wait(dve, n)
            s_hi.wait(dve, n - 1)
            s_lo.wait(dve, n - 1)
            s_f.wait(dve, n - 1)
            q = pW[:, 0:TT, 0:QA].rearrange("p t (h d) -> p t h d", d=DQ)
            x1, x2 = q[:, :, :, DC::2], q[:, :, :, DC + 1::2]
            cos, sin = (tab[:, k, :, :].unsqueeze(2).broadcast_to((P, TT, H1 + 1, DR // 2)) for k in range(2))
            for to, x, by in ((rt[0], x1, cos), (rt[1], x2, sin), (rt[2], x1, sin), (rt[3], x2, cos)):
                last = dve.tensor_tensor(to[:, :, :, :], x, by, ALU.mult)
            rope.begin(dve, n)
            rope.step(last)
            for t in range(TT):
                dve.tensor_copy(qf[:, t, 0:H1, 0:DC], q[:, t, 0:H1, 0:DC])
                dve.tensor_copy(kf[:, t, :, 0:DC], pW[:, t, KA:KA + HD].rearrange("p (h d) -> p h d", d=DC))
            dve.tensor_tensor(qf[:, :, :, DC::2], rt[0][:, :, :, :], rt[1][:, :, :, :], ALU.subtract)
            rope.step(dve.tensor_tensor(qf[:, :, :, DC + 1::2], rt[2][:, :, :, :], rt[3][:, :, :, :], ALU.add))
            for t in range(TT):
                last = dve.tensor_copy(kf[:, t, :, DC:DQ], qf[:, t, H1, DC:DQ].unsqueeze(1).broadcast_to((P, H1, DR)))
            s_f.up(last)
            rope.end()
            s_va.wait(dve, n - 1)
            s_rd.up(dve.tensor_copy(vs[:, :, :], pW[:, 0:TT, VA_:VA_ + HD]))

        rope = Chain(nc, ctx, "c_rope", 2)

        def dve_stacks(dve, n):
            s_sc.wait(dve, n - 1)
            for t in range(TT):
                i = slice(t * P, (t + 1) * P)
                s_tr.wait(dve, n, 2 * t + 1)
                s_ev.up(dve.tensor_copy(qs[:, :, i], pW[:, 2 * t % 3, :].bitcast(F16).rearrange("p (h i) -> p h i", i=P)))
                s_tr.wait(dve, n, 2 * t + 2)
                k = pW[:, (2 * t + 1) % 3, :].bitcast(F16).rearrange("p (h i) -> p h i", i=P)
                dve.tensor_copy(ks[0:SW, 0::2, i], k[0:SW, :, :])
                s_ev.up(dve.tensor_copy(ks[SW:P, 1::2, i], k[SW:P, :, :]))

        def dve_clip(dve, n, g):
            s_ex.wait(dve, n, g + 1)
            p = pr[g % 2][:, :]
            s_cl.up(dve.tensor_scalar(p, p, most, least, ALU.min, ALU.max))

        def dve_normalise(dve, n):
            chain.begin(dve, n)
            s_bT.wait(dve, n - 1)
            for t in range(TT):
                s_aT.wait(dve, n, t + 1)
                heads = pW[:, 1 + t, :].rearrange("p (h w) -> p h w", w=VW)
                chain.step(dve.reciprocal(rl[:, t, :], heads[:, :, DC]))
                s_nm.up(dve.tensor_tensor(an[:, t, :, :], heads[:, :, 0:DC],
                                          rl[:, t, :].unsqueeze(2).broadcast_to((P, H1, DC)), ALU.mult))
            chain.end()

        def dve_gate(dve, n):
            s_o.wait(dve, n)
            s_oT.wait(dve, n - 1)
            s_og.up(dve.tensor_scalar(og[:, :], pW[:, 2, 0:N], c.mod[:, 1, 2, bass.ds(n, 1)], None, ALU.mult))

        def dve_add(dve, n):
            s_oT.wait(dve, n)
            add_and_measure(dve, c, s_st, n, TT, pW[:, 2, 0:N])

        def dve_run(dve, n, tail=True, front=True):
            if front:
                dve_front(dve, n + 1)
            dve_clip(dve, n, 0)
            if front:
                dve_modulate(dve, n + 1)
            if tail:
                dve_normalise(dve, n - 1)
            dve_clip(dve, n, 1)
            if front:
                dve_heads(dve, n + 1)
            dve_clip(dve, n, 2)
            if tail:
                dve_gate(dve, n - 1)
            dve_clip(dve, n, 3)
            if tail:
                dve_add(dve, n - 1)
            if front:
                dve_stacks(dve, n + 1)

        @block.vector
        def _(dve):
            turner.vector(dve)
            step = steps.on(dve)
            step(dve.memset(wa[:, :], 0.0))
            s_wm.wait(dve, 0)
            q = wa[:, 0:QA].rearrange("p (h d) -> p h d", d=DQ)
            dve.tensor_copy(q[:, 0:H1, 0:DC], pW[:, 0, 0:HD].rearrange("p (h d) -> p h d", d=DC))
            dve.tensor_copy(q[:, 0:H1, DC:DQ], pW[:, 0, 3 * HD:3 * HD + H1 * DR].rearrange("p (h d) -> p h d", d=DR))
            dve.tensor_copy(q[:, H1, DC:DQ], kr[:, :])
            step(dve.tensor_copy(wa[:, KA:COLS], pW[:, 0, HD:3 * HD]))
            s_wr.up(dve.memset(qf[:, :, H1, 0:DC], 0.0))
            dve_front(dve, 0)
            dve_modulate(dve, 0)
            dve_heads(dve, 0)
            s_z.wait(dve, 0)
            dve_stacks(dve, 0)
            dve_run(dve, 0, tail=False)
            with dve.Fori(1, B - 1) as n:
                dve_run(dve, n)
            dve_run(dve, B - 1, front=False)
            dve_normalise(dve, B - 1)
            dve_gate(dve, B - 1)
            dve_add(dve, B - 1)
            s_st.wait(dve, B - 1)
            ln_scales(step, dve, c)

        def parts(x, t, first, gap):
            return x[:, t, :, 0:4 * DQ].rearrange("p h (k d) -> p h k d", d=DQ)[:, :, first:first + gap + 1:gap, :]

        def twice(x, t):
            return x[:, t, 0:H1, :].unsqueeze(2).broadcast_to((P, H1, 2, DQ))

        def act_hi(act, n, t):
            s_f.wait(act, n)
            s_tr.wait(act, n - 1)
            act.activation(parts(qp, t, 0, 1), twice(qf, t), ACT.Copy)
            s_hi.up(act.activation(parts(kp, t, 0, 2), twice(kf, t), ACT.Copy))

        def act_exp(act, n, g):
            s_sc.wait(act, n, g + 1)
            s_pv.wait(act, n - 1 if g < 2 else n, groups + g - 1 if g < 2 else g - 1)
            s_ex.up(act.activation(pr[g % 2][:, :], pS[:, :], ACT.Exp, scale=float(1.0 / np.sqrt(np.float32(DQ)))))

        def act_take_values(act, n, g):
            s_pv.wait(act, n, g + 1)
            if g == 0:
                s_aT.wait(act, n - 1)
            s_vu.up(act.activation(vu[:, g, :], pV[g % 2][:, 0:N], ACT.Copy))

        def act_take_heads(act, n):
            s_bT.wait(act, n)
            s_o.wait(act, n - 1)
            s_at.up(act.activation(at[:, :], pW[:, 2, 0:N], ACT.Copy))

        def act_place_values(act, n):
            s_rd.wait(act, n)
            s_pv.wait(act, n - 1)
            if isinstance(n, int) and n == 0:
                s_z.wait(act, 0)
            s_va.up(act.activation(va[:, :, :, 0:DC].rearrange("p t h d -> p (t h) d"),
                                   vs[:, :, :].rearrange("p t (h d) -> p (t h) d", d=DC), ACT.Copy))

        def act_run(act, n, tail=True, front=True):
            act_exp(act, n, 0)
            act_exp(act, n, 1)
            act_take_values(act, n, 0)
            if tail:
                act_take_heads(act, n - 1)
            act_exp(act, n, 2)
            act_take_values(act, n, 1)
            if front:
                act_hi(act, n + 1, 0)
            act_exp(act, n, 3)
            if front:
                act_hi(act, n + 1, 1)
            act_take_values(act, n, 2)
            act_take_values(act, n, 3)
            if front:
                act_place_values(act, n + 1)

        @block.scalar
        def _(act):
            act_hi(act, 0, 0)
            act_hi(act, 0, 1)
            act_place_values(act, 0)
            act_run(act, 0, tail=False)
            with act.Fori(1, B - 1) as n:
                act_run(act, n)
            act_run(act, B - 1, front=False)
            act_take_heads(act, B - 1)

        def gp_lo(gp, n, t):
            s_hi.wait(gp, n, t + 1)
            gp.tensor_tensor(parts(qp, t, 2, 1), twice(qf, t), parts(qp, t, 0, 1), ALU.subtract)
            s_lo.up(gp.tensor_tensor(parts(kp, t, 1, 2), twice(kf, t), parts(kp, t, 0, 2), ALU.subtract))

        def gp_mask(gp, n, g):
            s_cl.wait_apart(gp, n, g + 1)
            p = pr[g % 2]
            for part in (p[:, 0:HPG * N].rearrange("p (h i) -> p h i", i=N)[:, :, 0:P],
                         p[:, HPG * N:].rearrange("p (h i) -> p h i", i=P)):
                last = gp.affine_select(out=part, in_=part, compare_op=ALU.is_ge, fill=0.0, base=0,
                                        pattern=[[0, HPG], [1, P]], channel_multiplier=-1)
            s_mk.up(last)

        def gp_run(gp, n, front=True):
            for g in range(groups):
                gp_mask(gp, n, g)
                if front and g >= 2:
                    gp_lo(gp, n + 1, g - 2)

        @block.gpsimd
        def _(gp):
            gp.memset(ks[:, :, :], 0.0)
            gp.memset(qp[:, :, :, 4 * DQ:], 0.0)
            gp.memset(kp[:, :, :, 4 * DQ:], 0.0)
            s_z.up(gp.memset(va[:, :, :, DC:], 0.0))
            s_z.wait(gp, 0, 1)
            s_z.up(gp.memset(va[:, :, :, DC:DC + 1], 1.0))
            gp_lo(gp, 0, 0)
            gp_lo(gp, 0, 1)
            gp_run(gp, 0)
            with gp.Fori(1, B - 1) as n:
                gp_run(gp, n)
            gp_run(gp, B - 1, front=False)


def mlp(nc, c, ins):
    with ExitStack() as ctx:
        def sb(name, shape, dt=F32):
            return ctx.enter_context(nc.sbuf_tensor("d_" + name, shape, dt))

        def sig(name, per=1):
            return Signal(nc, ctx, "d_" + name, per)
        S2 = 2
        RUNS = B // S2
        T4, W = S2 * TT, S2 * N
        HT = HID // P
        wave = [[(i, o) for o in range(HT) for i in range(HT) if max(i, o) == w] for w in range(HT)]
        wave[-1].sort(key=lambda x: (x[1], x[0]))
        nat = {k: sb(k, [P, HT, D]) for k in ("w1", "w2")}
        nat |= {k: sb(k, [P, HT, HID]) for k in ("h1", "h2")}
        nat["w3"] = sb("w3", [P, HID])
        w1T, w2T, w3T = (sb(x, [P, HID], F16) for x in ("w1T", "w2T", "w3T"))
        h1T, h2T = (sb(x, [P, HT, HID], F16) for x in ("h1T", "h2T"))
        sc = {k: sb(k + "s", [P, HT]) for k in ("w1", "w2", "h1", "h2")}
        sc3 = sb("w3s", [D, 1])
        s12, s1h = sb("s12", [P, HT]), sb("s1h", [P, HT])
        gate = sb("gate", [D, B])
        xn, hf = sb("xn", [P, T4, D]), sb("hf", [D, W])
        hx = sb("hx", [D, 2, W], F16)
        th, gf, uf = sb("th", [P, W]), sb("gf", [P, W]), [sb(f"uf{k}", [P, W]) for k in range(2)]
        a1, a2, a3 = (sb(x, [P, HT, 2, W], F16) for x in ("a1", "a2", "a3"))
        ge = [sb(f"ge{k}", [P, W]) for k in range(3)]
        og = sb("og", [D, W])
        pH = [ctx.enter_context(nc.psum_tensor(f"d_pH{k}", [P, BANK], F32)) for k in range(HT)]
        pA, pB, pD, pX = (ctx.enter_context(nc.psum_tensor("d_p" + x, [P, BANK], F32)) for x in "ABDX")

        s_w = Signal(nc, ctx, "d_w", 16 * 10)
        steps = Steps(nc, ctx, "d_steps")
        turner = Turner(nc, ctx, c, "d", pH)
        for k, to in (("w1", w1T), ("w2", w2T)):
            turner.add(to[:, :], [nat[k][:, j, :] for j in range(HT)])
        for k, to in (("h1", h1T), ("h2", h2T)):
            for i in range(HT):
                turner.add(to[:, i, :], [nat[k][:, o, i * P:(i + 1) * P] for o in range(HT)])
        turner.add(w3T[:, :], [nat["w3"][:, i * P:(i + 1) * P] for i in range(HT)])
        s_c = sig("c")
        s_xn, s_xT, s_hf, s_hx = sig("xn"), sig("xT"), sig("hf"), sig("hx")
        s_in, s_th, s_gf, s_uf, s_uh, s_a1 = (sig(x, HT) for x in ("in", "th", "gf", "uf", "uh", "a1"))
        s_m2, s_m3, s_g2, s_g3, s_a2, s_a3 = (sig(x, HT) for x in ("m2", "m3", "g2", "g3", "a2", "a3"))
        s_h2, s_h3 = sig("h2", HT), sig("h3", HT)
        s_o, s_og, s_oT, s_st = sig("o"), sig("og"), sig("oT"), sig("st")
        block = ctx.enter_context(nc.Block())

        @block.sync
        def _(sp):
            for to, of in ((nat["w1"][:, :, :], ins["L1_ffn_w1_w"].rearrange("(j p) d -> p j d", p=P)),
                           (nat["w2"][:, :, :], ins["L1_ffn_w2_w"].rearrange("(j p) d -> p j d", p=P)),
                           (nat["h1"][:, :, :], ins["L1_ffn_h1_w"].rearrange("(j p) d -> p j d", p=P)),
                           (nat["h2"][:, :, :], ins["L1_ffn_h2_w"].rearrange("(j p) d -> p j d", p=P)),
                           (nat["w3"][:, :], ins["L1_ffn_w3_w"]),
                           (sc3[:, :], ins["L1_ffn_w3_s"].rearrange("(p a) -> p a", a=1))):
                s_w.up(sp.dma_start(to, of), 16)
            for k in sc:
                s_w.up(sp.dma_start(sc[k][:, :], ins[f"L1_ffn_{k}_s"].rearrange("(j p) -> p j", p=P),
                                   allow_slow_non_contiguous=True), 16)

        def pe_front(pe, n):
            s_xn.wait(pe, n)
            for t in range(T4):
                last = pe.transpose(pX[:, t * P:(t + 1) * P], xn[:, t, :], c.id32[:, :])
            s_xT.up(last)

        def pe_first(pe, n, j):
            if j == 0:
                s_hx.wait(pe, n)
            s_uf.wait(pe, n - 1 if j == 0 else n, HT if j == 0 else j)
            for out, w in ((pA, w1T), (pB, w2T)):
                for part in range(2):
                    last = pe.matmul(out[:, :], w[:, j * P:(j + 1) * P], hx[:, part, :], start=part == 0, stop=part == 1)
            s_in.up(last)

        def pe_hidden(pe, n, w, weights, a, have, read, k_of, done):
            for m, (i, o) in enumerate(wave[w]):
                if m == 0:
                    have.wait(pe, n, w + 1)
                    read(pe, n, w)
                for part in range(2):
                    last = pe.matmul(pH[o][:, :], weights[:, i, o * P:(o + 1) * P], a[:, i, part, :],
                                     start=k_of(i, o) and part == 0, stop=i == HT - 1 and part == 1)
                if i == HT - 1:
                    done.up(last)

        def pe_second(pe, n, w):
            pe_hidden(pe, n, w, h1T, a1, s_a1, lambda pe, n, w: s_g3.wait(pe, n - 1, w + 1), lambda i, o: i == 0, s_m2)

        def pe_third(pe, n, w):
            pe_hidden(pe, n, w, h2T, a2, s_a2, lambda pe, n, w: s_g2.wait(pe, n, w + 1), lambda i, o: i == 0, s_m3)

        def pe_out(pe, n):
            s_og.wait(pe, n - 1)
            for i in range(HT):
                s_a3.wait(pe, n, i + 1)
                for part in range(2):
                    last = pe.matmul(pD[:, :], w3T[:, i * P:(i + 1) * P], a3[:, i, part, :],
                                     start=i == 0 and part == 0, stop=i == HT - 1 and part == 1)
            s_o.up(last)

        def pe_back(pe, n, last_run=False):
            s_og.wait(pe, n)
            if last_run:
                s_st.wait(pe, n - 1, 1)
            else:
                s_hf.wait(pe, n + 2)
            for t in range(T4):
                last = pe.transpose(pX[:, t * P:(t + 1) * P], og[:, t * P:(t + 1) * P], c.id32[:, :])
            s_oT.up(last)

        def pe_run(pe, n, tail=True, front=True):
            pe_second(pe, n, 0)
            if front:
                if tail:
                    s_st.wait(pe, n - 2, 1)
                pe_front(pe, n + 1)
            pe_second(pe, n, 1)
            pe_second(pe, n, 2)
            if tail:
                pe_back(pe, n - 1, not front)
            pe_second(pe, n, 3)
            if front:
                pe_first(pe, n + 1, 0)
            for w in range(HT - 1):
                pe_third(pe, n, w)
            if front:
                pe_first(pe, n + 1, 1)
            pe_third(pe, n, HT - 1)
            if front:
                pe_first(pe, n + 1, 2)
            pe_out(pe, n)
            if front:
                pe_first(pe, n + 1, 3)

        @block.tensor
        def _(pe):
            s_w.wait(pe, 0)
            turner.tensor(pe)
            turner.wait(pe)
            pe_front(pe, 0)
            for j in range(HT):
                pe_first(pe, 0, j)
            pe_run(pe, 0, tail=False)
            pe_run(pe, 1)
            with pe.Fori(2, RUNS - 1) as n:
                pe_run(pe, n)
            pe_run(pe, RUNS - 1, front=False)
            pe_back(pe, RUNS - 1, True)

        def dve_front(dve, n):
            s_xT.wait(dve, n - 1)
            for t in range(T4):
                last = normalise(dve, c, xn[:, t, :], n * T4 + t)
            s_xn.up(last)

        def dve_modulate(dve, n):
            s_xT.wait(dve, n)
            for m in range(S2):
                last = dve.tensor_scalar(hf[:, m * N:(m + 1) * N], pX[:, m * N:(m + 1) * N],
                                         c.mod[:, 1, 4, bass.ds(n * S2 + m, 1)], c.mod[:, 1, 3, bass.ds(n * S2 + m, 1)],
                                         ALU.mult, ALU.add)
            s_hf.up(last)
            s_hf.wait(dve, n)
            s_in.wait(dve, n - 1)
            split(dve, n, hx[:, 0, :], hx[:, 1, :], hf[:, :], s_hh, 1, s_hx)

        s_hh = sig("hh")

        def split(dve, n, hi, lo, x, mid, k, done):
            mid.up(dve.tensor_copy(hi, x))
            mid.wait(dve, n, k)
            done.up(dve.tensor_tensor(lo, x, hi, ALU.subtract))

        def dve_gated(dve, n, j):
            s_th.wait(dve, n, j + 1)
            s_gf.up(dve.scalar_tensor_tensor(gf[:, :], th[:, :], 1.0, pA[:, :], ALU.add, ALU.mult))
            s_gf.wait(dve, n, j + 1)
            if j < 2:
                s_a1.wait(dve, n - 1, HT + j - 1)
            else:
                s_a1.wait(dve, n, j - 1)
            s_uf.up(dve.scalar_tensor_tensor(uf[j % 2][:, :], gf[:, :], s12[:, j:j + 1], pB[:, :], ALU.mult, ALU.mult))

        def dve_parts(dve, n, o, layer):
            ready, mid, done, a, reader = ((s_g2, s_h2, s_a2, a2, s_m3), (s_g3, s_h3, s_a3, a3, s_o))[layer]
            ready.wait(dve, n, o + 1)
            if o == 0:
                reader.wait(dve, n - 1)
            split(dve, n, a[:, o, 0, :], a[:, o, 1, :], ge[o % 3][:, :], mid, o + 1, done)

        def dve_gate(dve, n):
            s_o.wait(dve, n)
            s_oT.wait(dve, n - 1)
            for m in range(S2):
                last = dve.tensor_scalar(og[:, m * N:(m + 1) * N], pD[:, m * N:(m + 1) * N],
                                         gate[:, bass.ds(n * S2 + m, 1)], None, ALU.mult)
            s_og.up(last)

        def dve_add(dve, n):
            s_oT.wait(dve, n)
            xt = x_tiles(c, n * T4, T4)
            s_st.up(dve.tensor_tensor(xt, xt, pX[:, :].rearrange("p (t d) -> p t d", t=T4), ALU.add))

        def dve_run(dve, n, tail=True, front=True):
            if front:
                dve_front(dve, n + 1)
            if tail:
                dve_gate(dve, n - 1)
            if front:
                dve_modulate(dve, n + 1)
            if tail:
                dve_add(dve, n - 1)
            for o in range(HT):
                dve_parts(dve, n, o, 0)
            if front:
                dve_gated(dve, n + 1, 0)
                dve_gated(dve, n + 1, 1)
            for o in range(HT):
                dve_parts(dve, n, o, 1)
            if front:
                dve_gated(dve, n + 1, 2)
                dve_gated(dve, n + 1, 3)

        @block.vector
        def _(dve):
            step = steps.on(dve)
            turner.vector(dve)
            s_w.wait(dve, 0)
            step(dve.tensor_scalar(s1h[:, :], sc["w1"][:, :], 0.5, None, ALU.mult))
            step(dve.tensor_tensor(s12[:, :], s1h[:, :], sc["w2"][:, :], ALU.mult))
            s_c.up(dve.tensor_scalar(gate[:, :], c.mod[:, 1, 5, :], sc3[:, 0:1], None, ALU.mult))
            s_c.wait(dve, 0)
            dve_front(dve, 0)
            dve_modulate(dve, 0)
            for j in range(HT):
                dve_gated(dve, 0, j)
            dve_run(dve, 0, tail=False)
            dve_run(dve, 1)
            with dve.Fori(2, RUNS - 1) as n:
                dve_run(dve, n)
            dve_run(dve, RUNS - 1, front=False)
            dve_gate(dve, RUNS - 1)
            dve_add(dve, RUNS - 1)

        def act_tanh(act, n, j):
            s_in.wait(act, n, j + 1)
            s_gf.wait(act, n - 1 if j == 0 else n, HT if j == 0 else j)
            s_th.up(act.activation(th[:, :], pA[:, :], ACT.Tanh, scale=s1h[:, j:j + 1]))

        def act_hi(act, n, j):
            s_uf.wait(act, n, j + 1)
            if j == 0:
                s_m2.wait(act, n - 1)
            s_uh.up(act.activation(a1[:, j, 0, :], uf[j % 2][:, :], ACT.Copy))

        def act_gelu(act, n, o, layer):
            made, done, key = ((s_m2, s_g2, "h1"), (s_m3, s_g3, "h2"))[layer]
            made.wait(act, n, o + 1)
            u = o - 3
            if u >= 0:
                (s_a2, s_a3)[layer].wait(act, n, u + 1)
            elif layer:
                s_a2.wait(act, n)
            else:
                s_a3.wait(act, n - 1)
            done.up(act.activation(ge[o % 3][:, :], pH[o][:, :], ACT.Gelu, scale=sc[key][:, o:o + 1]))

        def act_run(act, n, tail=True, front=True):
            for o in range(HT):
                act_gelu(act, n, o, 0)
            if front:
                act_tanh(act, n + 1, 0)
                act_hi(act, n + 1, 0)
                act_tanh(act, n + 1, 1)
                act_hi(act, n + 1, 1)
            for o in range(HT):
                act_gelu(act, n, o, 1)
            if front:
                act_tanh(act, n + 1, 2)
                act_hi(act, n + 1, 2)
                act_tanh(act, n + 1, 3)
                act_hi(act, n + 1, 3)

        @block.scalar
        def _(act):
            act.preload_act_table(ACT.Gelu)
            s_c.wait(act, 0)
            for j in range(HT):
                act_tanh(act, 0, j)
                act_hi(act, 0, j)
            act_run(act, 0, tail=False)
            act_run(act, 1)
            with act.Fori(2, RUNS - 1) as n:
                act_run(act, n)
            act_run(act, RUNS - 1, front=False)

        def gp_lo(gp, n, j):
            s_uh.wait(gp, n, j + 1)
            s_a1.up(gp.tensor_tensor(a1[:, j, 1, :], uf[j % 2][:, :], a1[:, j, 0, :], ALU.subtract))

        def gp_run(gp, n):
            for j in range(HT):
                gp_lo(gp, n, j)

        @block.gpsimd
        def _(gp):
            gp_run(gp, 0)
            with gp.Fori(1, RUNS) as n:
                gp_run(gp, n)


def store(nc, c, out):
    with ExitStack() as ctx:
        s_out = Signal(nc, ctx, "out", 16)
        block = ctx.enter_context(nc.Block())

        @block.sync
        def _(sp):
            s_out.up(sp.dma_start(out.rearrange("b (t p) d -> p (b t) d", p=P), c.x[:, :, :]), 16)
            s_out.wait(sp, 0)


def build(nc, ins, out):
    with ExitStack() as ctx:
        c = Core(nc, ctx)
        setup(nc, c, ins)
        attention0(nc, c, ins)
        moe(nc, c, ins)
        attention1(nc, c, ins)
        mlp(nc, c, ins)
        store(nc, c, out)


def kernel(**inputs):
    import numpy as _np
    import concourse.bacc as _bacc
    from concourse.bass_utils import run_bass_kernel_spmd as _run

    nc = _bacc.Bacc("TRN2", target_bir_lowering=False, num_devices=1)
    arrays, ins = {}, {}
    for name, value in {**inputs, "rope": rope_tables()}.items():
        a = _np.ascontiguousarray(value)
        arrays[f"in_{name}_dram"] = a
        ins[name] = nc.dram_tensor(f"in_{name}_dram", a.shape, mybir.dt.from_np(a.dtype), kind="ExternalInput").ap()
    out = nc.dram_tensor("out_0_dram", (B, N, D), F32, kind="ExternalOutput").ap()
    build(nc, ins, out)
    r = _run(nc, [arrays], core_ids=[0])
    return r.results[0]["out_0_dram"]
```

```python
from contextlib import ExitStack

import numpy as np

import concourse.bass as bass
from concourse import mybir

F32 = mybir.dt.float32
F16 = mybir.dt.float16
I32 = mybir.dt.int32
ALU = mybir.AluOpType
ACT = mybir.ActivationFunctionType
AX = mybir.AxisListType

P = 128
B, N, D = 32, 256, 128
TT = N // P
TILES = B * TT
LN_EPS = 1e-5
QH, KH, DH = 16, 8, 64
G2 = QH // KH
HPG = 4
GROUPS = QH // HPG
QW, KW = QH * DH, KH * DH
VC = 96
RMS_EPS = float(np.finfo(np.float32).eps)
SOFTCLAMP = 50.0
E, EI, SI = 16, 64, 256
NG, EG = 4, 4
TOPG, TOPK, ROUTED = 2, 4, 2.5
H1, DC, DR, LAT = 16, 8, 4, 32
DQ = DC + DR
CLIP = 80.0
HID = 512
BANK = 512


class Signal:

    def __init__(self, nc, ctx, name, per=1, runs=None):
        self.sem, self.per, self.name, self.runs = ctx.enter_context(nc.semaphore(name)), per, name, runs

    def up(self, instruction, by=1):
        instruction.then_inc(self.sem, by)

    def wait(self, engine, n, k=None):
        value = n * self.per + (self.per if k is None else k)
        if isinstance(value, int) and self.runs:
            value = min(value, self.runs * self.per)
        if isinstance(value, int) and value <= 0:
            return
        engine.wait_ge(self.sem, value)

    def wait_apart(self, engine, n, k=None):
        self.wait(engine, n, k)
        engine.nop(nofuse=True)


class Chain:

    def __init__(self, nc, ctx, name, per, runs=None):
        self.raised, self.k = Signal(nc, ctx, name, per, runs), 0

    def begin(self, engine, n):
        self.engine, self.n, self.k = engine, n, 0

    def step(self, instruction):
        self.k += 1
        self.raised.up(instruction)
        self.raised.wait(self.engine, self.n, self.k)

    def end(self):
        assert self.k == self.raised.per, (self.raised.name, self.k)


def pipeline(engine, plan, count, runs=(-2, 1)):
    def run(n, k):
        for shift, stage, *which in plan:
            if not isinstance(n, int) or 0 <= n + shift < count:
                stage(engine, n + shift, (k + shift) % 2, *which)
    first, last = runs
    pairs = (count - 4) // 2
    for n in range(first, 2):
        run(n, n % 2)
    with engine.Fori(0, pairs) as i:
        for k in range(2):
            run(i * 2 + (2 + k), k)
    for n in range(2 * pairs + 2, count + last):
        run(n, n % 2)


class Steps:

    def __init__(self, nc, ctx, name):
        self.sem, self.k = ctx.enter_context(nc.semaphore(name)), 0

    def on(self, engine):
        def step(instruction):
            self.k += 1
            instruction.then_inc(self.sem, 1)
            engine.wait_ge(self.sem, self.k)
        return step


RSQRT_STEPS = 12


def rsqrt(step, dve, y, v, tmp, half):
    step(dve.tensor_scalar(tmp.bitcast(I32), v.bitcast(I32), 1, None, ALU.logical_shift_right))
    step(dve.tensor_scalar(y.bitcast(I32), tmp.bitcast(I32), -1.0, float(0x5F3759DF), ALU.mult, ALU.add))
    step(dve.tensor_scalar(half, v, -0.5, None, ALU.mult))
    for _ in range(3):
        step(dve.tensor_tensor(tmp, y, y, ALU.mult))
        step(dve.tensor_tensor(tmp, tmp, half, ALU.mult))
        step(dve.scalar_tensor_tensor(y, tmp, 1.5, y, ALU.add, ALU.mult))


class Core:

    def __init__(self, nc, ctx):
        def sb(name, shape, dt=F32):
            return ctx.enter_context(nc.sbuf_tensor(name, shape, dt))
        self.x = sb("x", [P, TILES, D])
        self.mv = sb("mv", [P, TILES, 2])
        self.rs = sb("rs", [P, TILES])
        self.var = sb("var", [P, TILES])
        self.tmp = sb("ln_tmp", [P, TILES])
        self.half = sb("ln_half", [P, TILES])
        self.stat = sb("stat", [P, TT * TT, 6])
        self.agg = sb("agg", [P, TT * TT, 2])
        self.mod = sb("mod", [P, 2, 6, B])
        self.id32 = sb("id32", [P, P])
        self.id16 = sb("id16", [P, P], F16)


LN_STEPS = 1 + RSQRT_STEPS


def ln_scales(step, dve, c):
    step(dve.tensor_scalar(c.var[:, :], c.mv[:, :, 1], LN_EPS, None, ALU.add))
    rsqrt(step, dve, c.rs[:, :], c.var[:, :], c.tmp[:, :], c.half[:, :])


def normalise(dve, c, out, tile):
    return dve.tensor_scalar(out, c.x[:, bass.ds(tile, 1), :].rearrange("p a d -> p (a d)"),
                             c.mv[:, bass.ds(tile, 1), 0], c.rs[:, bass.ds(tile, 1)],
                             ALU.subtract, ALU.mult)


def x_tiles(c, tile, count):
    return c.x[:, bass.ds(tile, count), :]


ADD_STEPS = 4


def add_and_measure(dve, c, s_st, n, tiles, out):
    xt = x_tiles(c, n * tiles, tiles)
    s_st.up(dve.tensor_tensor(xt, xt, out.rearrange("p (t d) -> p t d", t=tiles), ALU.add))
    s_st.wait_apart(dve, n, 1)
    for t in range(tiles):
        last = dve.bn_stats(c.stat[:, t, :], x_tiles(c, n * tiles + t, 1).rearrange("p a d -> p (a d)"))
    s_st.up(last)
    s_st.wait_apart(dve, n, 2)
    for t in range(tiles):
        last = dve.bn_aggr(c.agg[:, t, :], c.stat[:, t, :])
    s_st.up(last)
    s_st.wait(dve, n, 3)
    s_st.up(dve.tensor_copy(c.mv[:, bass.ds(n * tiles, tiles), :], c.agg[:, 0:tiles, :]))


def setup(nc, c, ins):
    with ExitStack() as ctx:
        def sb(name, shape, dt=F32):
            return ctx.enter_context(nc.sbuf_tensor(name, shape, dt))
        CH = 8
        TC = TILES // CH
        cin = [sb(f"cin{l}", [B, D]) for l in range(2)]
        sg = [sb(f"sg{l}", [B, D]) for l in range(2)]
        wmod = [sb(f"wmod{l}", [D, 6 * D]) for l in range(2)]
        cT = sb("cT", [D, 2, B])
        sgn, mag = sb("sgn", [P, B]), sb("mag", [P, B])
        st = sb("st", [P, TILES, 6])
        psc = ctx.enter_context(nc.psum_tensor("psc", [D, BANK], F32))
        psm = [ctx.enter_context(nc.psum_tensor(f"psm{l}", [D, BANK], F32)) for l in range(2)]
        s_c = [Signal(nc, ctx, f"su_c{l}", 32) for l in range(2)]
        s_x = [Signal(nc, ctx, f"su_x{k}", 16) for k in range(CH)]
        s_id = Signal(nc, ctx, "su_id", 4)
        s_exp = Signal(nc, ctx, "su_exp", 2)
        s_silu = Signal(nc, ctx, "su_silu", 1)
        s_cT = Signal(nc, ctx, "su_cT", 1)
        s_cTs = Signal(nc, ctx, "su_cTs", 1)
        s_mod = Signal(nc, ctx, "su_mod", 1)
        s_st = Signal(nc, ctx, "su_st", 1)
        steps = Steps(nc, ctx, "su_dve")
        x_dram = ins["L0_attn_tokens"].rearrange("b (t p) d -> p (b t) d", p=P)
        block = ctx.enter_context(nc.Block())

        @block.sync
        def _(sp):
            for l in range(2):
                s_c[l].up(sp.dma_start(cin[l][:, :], ins[f"L{l}_c"]), 16)
                s_c[l].up(sp.dma_start(wmod[l][:, :], ins[f"L{l}_wmod"]), 16)
            for k in range(CH):
                s_x[k].up(sp.dma_start(c.x[:, k * TC:(k + 1) * TC, :], x_dram[:, k * TC:(k + 1) * TC, :]), 16)

        @block.gpsimd
        def _(gp):
            s_id.up(gp.memset(c.id32[:, :], 0.0))
            s_id.up(gp.memset(c.id16[:, :], 0.0))
            s_id.wait(gp, 0, 2)
            for m in (c.id32, c.id16):
                s_id.up(gp.affine_select(out=m[:, :], in_=m[:, :], compare_op=ALU.not_equal, fill=1.0,
                                         base=0, pattern=[[-1, P]], channel_multiplier=1))

        @block.scalar
        def _(act):
            for l in range(2):
                s_c[l].wait(act, 0)
                s_exp.up(act.activation(sg[l][:, :], cin[l][:, :], ACT.Exp, scale=-1.0))

        @block.tensor
        def _(pe):
            s_id.wait(pe, 0)
            s_silu.wait(pe, 0)
            for l in range(2):
                last = pe.transpose(psc[:, l * B:(l + 1) * B], sg[l][:, :], c.id32[0:B, 0:B])
            s_cT.up(last)
            s_cTs.wait(pe, 0)
            for l in range(2):
                s_c[l].wait(pe, 0)
                for j in range(6):
                    last = pe.matmul(psm[l][:, j * B:(j + 1) * B], wmod[l][:, j * D:(j + 1) * D],
                                     cT[:, l, :], start=True, stop=True)
            s_mod.up(last)

        @block.vector
        def _(dve):
            step = steps.on(dve)
            for l in range(2):
                s_exp.wait(dve, 0, l + 1)
                step(dve.tensor_scalar(sg[l][:, :], sg[l][:, :], 1.0, None, ALU.add))
                step(dve.reciprocal(sg[l][:, :], sg[l][:, :]))
                last = dve.tensor_tensor(sg[l][:, :], sg[l][:, :], cin[l][:, :], ALU.mult)
                if l == 0:
                    step(last)
            s_silu.up(last)
            s_cT.wait(dve, 0)
            s_cTs.up(dve.tensor_copy(cT[:, :, :].rearrange("p l b -> p (l b)"), psc[:, 0:2 * B]))
            s_mod.wait(dve, 0)
            for l in range(2):
                out, got = c.mod[:, l, :, :], psm[l][:, 0:6 * B].rearrange("p (j b) -> p j b", j=6)
                for j in (0, 3):
                    step(dve.tensor_copy(out[:, j, :], got[:, j, :]))
                    step(dve.tensor_scalar(out[:, j + 1, :], got[:, j + 1, :], 1.0, None, ALU.add))
                    step(dve.tensor_scalar(sgn[:, :], got[:, j + 2, :], 0.0, 2.0, ALU.is_ge, ALU.mult))
                    step(dve.tensor_copy(mag[:, :], got[:, j + 2, :]))
                    step(dve.scalar_tensor_tensor(mag[:, :], mag[:, :], -1.0, mag[:, :], ALU.mult, ALU.max))
                    step(dve.tensor_scalar(mag[:, :], mag[:, :], 0.25, None, ALU.max))
                    step(dve.scalar_tensor_tensor(out[:, j + 2, :], sgn[:, :], -1.0, mag[:, :], ALU.add, ALU.mult))
            for t in range(TILES):
                if t % TC == 0:
                    s_x[t // TC].wait(dve, 0)
                last = dve.bn_stats(st[:, t, :], c.x[:, t, :])
            s_st.up(last)
            s_st.wait(dve, 0)
            for t in range(TILES):
                last = dve.bn_aggr(c.mv[:, t, :], st[:, t, :])
            step(last)
            ln_scales(step, dve, c)


def attention0(nc, c, ins):
    with ExitStack() as ctx:
        def sb(name, shape, dt=F32):
            return ctx.enter_context(nc.sbuf_tensor(name, shape, dt))

        def sig(name, per=1):
            return Signal(nc, ctx, "a_" + name, per, B)
        wq, wkv = sb("wq", [D, QW]), sb("wkv", [D, 2 * KW])
        wo = sb("wo", [P, KW // P, D])
        nw = sb("nw", [D, 1])
        gam = sb("gam", [P, QW + KW])
        gk = sb("gk", [P, KW])
        ones = sb("ones", [P, 1])
        xn, hsq = sb("xn", [P, TT, D]), sb("hsq", [D, N])
        hT = [sb(f"hT{k}", [D, N]) for k in range(2)]
        sq = sb("sq", [P, QW + KW])
        qg = sb("qg", [P, TT, QW + KW])
        heads = QH + KH
        ss = sb("ss", [P, TT * heads + TT])
        rr, rtmp, rhalf = (sb(x, [P, TT * heads + TT]) for x in ("rr", "rtmp", "rhalf"))
        rlim = sb("rlim", [P, TT])
        rv = sb("rv", [P, TT])
        qp = sb("qp", [P, TT, QH, 2 * DH], F16)
        kp = sb("kp", [P, TT, KH, 3 * DH], F16)
        qs = [sb(f"qs{k}", [P, QH, N], F16) for k in range(2)]
        k1 = [sb(f"k1{k}", [P, KH, N], F16) for k in range(2)]
        k2 = [sb(f"k2{k}", [P, KH, N], F16) for k in range(2)]
        va = [sb(f"va{k}", [P, TT, KH, VC]) for k in range(2)]
        SC = HPG * (N + P)
        th = sb("th", [P, SC])
        pr = [sb(f"pr{k}", [P, SC]) for k in range(2)]
        rl = sb("rl", [P, TT, HPG])
        on = [sb(f"on{k}", [P, TT, HPG, DH]) for k in range(2)]
        as_ = sb("as", [P, TT, KW])
        at = sb("at", [P, KW // P, N])
        og = sb("og", [D, N])
        pS = ctx.enter_context(nc.psum_tensor("a_pS", [P, 3 * BANK], F32))
        pO = ctx.enter_context(nc.psum_tensor("a_pO", [P, TT, BANK], F32))
        pW = ctx.enter_context(nc.psum_tensor("a_pW", [P, 3, BANK], F32))

        s_w = Signal(nc, ctx, "a_w", 16 * 6)
        s_prep = Signal(nc, ctx, "a_prep")
        steps = Steps(nc, ctx, "a_steps")
        s_aT, s_at, s_o, s_og, s_oT, s_st = (
            sig(x, p) for x, p in (("aT", TT), ("at", TT), ("o", 1), ("og", 1), ("oT", 1), ("st", ADD_STEPS)))
        s_sc, s_th, s_pr, s_mk, s_pv, s_rl, s_on, s_as = (
            sig(x, GROUPS) for x in ("sc", "th", "pr", "mk", "pv", "rl", "on", "as"))
        BANKS = (1, 2, 0)
        s_xn, s_xT, s_hT, s_hsq, s_ms, s_msv = (sig(x) for x in ("xn", "xT", "hT", "hsq", "ms", "msv"))
        s_qk, s_sq, s_qg = (sig(x, TT * len(BANKS)) for x in ("qk", "sq", "qg"))
        s_ss, s_qn, s_hi, s_lo = (sig(x, TT) for x in ("ss", "qn", "hi", "lo"))
        s_tr, s_trv = sig("tr", 8), sig("trv", 4)
        s_trk = sig("trk", 4)
        s_v, s_va = sig("v", TT), sig("va", TT)
        chain = Chain(nc, ctx, "a_rs", RSQRT_STEPS + 1 + TT, B)

        block = ctx.enter_context(nc.Block())

        @block.sync
        def _(sp):
            for to, of in ((wq[:, :], ins["L0_attn_Wq"]), (wkv[:, :], ins["L0_attn_Wkv"]),
                           (wo[:, :, :], ins["L0_attn_Wout"].rearrange("(j p) n -> p j n", p=P)),
                           (nw[:, :], ins["L0_attn_norm_w"].rearrange("(p a) -> p a", a=1)),
                           (gam[:, 0:QW], ins["L0_attn_q_gamma"].rearrange("h d -> (h d)").partition_broadcast(P)),
                           (gk[:, :], ins["L0_attn_k_gamma"].rearrange("h d -> (h d)").partition_broadcast(P))):
                s_w.up(sp.dma_start(to, of), 16)

        def pe_transpose_x(pe, n, k):
            s_xn.wait(pe, n)
            s_qg.wait(pe, n - 1)
            for t in range(TT):
                last = pe.transpose(pW[:, 0, t * P:(t + 1) * P], xn[:, t, :], c.id32[:, :])
            s_xT.up(last)

        def pe_values(pe, n, k):
            s_qg.wait(pe, n)
            for t in range(TT):
                s_v.up(pe.matmul(pW[:, 1 + t, :], hT[k][:, t * P:(t + 1) * P], wkv[:, KW:2 * KW],
                                 start=True, stop=True))

        def pe_mean_square(pe, n, k):
            s_hsq.wait(pe, n)
            s_hT.wait(pe, n)
            for t in range(TT):
                last = pe.matmul(pW[:, 0, t:t + 1], hsq[:, t * P:(t + 1) * P], ones[:, :], start=True, stop=True)
            s_ms.up(last)

        def pe_out_transposes(pe, n, k):
            s_as.wait(pe, n)
            for t in range(TT):
                s_va.wait(pe, n + 2, t + 1)
                for j in range(KW // P):
                    last = pe.transpose(pW[:, 1 + t, j * P:(j + 1) * P], as_[:, t, j * P:(j + 1) * P], c.id32[:, :])
                s_aT.up(last)

        def pe_split_transposes(pe, n, k, t):
            s_hi.wait(pe, n, t + 1)
            s_lo.wait(pe, n, t + 1)
            for u in range(4):
                m = 4 * t + u
                if m == 0:
                    s_qg.wait(pe, n)
                    s_msv.wait(pe, n + 1)
                elif m in (1, 2):
                    s_va.wait(pe, n, m)
                    s_at.wait(pe, n - 2, m)
                elif m == 3:
                    s_trv.wait(pe, n, 1)
                elif m == 4:
                    s_trk.wait(pe, n, 2)
                elif m == 5:
                    s_trv.wait(pe, n, 2)
                    s_og.wait(pe, n - 2)
                elif m == 6:
                    s_trk.wait(pe, n, 1)
                    if not isinstance(n, int) or n >= 2:
                        s_st.wait(pe, n - 2, 1)
                else:
                    s_trv.wait(pe, n, 3)
                bank = pW[:, (0, 1, 2, 0, 0, 1, 2, 0)[m], :].bitcast(F16)
                for j in range(8):
                    src = (qp[:, t, 8 * u + j, :] if u < 2 else
                           kp[:, t, j, (u - 2) * DH:(u - 2) * DH + 2 * DH])
                    last = pe.transpose(bank[:, j * P:(j + 1) * P], src, c.id16[:, :])
                s_tr.up(last)

        def pe_out_project(pe, n, k):
            s_at.wait(pe, n)
            s_trv.wait(pe, n + 2, 2)
            for j in range(KW // P):
                last = pe.matmul(pW[:, 1, 0:N], wo[:, j, :], at[:, j, :], start=j == 0, stop=j == KW // P - 1)
            s_o.up(last)

        def pe_out_back(pe, n, k):
            s_og.wait(pe, n)
            s_trk.wait(pe, n + 2, 1)
            for t in range(TT):
                last = pe.transpose(pW[:, 2, t * P:(t + 1) * P], og[:, t * P:(t + 1) * P], c.id32[:, :])
            s_oT.up(last)

        def pe_project_qk(pe, n, k, t):
            if t == 0:
                s_hT.wait(pe, n)
                s_msv.wait(pe, n)
                s_trv.wait(pe, n - 1, 4)
                s_trk.wait(pe, n - 1, 4)
            for j, b in enumerate(BANKS):
                if t:
                    s_qg.wait(pe, n, (t - 1) * len(BANKS) + j + 1)
                w = wkv[:, 0:KW] if b == 2 else wq[:, b * BANK:(b + 1) * BANK]
                s_qk.up(pe.matmul(pW[:, b, :], hT[k][:, t * P:(t + 1) * P], w, start=True, stop=True))

        def pe_scores(pe, n, k, g):
            if g == 0:
                s_trv.wait(pe, n)
                s_trk.wait(pe, n)
            s_th.wait(pe, n - 1 if g == 0 else n, GROUPS if g == 0 else g)
            for hh in range(HPG):
                h = g * HPG + hh
                for out, keys, i0 in ((pS[:, hh * N:(hh + 1) * N], 0, 0),
                                      (pS[:, HPG * N + hh * P:HPG * N + (hh + 1) * P], 1, P)):
                    for first, kk in ((True, k1[k]), (False, k2[k])):
                        last = pe.matmul(out, kk[:, h // G2, keys * P:(keys + 1) * P], qs[k][:, h, i0:N],
                                         start=first, stop=not first)
            s_sc.up(last)

        def pe_weighted_values(pe, n, k, g):
            if g == 0:
                s_va.wait(pe, n)
            s_mk.wait(pe, n, g + 1)
            s_on.wait(pe, n - 1 if g == 0 else n, GROUPS if g == 0 else g)
            p = pr[g % 2]
            for hh in range(HPG):
                v = (g * HPG + hh) // G2
                for t in range(TT):
                    out = pO[:, t, hh * VC:(hh + 1) * VC]
                    pe.matmul(out, p[:, hh * N + t * P:hh * N + (t + 1) * P], va[k][:, 0, v, :],
                              start=True, stop=t == 0)
                last = pe.matmul(out, p[:, HPG * N + hh * P:HPG * N + (hh + 1) * P], va[k][:, 1, v, :],
                                 start=False, stop=True)
            s_pv.up(last)

        PE = ((0, pe_scores, 0), (-1, pe_weighted_values, 3), (1, pe_values), (0, pe_scores, 1),
              (0, pe_weighted_values, 0), (2, pe_transpose_x), (0, pe_scores, 2), (-1, pe_out_transposes),
              (0, pe_weighted_values, 1), (2, pe_mean_square), (1, pe_split_transposes, 0), (-1, pe_out_project),
              (0, pe_scores, 3), (-1, pe_out_back), (1, pe_split_transposes, 1), (0, pe_weighted_values, 2),
              (2, pe_project_qk, 0), (2, pe_project_qk, 1))

        @block.tensor
        def _(pe):
            s_prep.wait(pe, 0)
            pipeline(pe, PE, B)

        def dve_normalise(dve, n, k):
            s_xT.wait(dve, n - 1)
            for t in range(TT):
                last = normalise(dve, c, xn[:, t, :], n * TT + t)
            s_xn.up(last)

        def dve_modulate(dve, n, k):
            s_xT.wait(dve, n)
            s_v.wait(dve, n - 2)
            s_hT.up(dve.tensor_scalar(hT[k][:, :], pW[:, 0, 0:N], c.mod[:, 0, 1, bass.ds(n, 1)],
                                      c.mod[:, 0, 0, bass.ds(n, 1)], ALU.mult, ALU.add))

        def dve_mean_square(dve, n, k):
            s_ms.wait(dve, n)
            chain.raised.wait(dve, n - 1)
            s_msv.up(dve.tensor_scalar(ss[:, TT * heads:], pW[:, 0, 0:TT], RMS_EPS, None, ALU.add))

        def dve_gains(dve, n, k, t):
            if t == 0:
                s_hi.wait(dve, n - 1)
                s_lo.wait(dve, n - 1)
            for j, b in enumerate(BANKS):
                s_sq.wait(dve, n, t * len(BANKS) + j + 1)
                cols = slice(b * BANK, (b + 1) * BANK)
                s_qg.up(dve.tensor_tensor(qg[:, t, cols], pW[:, b, :], gam[:, cols], ALU.mult))
            s_ss.up(dve.tensor_reduce(ss[:, t * heads:(t + 1) * heads],
                                      sq[:, :].rearrange("p (h d) -> p h d", d=DH), AX.X, ALU.add))

        def dve_factors(dve, n, k):
            chain.begin(dve, n)
            s_ss.wait(dve, n)
            s_msv.wait(dve, n)
            s_va.wait(dve, n - 1)
            s_qn.wait(dve, n - 1)
            rsqrt(chain.step, dve, rr[:, :], ss[:, :], rtmp[:, :], rhalf[:, :])
            dve.tensor_copy(rv[:, :], rr[:, TT * heads:])
            chain.step(dve.tensor_scalar(rlim[:, :], rr[:, TT * heads:], 1e12, None, ALU.mult))
            for t in range(TT):
                r = rr[:, t * heads:(t + 1) * heads]
                chain.step(dve.tensor_scalar(r, r, rlim[:, t:t + 1], None, ALU.min))
            chain.end()

        def dve_norm(dve, n, k, t):
            if t == 0:
                s_qg.wait(dve, n)
            r = rr[:, t * heads:(t + 1) * heads].unsqueeze(2).broadcast_to((P, heads, DH))
            q = qg[:, t, :].rearrange("p (h d) -> p h d", d=DH)
            s_qn.up(dve.tensor_tensor(q, q, r, ALU.mult))

        def dve_outputs(dve, n, k, g):
            s_pv.wait(dve, n, g + 1)
            s_as.wait(dve, n - 1 if g < 2 else n, GROUPS + g - 1 if g < 2 else g - 1)
            o = pO[:, :, 0:HPG * VC].rearrange("p t (h w) -> p t h w", w=VC)
            s_rl.up(dve.reciprocal(rl[:, :, :], o[:, :, :, DH]))
            s_rl.wait(dve, n, g + 1)
            for t in range(TT):
                last = dve.tensor_tensor(on[g % 2][:, t, :, :], o[:, t, :, 0:DH],
                                         rl[:, t, :].unsqueeze(2).broadcast_to((P, HPG, DH)), ALU.mult)
            s_on.up(last)

        def dve_take_q(dve, n, k, t):
            if t == 0:
                s_sc.wait(dve, n - 2)
            for u in range(2):
                m = 4 * t + u
                s_tr.wait(dve, n, m + 1)
                s_trv.up(dve.tensor_copy(qs[k][:, 8 * u:8 * u + 8, t * P:(t + 1) * P],
                                         pW[:, u, :].bitcast(F16).rearrange("p (h i) -> p h i", i=P)))

        def dve_gate(dve, n, k):
            s_o.wait(dve, n)
            s_oT.wait(dve, n - 1)
            s_og.up(dve.tensor_scalar(og[:, :], pW[:, 1, 0:N], c.mod[:, 0, 2, bass.ds(n, 1)], None, ALU.mult))

        def dve_add(dve, n, k):
            s_oT.wait(dve, n)
            add_and_measure(dve, c, s_st, n, TT, pW[:, 2, 0:N])

        DVE = ((-1, dve_outputs, 3), (1, dve_factors), (1, dve_norm, 0), (0, dve_outputs, 0), (2, dve_normalise),
               (1, dve_norm, 1), (2, dve_modulate), (2, dve_mean_square), (0, dve_outputs, 1),
               (1, dve_take_q, 0), (-1, dve_gate), (-1, dve_add), (1, dve_take_q, 1), (0, dve_outputs, 2),
               (2, dve_gains, 0), (2, dve_gains, 1))

        @block.vector
        def _(dve):
            step = steps.on(dve)
            s_w.wait(dve, 0)
            step(dve.tensor_scalar(wq[:, :], wq[:, :], nw[:, 0:1], None, ALU.mult))
            step(dve.tensor_scalar(wkv[:, :], wkv[:, :], nw[:, 0:1], None, ALU.mult))
            step(dve.tensor_scalar(gam[:, 0:QW], gam[:, 0:QW], 1.0, float(DH) ** 0.5, ALU.add, ALU.mult))
            step(dve.tensor_scalar(gk[:, :], gk[:, :], 1.0, None, ALU.add))
            gq = gam[:, 0:QW].rearrange("p (h g d) -> p h g d", g=G2, d=DH)
            for g in range(G2):
                step(dve.tensor_tensor(gq[:, :, g, :], gq[:, :, g, :],
                                       gk[:, :].rearrange("p (h d) -> p h d", d=DH), ALU.mult))
            step(dve.memset(gam[:, QW:], float(DH) ** 0.5))
            step(dve.memset(ones[:, :], 1.0 / D))
            step(dve.memset(va[0][:, :, :, DH:VC], 1.0))
            s_prep.up(dve.memset(va[1][:, :, :, DH:VC], 1.0))
            pipeline(dve, DVE, B)
            s_st.wait(dve, B - 1)
            ln_scales(step, dve, c)

        def act_square_qk(act, n, k, t):
            for j, b in enumerate(BANKS):
                s_qk.wait(act, n, t * len(BANKS) + j + 1)
                if j == 0:
                    s_ss.wait(act, n - 1 if t == 0 else n, TT if t == 0 else t)
                s_sq.up(act.activation(sq[:, b * BANK:(b + 1) * BANK], pW[:, b, :], ACT.Square))

        def act_hi(act, n, k, t):
            s_qn.wait(act, n, t + 1)
            s_tr.wait(act, n - 1, 4 * t + 4)
            act.activation(qp[:, t, :, 0:DH], qg[:, t, 0:QW].rearrange("p (h d) -> p h d", d=DH), ACT.Copy)
            k = qg[:, t, QW:].rearrange("p (h d) -> p h d", d=DH)
            act.activation(kp[:, t, :, 0:DH], k, ACT.Copy)
            s_hi.up(act.activation(kp[:, t, :, 2 * DH:3 * DH], k, ACT.Copy))

        def act_softmax(act, n, k, g):
            s_sc.wait(act, n, g + 1)
            s_pr.wait(act, n - 1 if g == 0 else n, GROUPS if g == 0 else g)
            s_th.up(act.activation(th[:, :], pS[:, :], ACT.Tanh, scale=1.0 / SOFTCLAMP))
            s_th.wait(act, n, g + 1)
            s_pv.wait(act, n - 1 if g < 2 else n, GROUPS + g - 1 if g < 2 else g - 1)
            s_pr.up(act.activation(pr[g % 2][:, :], th[:, :], ACT.Exp, scale=SOFTCLAMP * DH ** -0.5))

        def act_take_heads(act, n, k):
            s_o.wait(act, n - 1)
            for t in range(TT):
                s_aT.wait(act, n, t + 1)
                s_at.up(act.activation(at[:, :, t * P:(t + 1) * P],
                                       pW[:, 1 + t, :].rearrange("p (j i) -> p j i", i=P), ACT.Copy))

        def act_take_k(act, n, k, t):
            if t == 0:
                s_sc.wait(act, n - 2)
            for u in range(2):
                m = 4 * t + 2 + u
                s_tr.wait(act, n, m + 1)
                s_trk.up(act.activation((k1, k2)[u][k][:, :, t * P:(t + 1) * P],
                                        pW[:, 2 - 2 * u, :].bitcast(F16).rearrange("p (h i) -> p h i", i=P), ACT.Copy))

        def act_take_values(act, n, k):
            s_pv.wait(act, n - 2)
            chain.raised.wait(act, n, RSQRT_STEPS + 1)
            for t in range(TT):
                s_v.wait(act, n, t + 1)
                s_va.up(act.activation(va[k][:, t, :, 0:DH], pW[:, 1 + t, :].rearrange("p (h d) -> p h d", d=DH),
                                       ACT.Copy, scale=rv[:, t:t + 1]))

        ACTS = ((0, act_softmax, 0), (0, act_softmax, 1), (1, act_take_values), (1, act_hi, 0),
                (0, act_softmax, 2), (1, act_hi, 1), (-1, act_take_heads), (1, act_take_k, 0),
                (0, act_softmax, 3), (1, act_take_k, 1), (2, act_square_qk, 0), (2, act_square_qk, 1))

        @block.scalar
        def _(act):
            pipeline(act, ACTS, B)

        def gp_square_h(gp, n, k):
            s_hT.wait(gp, n)
            s_ms.wait(gp, n - 1)
            s_hsq.up(gp.tensor_tensor(hsq[:, :], hT[k][:, :], hT[k][:, :], ALU.mult))

        def gp_lo(gp, n, k, t):
            s_hi.wait(gp, n, t + 1)
            gp.tensor_tensor(qp[:, t, :, DH:2 * DH], qg[:, t, 0:QW].rearrange("p (h d) -> p h d", d=DH),
                             qp[:, t, :, 0:DH], ALU.subtract)
            s_lo.up(gp.tensor_tensor(kp[:, t, :, DH:2 * DH], qg[:, t, QW:].rearrange("p (h d) -> p h d", d=DH),
                                     kp[:, t, :, 0:DH], ALU.subtract))

        def gp_mask(gp, n, k, g):
            s_pr.wait_apart(gp, n, g + 1)
            p = pr[g % 2]
            for part in (p[:, 0:HPG * N].rearrange("p (h i) -> p h i", i=N)[:, :, 0:P],
                         p[:, HPG * N:].rearrange("p (h i) -> p h i", i=P)):
                last = gp.affine_select(out=part, in_=part, compare_op=ALU.is_ge, fill=0.0, base=0,
                                        pattern=[[0, HPG], [1, P]], channel_multiplier=-1)
            s_mk.up(last)

        def gp_sum(gp, n, k, g):
            s_on.wait(gp, n, g + 1)
            if g == 0:
                s_aT.wait(gp, n - 1)
            o = on[g % 2][:, :, :, :].rearrange("p t (h g) d -> p t h g d", g=G2)
            w = HPG // G2 * DH
            for t in range(TT):
                last = gp.tensor_tensor(as_[:, t, g * w:(g + 1) * w].rearrange("p (h d) -> p h d", d=DH),
                                        o[:, t, :, 0, :], o[:, t, :, 1, :], ALU.add)
            s_as.up(last)

        GP = ((0, gp_mask, 0), (-1, gp_sum, 3), (0, gp_mask, 1), (2, gp_square_h), (1, gp_lo, 0),
              (0, gp_sum, 0), (0, gp_mask, 2), (1, gp_lo, 1), (0, gp_sum, 1), (0, gp_mask, 3), (0, gp_sum, 2))

        @block.gpsimd
        def _(gp):
            pipeline(gp, GP, B)


class Turner:

    def __init__(self, nc, ctx, c, name, banks):
        self.c, self.banks, self.groups = c, banks, []
        self.turned = Signal(nc, ctx, name + "_turned", 1)
        self.taken = Signal(nc, ctx, name + "_taken", 1)

    def add(self, out, blocks):
        self.groups.append((out, blocks))

    def tensor(self, pe):
        nb = len(self.banks)
        for m, (_, blocks) in enumerate(self.groups):
            self.taken.wait(pe, m - nb)
            at = 0
            for b in blocks:
                rows, cols = b.shape
                last = pe.transpose(self.banks[m % nb][0:cols, at:at + rows], b, self.c.id32[0:rows, 0:rows])
                at += rows
            self.turned.up(last)

    def vector(self, dve):
        for m, (out, blocks) in enumerate(self.groups):
            self.turned.wait(dve, m)
            rows, cols = sum(b.shape[0] for b in blocks), blocks[0].shape[1]
            self.taken.up(dve.tensor_copy(out, self.banks[m % len(self.banks)][0:cols, 0:rows]))

    def wait(self, engine):
        self.taken.wait(engine, len(self.groups) - 1)


def moe(nc, c, ins):
    with ExitStack() as ctx:
        def sb(name, shape, dt=F32):
            return ctx.enter_context(nc.sbuf_tensor("b_" + name, shape, dt))

        def sig(name, per=1):
            return Signal(nc, ctx, "b_" + name, per)
        S2 = 2
        RUNS = B // S2
        T4, W = S2 * TT, S2 * N
        RT, ST = E * EI // P, SI // P
        IT = RT + ST
        DEPTH = 3
        un, dn, gn = sb("un", [P, IT, D]), sb("dn", [D, IT * P]), sb("gn", [E, D])
        uT, dT, gT = sb("uT", [D, IT * P]), sb("dT", [P, IT * D]), sb("gT", [D, E])
        bias = sb("bias", [P, E])
        sel = sb("sel", [2 * E, RT, P], F16)
        lt4, lt16 = sb("lt4", [P, NG, NG]), sb("lt16", [P, E, E])
        xn = sb("xn", [P, T4, D])
        hT = [sb(f"hT{k}", [D, W]) for k in range(2)]
        s, sc, mk, cw, rank = (sb(x, [P, T4, E]) for x in ("s", "sc", "mk", "cw", "rank"))
        pm, qm = sb("pm", [P, T4 * NG, 2]), sb("qm", [P, T4 * NG, 2])
        m1, m2, m3, gs, gr = (sb(x, [P, T4 * NG]) for x in ("m1", "m2", "m3", "gs", "gr"))
        gt4, eq4 = sb("gt4", [P, T4, NG, NG]), sb("eq4", [P, T4, NG, NG])
        gt16, eq16 = sb("gt16", [P, T4, E, E]), sb("eq16", [P, T4, E, E])
        tot = sb("tot", [P, T4])
        cwp = sb("cwp", [P, T4, 2 * E], F16)
        cwT = [sb(f"cwT{k}", [2 * E, W], F16) for k in range(2)]
        r = [sb(f"r{k}", [P, W]) for k in range(3)]
        rc = [sb(f"rc{k}", [P, W]) for k in range(3)]
        a = [sb(f"a{k}", [P, W]) for k in range(4)]
        og = sb("og", [D, W])
        pX, pR, pD, pB = (ctx.enter_context(nc.psum_tensor("b_p" + x, [P, BANK], F32)) for x in "XRDB")
        pU = [ctx.enter_context(nc.psum_tensor(f"b_pU{k}", [P, BANK], F32)) for k in range(2)]
        pC = [ctx.enter_context(nc.psum_tensor(f"b_pC{k}", [P, BANK], F32)) for k in range(2)]

        s_w, s_k, s_km = Signal(nc, ctx, "b_w", 16 * 6), sig("k", 5), sig("km")
        steps = Steps(nc, ctx, "b_steps")
        turner = Turner(nc, ctx, c, "b", [pU[0], pU[1], pC[0], pC[1]])
        s_xn, s_xT, s_hT, s_lg, s_ex, s_cT, s_cw = (
            sig(x, p) for x, p in (("xn", 1), ("xT", 1), ("hT", 1), ("lg", 1), ("ex", 1), ("cT", 1), ("cw", 1)))
        s_up, s_r, s_dn, s_a = (sig(x, IT) for x in ("up", "r", "dn", "a"))
        s_cb, s_rc = sig("cb", RT), sig("rc", RT)
        s_og, s_oT, s_st = sig("og"), sig("oT"), sig("st", ADD_STEPS)
        for lo in range(0, IT, 4):
            hi = min(lo + 4, IT)
            turner.add(uT[:, lo * P:hi * P], [un[:, t, :] for t in range(lo, hi)])
        for lo in range(0, IT, 4):
            hi = min(lo + 4, IT)
            turner.add(dT[:, lo * D:hi * D], [dn[:, t * P:(t + 1) * P] for t in range(lo, hi)])
        turner.add(gT[:, :], [gn[:, :]])

        block = ctx.enter_context(nc.Block())

        @block.sync
        def _(sp):
            for to, of in ((un[:, 0:RT, :], ins["L0_ffn_up_w"].rearrange("e i d -> (e i) d").rearrange("(t p) d -> p t d", p=P)),
                           (un[:, RT:IT, :], ins["L0_ffn_shared_up"].rearrange("(t p) d -> p t d", p=P)),
                           (dn[:, 0:RT * P].rearrange("p (e i) -> p e i", i=EI), ins["L0_ffn_down_w"].rearrange("e d i -> d e i")),
                           (dn[:, RT * P:], ins["L0_ffn_shared_down"]),
                           (gn[:, :], ins["L0_ffn_gate_w"]),
                           (bias[:, :], ins["L0_ffn_bias_e"].partition_broadcast(P))):
                s_w.up(sp.dma_start(to, of), 16)

        def pe_front(pe, n):
            s_xn.wait(pe, n)
            s_hT.wait(pe, n - 1)
            for t in range(T4):
                last = pe.transpose(pX[:, t * P:(t + 1) * P], xn[:, t, :], c.id32[:, :])
            s_xT.up(last)

        def pe_route(pe, n, k):
            s_hT.wait(pe, n)
            s_cw.wait(pe, n - 1)
            for t in range(T4):
                last = pe.matmul(pR[:, t * E:(t + 1) * E], hT[k][:, t * P:(t + 1) * P], gT[:, :], start=True, stop=True)
            s_lg.up(last)

        def pe_turn_weights(pe, n):
            chain.raised.wait(pe, n)
            out = pR[0:2 * E, BANK // 2:BANK].bitcast(F16)
            for t in range(T4):
                last = pe.transpose(out[:, t * P:(t + 1) * P], cwp[:, t, :], c.id16[:, :])
            s_cT.up(last)

        def pe_up(pe, n, t, k):
            before = n * IT + t - 2
            pe_at(pe, s_r, before)
            s_up.up(pe.matmul(pU[t % 2][:, :], uT[:, t * P:(t + 1) * P], hT[k][:, :], start=True, stop=True))
            if t < RT:
                pe_at(pe, s_rc, n * RT + t - 2)
                if t == 0:
                    s_cw.wait(pe, n)
                s_cb.up(pe.matmul(pC[t % 2][:, :], sel[:, t, :], cwT[k][:, :], start=True, stop=True))

        def pe_at(engine, signal, count):
            if isinstance(count, int) and count < 0:
                return
            engine.wait_ge(signal.sem, count + 1)

        def pe_down(pe, n, t):
            s_a.wait(pe, n, t + 1)
            if t == 0:
                s_og.wait(pe, n - 1)
            s_dn.up(pe.matmul(pD[:, :], dT[:, t * D:(t + 1) * D], a[t % 4][:, :], start=t == 0, stop=t == IT - 1))

        def pe_back(pe, n):
            s_og.wait(pe, n)
            for t in range(T4):
                last = pe.transpose(pB[:, t * P:(t + 1) * P], og[:, t * P:(t + 1) * P], c.id32[:, :])
            s_oT.up(last)

        def pe_run(pe, n, k, tail=True, front=True):
            for t in range(IT + DEPTH):
                if t < IT:
                    pe_up(pe, n, t, k)
                if t == 0 and front:
                    pe_front(pe, n + 1)
                if t == 1 and front:
                    pe_route(pe, n + 1, 1 - k)
                if t == 2 and tail:
                    pe_back(pe, n - 1)
                if t == IT + 1 and front:
                    pe_turn_weights(pe, n + 1)
                if t >= DEPTH:
                    pe_down(pe, n, t - DEPTH)

        chain = Chain(nc, ctx, "b_rt", 29)

        def runs(engine, run):
            run(engine, 0, 0, tail=False)
            with engine.Fori(0, (RUNS - 2) // 2) as i:
                run(engine, i * 2 + 1, 1)
                run(engine, i * 2 + 2, 0)
            run(engine, RUNS - 1, 1, front=False)

        @block.tensor
        def _(pe):
            s_w.wait(pe, 0)
            turner.tensor(pe)
            turner.wait(pe)
            s_k.wait(pe, 0)
            s_km.wait(pe, 0)
            pe_front(pe, 0)
            pe_route(pe, 0, 0)
            pe_turn_weights(pe, 0)
            runs(pe, pe_run)
            pe_back(pe, RUNS - 1)

        def dve_front(dve, n, k):
            s_xT.wait(dve, n - 1)
            for t in range(T4):
                last = normalise(dve, c, xn[:, t, :], n * T4 + t)
            s_xn.up(last)

        def dve_modulate(dve, n, k):
            s_xT.wait(dve, n)
            for m in range(S2):
                last = dve.tensor_scalar(hT[k][:, m * N:(m + 1) * N], pX[:, m * N:(m + 1) * N],
                                         c.mod[:, 0, 4, bass.ds(n * S2 + m, 1)], c.mod[:, 0, 3, bass.ds(n * S2 + m, 1)],
                                         ALU.mult, ALU.add)
            s_hT.up(last)

        def dve_routing(dve, n):
            tt, ts, stt = dve.tensor_tensor, dve.tensor_scalar, dve.scalar_tensor_tensor

            def rows(x):
                return x[:, :, :].rearrange("p t (g e) -> p (t g) e", e=EG)
            pairs = rows(sc).rearrange("p a (x y) -> p a x y", y=2)
            g3 = gs[:, :].rearrange("p (t g) -> p t g", g=NG)
            s4, s16 = (P, T4, NG, NG), (P, T4, E, E)
            a4, b4 = g3.unsqueeze(2).broadcast_to(s4), g3.unsqueeze(3).broadcast_to(s4)
            a16, b16 = mk[:, :, :].unsqueeze(2).broadcast_to(s16), mk[:, :, :].unsqueeze(3).broadcast_to(s16)
            return [
                lambda: (s_ex.wait(dve, n), ts(s[:, :, :], s[:, :, :], 1.0, None, ALU.add))[1],
                lambda: dve.reciprocal(s[:, :, :], s[:, :, :]),
                lambda: tt(sc[:, :, :], s[:, :, :], bias[:, :].unsqueeze(1).broadcast_to((P, T4, E)), ALU.add),
                lambda: tt(pm[:, :, :], pairs[:, :, :, 0], pairs[:, :, :, 1], ALU.max),
                lambda: tt(qm[:, :, :], pairs[:, :, :, 0], pairs[:, :, :, 1], ALU.min),
                lambda: tt(m1[:, :], pm[:, :, 0], pm[:, :, 1], ALU.max),
                lambda: tt(m2[:, :], pm[:, :, 0], pm[:, :, 1], ALU.min),
                lambda: tt(m3[:, :], qm[:, :, 0], qm[:, :, 1], ALU.max),
                lambda: tt(m2[:, :], m2[:, :], m3[:, :], ALU.max),
                lambda: tt(gs[:, :], m1[:, :], m2[:, :], ALU.add),
                lambda: tt(gt4[:, :, :, :], a4, b4, ALU.is_gt),
                lambda: tt(eq4[:, :, :, :], a4, b4, ALU.is_equal),
                lambda: tt(eq4[:, :, :, :], eq4[:, :, :, :], lt4[:, :, :].unsqueeze(1).broadcast_to(s4), ALU.mult),
                lambda: tt(gt4[:, :, :, :], gt4[:, :, :, :], eq4[:, :, :, :], ALU.add),
                lambda: dve.tensor_reduce(gr[:, :], gt4[:, :, :, :].rearrange("p t a b -> p (t a) b"), AX.X, ALU.add),
                lambda: ts(gr[:, :], gr[:, :], float(TOPG), None, ALU.is_lt),
                lambda: tt(rows(mk), rows(sc), gr[:, :].unsqueeze(2).broadcast_to((P, T4 * NG, EG)), ALU.mult),
                lambda: tt(gt16[:, :, :, :], a16, b16, ALU.is_gt),
                lambda: tt(eq16[:, :, :, :], a16, b16, ALU.is_equal),
                lambda: tt(eq16[:, :, :, :], eq16[:, :, :, :], lt16[:, :, :].unsqueeze(1).broadcast_to(s16), ALU.mult),
                lambda: tt(gt16[:, :, :, :], gt16[:, :, :, :], eq16[:, :, :, :], ALU.add),
                lambda: dve.tensor_reduce(rank[:, :, :], gt16[:, :, :, :], AX.X, ALU.add),
                lambda: stt(cw[:, :, :], rank[:, :, :], float(TOPK), s[:, :, :], ALU.is_lt, ALU.mult),
                lambda: dve.tensor_reduce(tot[:, :], cw[:, :, :], AX.X, ALU.add),
                lambda: ts(tot[:, :], tot[:, :], 1e-20, None, ALU.add),
                lambda: dve.reciprocal(tot[:, :], tot[:, :]),
                lambda: stt(cw[:, :, :], cw[:, :, :], ROUTED, tot[:, :].unsqueeze(2).broadcast_to((P, T4, E)), ALU.mult, ALU.mult),
                lambda: (s_cT.wait(dve, n - 1), dve.tensor_copy(cwp[:, :, 0:E], cw[:, :, :]))[1],
                lambda: tt(cwp[:, :, E:2 * E], cw[:, :, :], cwp[:, :, 0:E], ALU.subtract),
            ]

        def dve_take_weights(dve, n, k):
            s_cT.wait(dve, n)
            s_cw.up(dve.tensor_copy(cwT[k][:, :], pR[0:2 * E, BANK // 2:BANK].bitcast(F16)))

        def dve_weigh(dve, n, t):
            s_r.wait(dve, n, t + 1)
            s_cb.wait(dve, n, t + 1)
            pe_at(dve, s_a, n * IT + t - 3)
            s_rc.up(dve.tensor_tensor(rc[t % 3][:, :], r[t % 3][:, :], pC[t % 2][:, :], ALU.mult))

        def dve_gate(dve, n):
            s_dn.wait(dve, n)
            s_oT.wait(dve, n - 1)
            for m in range(S2):
                last = dve.tensor_scalar(og[:, m * N:(m + 1) * N], pD[:, m * N:(m + 1) * N],
                                         c.mod[:, 0, 5, bass.ds(n * S2 + m, 1)], None, ALU.mult)
            s_og.up(last)

        def dve_add(dve, n):
            s_oT.wait(dve, n)
            add_and_measure(dve, c, s_st, n, T4, pB[:, :])

        def dve_run(dve, n, k, tail=True, front=True):
            todo = []
            if front:
                dve_front(dve, n + 1, 1 - k)
                chain.begin(dve, n + 1)
                chain.raised.wait(dve, n)
                todo = dve_routing(dve, n + 1)
            if tail:
                dve_gate(dve, n - 1)
            if front:
                dve_modulate(dve, n + 1, 1 - k)
            for t in range(RT):
                dve_weigh(dve, n, t)
                for step in todo[:4]:
                    chain.step(step())
                todo = todo[4:]
                if t == 2 and tail:
                    dve_add(dve, n - 1)
            if front:
                chain.end()
                dve_take_weights(dve, n + 1, 1 - k)

        @block.vector
        def _(dve):
            turner.vector(dve)
            dve_front(dve, 0, 0)
            dve_modulate(dve, 0, 0)
            s_km.wait(dve, 0)
            chain.begin(dve, 0)
            for step in dve_routing(dve, 0):
                chain.step(step())
            chain.end()
            dve_take_weights(dve, 0, 0)
            runs(dve, dve_run)
            dve_gate(dve, RUNS - 1)
            dve_add(dve, RUNS - 1)
            s_st.wait(dve, RUNS - 1)
            ln_scales(steps.on(dve), dve, c)

        def act_exp(act, n):
            s_lg.wait(act, n)
            chain.raised.wait(act, n - 1, 23)
            s_ex.up(act.activation(s[:, :, :].rearrange("p t e -> p (t e)"), pR[:, 0:T4 * E], ACT.Exp, scale=-1.0))

        def act_relu(act, n, t):
            s_up.wait(act, n, t + 1)
            pe_at(act, s_a, n * IT + t - 3)
            s_r.up(act.activation(r[(t) % 3][:, :], pU[t % 2][:, :], ACT.Relu))

        def act_run(act, n, k, tail=True, front=True):
            for t in range(IT):
                act_relu(act, n, t)
                if t == 2 and front:
                    act_exp(act, n + 1)

        @block.scalar
        def _(act):
            act_exp(act, 0)
            runs(act, act_run)

        def gp_square(gp, n, t):
            if t < RT:
                s_rc.wait(gp, n, t + 1)
            else:
                s_r.wait(gp, n, t + 1)
            pe_at(gp, s_dn, n * IT + t - 4)
            other = rc[t % 3] if t < RT else r[t % 3]
            s_a.up(gp.tensor_tensor(a[t % 4][:, :], r[t % 3][:, :], other[:, :], ALU.mult))

        def gp_run(gp, n, k, tail=True, front=True):
            for t in range(IT):
                gp_square(gp, n, t)

        @block.gpsimd
        def _(gp):
            s_k.up(gp.memset(sel[:, :, :], 0.0))
            s_k.up(gp.memset(lt4[:, :, :], 1.0))
            s_k.up(gp.memset(lt16[:, :, :], 1.0))
            for k in range(2):
                s_k.wait(gp, 0, 3 + k)
                m = sel[:, :, :].rearrange("r t (x i) -> r t x i", i=EI)
                s_k.up(gp.affine_select(out=m, in_=m, compare_op=ALU.not_equal, fill=1.0, base=k * E,
                                        pattern=[[2, RT], [1, 2], [0, EI]], channel_multiplier=-1))
            for m, w in ((lt4, NG), (lt16, E)):
                last = gp.affine_select(out=m[:, :, :], in_=m[:, :, :], compare_op=ALU.is_gt, fill=0.0, base=0,
                                        pattern=[[1, w], [-1, w]], channel_multiplier=0)
            s_km.up(last)
            runs(gp, gp_run)


def rope_tables():
    inverse = np.float32(10000.0) ** (-np.arange(0, DR, 2, dtype=np.float32) / np.float32(DR))
    angle = np.arange(N, dtype=np.float32)[:, None] * inverse
    both = [f(angle).astype(np.float32).reshape(TT, P, DR // 2).transpose(1, 0, 2) for f in (np.cos, np.sin)]
    return np.ascontiguousarray(np.stack(both, axis=1))


def attention1(nc, c, ins):
    with ExitStack() as ctx:
        def sb(name, shape, dt=F32):
            return ctx.enter_context(nc.sbuf_tensor("c_" + name, shape, dt))

        def sig(name, per=1):
            return Signal(nc, ctx, "c_" + name, per, B)
        HD = H1 * DC
        QA = (H1 + 1) * DQ
        KA, VA_ = QA, QA + HD
        COLS = VA_ + HD
        SW = 64
        VW = 32
        SC = HPG * (N + P)
        groups = H1 // HPG
        lim = float(CLIP / np.sqrt(np.float32(DQ)))
        most, least = float(np.float32(np.exp(lim))), float(np.float32(np.exp(-lim)))
        dq_, dkv = sb("dq", [D, LAT]), sb("dkv", [D, LAT])
        up = sb("up", [LAT, 3 * HD + H1 * DR])
        dT = sb("dT", [LAT, 2, D])
        wa = sb("wa", [D, COLS])
        kr = sb("kr", [D, DR])
        wo = sb("wo", [HD, D])
        tab = sb("tab", [P, 2, TT, DR // 2])
        xn, hT = sb("xn", [P, TT, D]), sb("hT", [D, N])
        rt = [sb(f"rt{k}", [P, TT, H1 + 1, DR // 2]) for k in range(4)]
        qf, kf = sb("qf", [P, TT, H1 + 1, DQ]), sb("kf", [P, TT, H1, DQ])
        qp, kp = sb("qp", [P, TT, H1, SW], F16), sb("kp", [P, TT, H1, SW], F16)
        qs = [sb(f"qs{k}", [P, H1 // 2, N], F16) for k in range(2)]
        ks = [sb(f"ks{k}", [P, H1, N], F16) for k in range(2)]
        vs = sb("vs", [P, TT, HD])
        va = [sb(f"va{k}", [P, TT, H1, VW]) for k in range(2)]
        pr = [sb(f"pr{k}", [P, SC]) for k in range(2)]
        vu = sb("vu", [P, groups, N])
        rl = sb("rl", [P, TT, H1])
        an, at, og = sb("an", [P, TT, H1, DC]), sb("at", [HD, N]), sb("og", [D, N])
        pS = ctx.enter_context(nc.psum_tensor("c_pS", [P, 3 * BANK], F32))
        pV = [ctx.enter_context(nc.psum_tensor(f"c_pV{k}", [P, BANK], F32)) for k in range(2)]
        pW = ctx.enter_context(nc.psum_tensor("c_pW", [P, 3, BANK], F32))

        s_w = Signal(nc, ctx, "c_w", 16 * 9)
        s_wm, s_wr, s_z = (Signal(nc, ctx, "c_" + x) for x in ("wm", "wr", "z"))
        steps = Steps(nc, ctx, "c_steps")
        turner = Turner(nc, ctx, c, "c", [pV[0], pV[1]])
        turner.add(dT[:, 0, :], [dq_[:, :]])
        turner.add(dT[:, 1, :], [dkv[:, :]])
        s_sc, s_ex, s_cl, s_mk, s_pv, s_vu = (sig(x, groups) for x in ("sc", "ex", "cl", "mk", "pv", "vu"))
        s_xn, s_xT, s_hT = sig("xn"), sig("xT"), sig("hT")
        s_pj, s_f, s_rd = sig("pj"), sig("f"), sig("rd")
        s_va = sig("va")
        s_hi, s_lo = sig("hi", TT), sig("lo", TT)
        s_tr, s_ev, s_evk = sig("tr", 2 * TT), sig("ev", 3), sig("evk")
        s_aT, s_nm, s_bT, s_at, s_o, s_og, s_oT, s_st = (
            sig(x, p) for x, p in (("aT", TT), ("nm", TT), ("bT", 1), ("at", 1), ("o", 1), ("og", 1), ("oT", 1), ("st", ADD_STEPS)))
        chain = Chain(nc, ctx, "c_rl", TT, B)
        block = ctx.enter_context(nc.Block())

        @block.sync
        def _(sp):
            for to, of in ((dq_[:, :], ins["L1_attn_W_DQ"]), (dkv[:, :], ins["L1_attn_W_DKV"]),
                           (up[:, 0:HD], ins["L1_attn_W_UQ"]), (up[:, HD:2 * HD], ins["L1_attn_W_UK"]),
                           (up[:, 2 * HD:3 * HD], ins["L1_attn_W_UV"]), (up[:, 3 * HD:], ins["L1_attn_W_QR"]),
                           (kr[:, :], ins["L1_attn_W_KR"]), (wo[:, :], ins["L1_attn_W_O"]),
                           (tab[:, :, :, :], ins["rope"])):
                s_w.up(sp.dma_start(to, of), 16)

        def pe_front(pe, n, k):
            s_xn.wait(pe, n)
            s_ev.wait(pe, n - 1)
            for t in range(TT):
                last = pe.transpose(pW[:, 0, t * P:(t + 1) * P], xn[:, t, :], c.id32[:, :])
            s_xT.up(last)

        def pe_project(pe, n, k):
            s_hT.wait(pe, n)
            s_evk.wait(pe, n - 1)
            s_nm.wait(pe, n - 3, 1)
            for t in range(TT):
                last = pe.matmul(pW[:, t, 0:COLS], hT[:, t * P:(t + 1) * P], wa[:, :], start=True, stop=True)
            s_pj.up(last)

        def pe_stacks(pe, n, k, t):
            s_hi.wait(pe, n, t + 1)
            s_lo.wait(pe, n, t + 1)
            for u, src in enumerate((qp, kp)):
                if t == 0:
                    s_rd.wait(pe, n)
                else:
                    s_ev.wait(pe, n, u + 1)
                bank = pW[:, u, :].bitcast(F16)
                for j in range(H1 // 2):
                    last = pe.transpose(bank[:, j * P:(j + 1) * P],
                                        src[:, t, 2 * j:2 * j + 2, :].rearrange("p h w -> p (h w)"), c.id16[:, :])
                s_tr.up(last)

        def pe_scores(pe, n, k, g):
            if g == 0:
                s_ev.wait(pe, n)
                s_evk.wait(pe, n)
            s_ex.wait(pe, n - 1 if g == 0 else n, groups if g == 0 else g)
            for hh in range(HPG):
                h = g * HPG + hh
                pe.matmul(pS[:, hh * N:(hh + 1) * N], ks[k][:, h, 0:P], qs[k][:, h // 2, :], start=True, stop=True)
                last = pe.matmul(pS[:, HPG * N + hh * P:HPG * N + (hh + 1) * P], ks[k][:, h, P:N], qs[k][:, h // 2, P:N],
                                 start=True, stop=True)
            s_sc.up(last)

        def pe_weighted_values(pe, n, k, g):
            if g == 0:
                s_va.wait(pe, n)
            s_mk.wait(pe, n, g + 1)
            s_vu.wait(pe, n - 1 if g < 2 else n, groups + g - 1 if g < 2 else g - 1)
            for keys in range(TT):
                for hh in range(HPG):
                    rows = slice(hh * VW, (hh + 1) * VW)
                    rhs = (pr[g % 2][:, hh * N:(hh + 1) * N] if keys == 0 else
                           pr[g % 2][:, HPG * N + hh * P:HPG * N + (hh + 1) * P])
                    last = pe.matmul(pV[g % 2][rows, keys * P:N], va[k][:, keys, g * HPG + hh, :], rhs,
                                     start=keys == 0, stop=keys == TT - 1, skip_group_check=True)
            s_pv.up(last)

        def pe_heads_back(pe, n, k):
            s_vu.wait(pe, n)
            s_evk.wait(pe, n + 2)
            if not isinstance(n, int) or n >= 1:
                s_st.wait(pe, n - 1, 1)
            for t in range(TT):
                for g in range(groups):
                    last = pe.transpose(pW[:, 1 + t, g * P:(g + 1) * P], vu[:, g, t * P:(t + 1) * P], c.id32[:, :])
                s_aT.up(last)

        def pe_heads_turned(pe, n, k):
            s_nm.wait(pe, n)
            for t in range(TT):
                last = pe.transpose(pW[:, 2, t * P:(t + 1) * P], an[:, t, :, :].rearrange("p h d -> p (h d)"), c.id32[:, :])
            s_bT.up(last)

        def pe_out_project(pe, n, k):
            s_at.wait(pe, n)
            s_o.up(pe.matmul(pW[:, 2, 0:N], wo[:, :], at[:, :], start=True, stop=True))

        def pe_out_back(pe, n, k):
            s_og.wait(pe, n)
            for t in range(TT):
                last = pe.transpose(pW[:, 2, t * P:(t + 1) * P], og[:, t * P:(t + 1) * P], c.id32[:, :])
            s_oT.up(last)

        PE = ((0, pe_scores, 0), (1, pe_stacks, 0), (-1, pe_weighted_values, 3), (0, pe_scores, 1),
              (1, pe_stacks, 1), (0, pe_weighted_values, 0), (2, pe_front), (-1, pe_heads_back),
              (0, pe_scores, 2), (2, pe_project), (0, pe_weighted_values, 1), (-1, pe_heads_turned),
              (0, pe_scores, 3), (-1, pe_out_project), (0, pe_weighted_values, 2), (-1, pe_out_back))

        @block.tensor
        def _(pe):
            s_w.wait(pe, 0)
            turner.tensor(pe)
            turner.wait(pe)
            for j, (a, u) in enumerate(((0, 0), (1, 1), (1, 2), (0, 3))):
                w = HD if j < 3 else H1 * DR
                last = pe.matmul(pW[:, 0, j * HD:j * HD + w], dT[:, a, :], up[:, u * HD:u * HD + w], start=True, stop=True)
            s_wm.up(last)
            s_wr.wait(pe, 0)
            s_z.wait(pe, 0)
            pipeline(pe, PE, B)

        def dve_front(dve, n, k):
            s_xT.wait(dve, n - 1)
            for t in range(TT):
                last = normalise(dve, c, xn[:, t, :], n * TT + t)
            s_xn.up(last)

        def dve_modulate(dve, n, k):
            s_xT.wait(dve, n)
            s_pj.wait(dve, n - 1)
            s_hT.up(dve.tensor_scalar(hT[:, :], pW[:, 0, 0:N], c.mod[:, 1, 1, bass.ds(n, 1)],
                                      c.mod[:, 1, 0, bass.ds(n, 1)], ALU.mult, ALU.add))

        def dve_heads(dve, n, k):
            s_pj.wait(dve, n)
            s_hi.wait(dve, n - 1)
            s_lo.wait(dve, n - 1)
            s_f.wait(dve, n - 1)
            q = pW[:, 0:TT, 0:QA].rearrange("p t (h d) -> p t h d", d=DQ)
            x1, x2 = q[:, :, :, DC::2], q[:, :, :, DC + 1::2]
            cos, sin = (tab[:, k, :, :].unsqueeze(2).broadcast_to((P, TT, H1 + 1, DR // 2)) for k in range(2))
            for to, x, by in ((rt[0], x1, cos), (rt[1], x2, sin), (rt[2], x1, sin), (rt[3], x2, cos)):
                last = dve.tensor_tensor(to[:, :, :, :], x, by, ALU.mult)
            rope.begin(dve, n)
            rope.step(last)
            for t in range(TT):
                dve.tensor_copy(qf[:, t, 0:H1, 0:DC], q[:, t, 0:H1, 0:DC])
                dve.tensor_copy(kf[:, t, :, 0:DC], pW[:, t, KA:KA + HD].rearrange("p (h d) -> p h d", d=DC))
            dve.tensor_tensor(qf[:, :, :, DC::2], rt[0][:, :, :, :], rt[1][:, :, :, :], ALU.subtract)
            rope.step(dve.tensor_tensor(qf[:, :, :, DC + 1::2], rt[2][:, :, :, :], rt[3][:, :, :, :], ALU.add))
            for t in range(TT):
                last = dve.tensor_copy(kf[:, t, :, DC:DQ], qf[:, t, H1, DC:DQ].unsqueeze(1).broadcast_to((P, H1, DR)))
            s_f.up(last)
            rope.end()
            s_va.wait(dve, n - 1)
            s_rd.up(dve.tensor_copy(vs[:, :, :], pW[:, 0:TT, VA_:VA_ + HD]))

        rope = Chain(nc, ctx, "c_rope", 2, B)

        def take_k(engine_copy, n, k, t):
            i = slice(t * P, (t + 1) * P)
            x = pW[:, 1, :].bitcast(F16).rearrange("p (h i) -> p h i", i=P)
            engine_copy(ks[k][0:SW, 0::2, i], x[0:SW, :, :])
            return engine_copy(ks[k][SW:P, 1::2, i], x[SW:P, :, :])

        def dve_stacks(dve, n, k, t):
            if t == 0:
                s_sc.wait(dve, n - 2)
            s_tr.wait(dve, n, 2 * t + 1)
            s_ev.up(dve.tensor_copy(qs[k][:, :, t * P:(t + 1) * P],
                                    pW[:, 0, :].bitcast(F16).rearrange("p (h i) -> p h i", i=P)))
            if t == 0:
                s_tr.wait(dve, n, 2)
                s_ev.up(take_k(dve.tensor_copy, n, k, t))

        def dve_clip(dve, n, k, g):
            s_ex.wait(dve, n, g + 1)
            p = pr[g % 2][:, :]
            s_cl.up(dve.tensor_scalar(p, p, most, least, ALU.min, ALU.max))

        def dve_normalise(dve, n, k):
            chain.begin(dve, n)
            s_bT.wait(dve, n - 1)
            for t in range(TT):
                s_aT.wait(dve, n, t + 1)
                heads = pW[:, 1 + t, :].rearrange("p (h w) -> p h w", w=VW)
                chain.step(dve.reciprocal(rl[:, t, :], heads[:, :, DC]))
                s_nm.up(dve.tensor_tensor(an[:, t, :, :], heads[:, :, 0:DC],
                                          rl[:, t, :].unsqueeze(2).broadcast_to((P, H1, DC)), ALU.mult))
            chain.end()

        def dve_gate(dve, n, k):
            s_o.wait(dve, n)
            s_oT.wait(dve, n - 1)
            s_og.up(dve.tensor_scalar(og[:, :], pW[:, 2, 0:N], c.mod[:, 1, 2, bass.ds(n, 1)], None, ALU.mult))

        def dve_add(dve, n, k):
            s_oT.wait(dve, n)
            add_and_measure(dve, c, s_st, n, TT, pW[:, 2, 0:N])

        DVE = ((1, dve_stacks, 0), (0, dve_clip, 0), (1, dve_stacks, 1), (2, dve_front), (0, dve_clip, 1),
               (2, dve_modulate), (-1, dve_normalise), (0, dve_clip, 2), (2, dve_heads), (-1, dve_gate),
               (0, dve_clip, 3), (-1, dve_add))

        @block.vector
        def _(dve):
            turner.vector(dve)
            step = steps.on(dve)
            step(dve.memset(wa[:, :], 0.0))
            s_wm.wait(dve, 0)
            q = wa[:, 0:QA].rearrange("p (h d) -> p h d", d=DQ)
            dve.tensor_copy(q[:, 0:H1, 0:DC], pW[:, 0, 0:HD].rearrange("p (h d) -> p h d", d=DC))
            dve.tensor_copy(q[:, 0:H1, DC:DQ], pW[:, 0, 3 * HD:3 * HD + H1 * DR].rearrange("p (h d) -> p h d", d=DR))
            dve.tensor_copy(q[:, H1, DC:DQ], kr[:, :])
            step(dve.tensor_copy(wa[:, KA:COLS], pW[:, 0, HD:3 * HD]))
            s_wr.up(dve.memset(qf[:, :, H1, 0:DC], 0.0))
            s_z.wait(dve, 0)
            pipeline(dve, DVE, B)
            s_st.wait(dve, B - 1)
            ln_scales(step, dve, c)

        def parts(x, t, first, gap):
            return x[:, t, :, 0:4 * DQ].rearrange("p h (k d) -> p h k d", d=DQ)[:, :, first:first + gap + 1:gap, :]

        def twice(x, t):
            return x[:, t, 0:H1, :].unsqueeze(2).broadcast_to((P, H1, 2, DQ))

        def act_hi(act, n, k, t):
            s_f.wait(act, n)
            s_tr.wait(act, n - 1)
            act.activation(parts(qp, t, 0, 1), twice(qf, t), ACT.Copy)
            s_hi.up(act.activation(parts(kp, t, 0, 2), twice(kf, t), ACT.Copy))

        def act_exp(act, n, k, g):
            s_sc.wait(act, n, g + 1)
            s_pv.wait(act, n - 1 if g < 2 else n, groups + g - 1 if g < 2 else g - 1)
            s_ex.up(act.activation(pr[g % 2][:, :], pS[:, :], ACT.Exp, scale=float(1.0 / np.sqrt(np.float32(DQ)))))

        def act_take_values(act, n, k, g):
            s_pv.wait(act, n, g + 1)
            if g == 0:
                s_aT.wait(act, n - 1)
            s_vu.up(act.activation(vu[:, g, :], pV[g % 2][:, 0:N], ACT.Copy))

        def act_take_heads(act, n, k):
            s_bT.wait(act, n)
            s_o.wait(act, n - 1)
            s_at.up(act.activation(at[:, :], pW[:, 2, 0:N], ACT.Copy))

        def act_place_values(act, n, k):
            s_rd.wait(act, n)
            s_pv.wait(act, n - 2)
            s_va.up(act.activation(va[k][:, :, :, 0:DC].rearrange("p t h d -> p (t h) d"),
                                   vs[:, :, :].rearrange("p t (h d) -> p (t h) d", d=DC), ACT.Copy))

        def act_stack(act, n, k):
            s_sc.wait(act, n - 2)
            s_tr.wait(act, n)
            s_evk.up(take_k(lambda out, x: act.activation(out, x, ACT.Copy), n, k, 1))

        ACTS = ((0, act_exp, 0), (-1, act_take_values, 3), (1, act_stack), (0, act_exp, 1),
                (1, act_place_values), (0, act_take_values, 0), (0, act_exp, 2), (0, act_take_values, 1),
                (-1, act_take_heads), (0, act_exp, 3), (2, act_hi, 0), (0, act_take_values, 2), (2, act_hi, 1))

        @block.scalar
        def _(act):
            s_z.wait(act, 0)
            pipeline(act, ACTS, B)

        def gp_lo(gp, n, k, t):
            s_hi.wait(gp, n, t + 1)
            gp.tensor_tensor(parts(qp, t, 2, 1), twice(qf, t), parts(qp, t, 0, 1), ALU.subtract)
            s_lo.up(gp.tensor_tensor(parts(kp, t, 1, 2), twice(kf, t), parts(kp, t, 0, 2), ALU.subtract))

        def gp_mask(gp, n, k, g):
            s_cl.wait_apart(gp, n, g + 1)
            p = pr[g % 2]
            for part in (p[:, 0:HPG * N].rearrange("p (h i) -> p h i", i=N)[:, :, 0:P],
                         p[:, HPG * N:].rearrange("p (h i) -> p h i", i=P)):
                last = gp.affine_select(out=part, in_=part, compare_op=ALU.is_ge, fill=0.0, base=0,
                                        pattern=[[0, HPG], [1, P]], channel_multiplier=-1)
            s_mk.up(last)

        GP = ((0, gp_mask, 0), (0, gp_mask, 1), (0, gp_mask, 2), (2, gp_lo, 0), (0, gp_mask, 3), (2, gp_lo, 1))

        @block.gpsimd
        def _(gp):
            gp.memset(qp[:, :, :, 4 * DQ:], 0.0)
            gp.memset(kp[:, :, :, 4 * DQ:], 0.0)
            for k in range(2):
                gp.memset(ks[k][:, :, :], 0.0)
                gp.memset(va[k][:, :, :, DC + 1:], 0.0)
                last = gp.memset(va[k][:, :, :, DC:DC + 1], 1.0)
            s_z.up(last)
            pipeline(gp, GP, B)


def mlp(nc, c, ins):
    with ExitStack() as ctx:
        def sb(name, shape, dt=F32):
            return ctx.enter_context(nc.sbuf_tensor("d_" + name, shape, dt))

        def sig(name, per=1):
            return Signal(nc, ctx, "d_" + name, per)
        S2 = 2
        RUNS = B // S2
        T4, W = S2 * TT, S2 * N
        HT = HID // P
        wave = [[(i, o) for o in range(HT) for i in range(HT) if max(i, o) == w] for w in range(HT)]
        wave[-1].sort(key=lambda x: (x[1], x[0]))
        nat = {k: sb(k, [P, HT, D]) for k in ("w1", "w2")}
        nat |= {k: sb(k, [P, HT, HID]) for k in ("h1", "h2")}
        nat["w3"] = sb("w3", [P, HID])
        w1T, w2T, w3T = (sb(x, [P, HID], F16) for x in ("w1T", "w2T", "w3T"))
        h1T, h2T = (sb(x, [P, HT, HID], F16) for x in ("h1T", "h2T"))
        sc = {k: sb(k + "s", [P, HT]) for k in ("w1", "w2", "h1", "h2")}
        sc3 = sb("w3s", [D, 1])
        s12, s1h = sb("s12", [P, HT]), sb("s1h", [P, HT])
        gate = sb("gate", [D, B])
        xn, hf = sb("xn", [P, T4, D]), sb("hf", [D, W])
        hx = sb("hx", [D, 2, W], F16)
        th, gf, uf = sb("th", [P, W]), sb("gf", [P, W]), [sb(f"uf{k}", [P, W]) for k in range(2)]
        a1, a2, a3 = (sb(x, [P, HT, 2, W], F16) for x in ("a1", "a2", "a3"))
        ge = [sb(f"ge{k}", [P, W]) for k in range(3)]
        og = sb("og", [D, W])
        pH = [ctx.enter_context(nc.psum_tensor(f"d_pH{k}", [P, BANK], F32)) for k in range(HT)]
        pA, pB, pD, pX = (ctx.enter_context(nc.psum_tensor("d_p" + x, [P, BANK], F32)) for x in "ABDX")

        s_w = Signal(nc, ctx, "d_w", 16 * 10)
        steps = Steps(nc, ctx, "d_steps")
        turner = Turner(nc, ctx, c, "d", pH)
        for k, to in (("w1", w1T), ("w2", w2T)):
            turner.add(to[:, :], [nat[k][:, j, :] for j in range(HT)])
        for k, to in (("h1", h1T), ("h2", h2T)):
            for i in range(HT):
                turner.add(to[:, i, :], [nat[k][:, o, i * P:(i + 1) * P] for o in range(HT)])
        turner.add(w3T[:, :], [nat["w3"][:, i * P:(i + 1) * P] for i in range(HT)])
        s_c = sig("c")
        s_xn, s_xT, s_hf, s_hx = sig("xn"), sig("xT"), sig("hf"), sig("hx")
        s_in, s_th, s_gf, s_uf, s_uh, s_a1 = (sig(x, HT) for x in ("in", "th", "gf", "uf", "uh", "a1"))
        s_m2, s_m3, s_g2, s_g3, s_a2, s_a3 = (sig(x, HT) for x in ("m2", "m3", "g2", "g3", "a2", "a3"))
        s_h2, s_h3 = sig("h2", HT), sig("h3", HT)
        s_o, s_og, s_oT, s_st = sig("o"), sig("og"), sig("oT"), sig("st")
        block = ctx.enter_context(nc.Block())

        @block.sync
        def _(sp):
            for to, of in ((nat["w1"][:, :, :], ins["L1_ffn_w1_w"].rearrange("(j p) d -> p j d", p=P)),
                           (nat["w2"][:, :, :], ins["L1_ffn_w2_w"].rearrange("(j p) d -> p j d", p=P)),
                           (nat["h1"][:, :, :], ins["L1_ffn_h1_w"].rearrange("(j p) d -> p j d", p=P)),
                           (nat["h2"][:, :, :], ins["L1_ffn_h2_w"].rearrange("(j p) d -> p j d", p=P)),
                           (nat["w3"][:, :], ins["L1_ffn_w3_w"]),
                           (sc3[:, :], ins["L1_ffn_w3_s"].rearrange("(p a) -> p a", a=1))):
                s_w.up(sp.dma_start(to, of), 16)
            for k in sc:
                s_w.up(sp.dma_start(sc[k][:, :], ins[f"L1_ffn_{k}_s"].rearrange("(j p) -> p j", p=P),
                                   allow_slow_non_contiguous=True), 16)

        def pe_front(pe, n):
            s_xn.wait(pe, n)
            for t in range(T4):
                last = pe.transpose(pX[:, t * P:(t + 1) * P], xn[:, t, :], c.id32[:, :])
            s_xT.up(last)

        def pe_first(pe, n, j):
            if j == 0:
                s_hx.wait(pe, n)
            s_uf.wait(pe, n - 1 if j == 0 else n, HT if j == 0 else j)
            for out, w in ((pA, w1T), (pB, w2T)):
                for part in range(2):
                    last = pe.matmul(out[:, :], w[:, j * P:(j + 1) * P], hx[:, part, :], start=part == 0, stop=part == 1)
            s_in.up(last)

        def pe_hidden(pe, n, w, weights, a, have, read, k_of, done):
            for m, (i, o) in enumerate(wave[w]):
                if m == 0:
                    have.wait(pe, n, w + 1)
                    read(pe, n, w)
                for part in range(2):
                    last = pe.matmul(pH[o][:, :], weights[:, i, o * P:(o + 1) * P], a[:, i, part, :],
                                     start=k_of(i, o) and part == 0, stop=i == HT - 1 and part == 1)
                if i == HT - 1:
                    done.up(last)

        def pe_second(pe, n, w):
            pe_hidden(pe, n, w, h1T, a1, s_a1, lambda pe, n, w: s_g3.wait(pe, n - 1, w + 1), lambda i, o: i == 0, s_m2)

        def pe_third(pe, n, w):
            pe_hidden(pe, n, w, h2T, a2, s_a2, lambda pe, n, w: s_g2.wait(pe, n, w + 1), lambda i, o: i == 0, s_m3)

        def pe_out(pe, n):
            s_og.wait(pe, n - 1)
            for i in range(HT):
                s_a3.wait(pe, n, i + 1)
                for part in range(2):
                    last = pe.matmul(pD[:, :], w3T[:, i * P:(i + 1) * P], a3[:, i, part, :],
                                     start=i == 0 and part == 0, stop=i == HT - 1 and part == 1)
            s_o.up(last)

        def pe_back(pe, n, last_run=False):
            s_og.wait(pe, n)
            if last_run:
                s_st.wait(pe, n - 1, 1)
            else:
                s_hf.wait(pe, n + 2)
            for t in range(T4):
                last = pe.transpose(pX[:, t * P:(t + 1) * P], og[:, t * P:(t + 1) * P], c.id32[:, :])
            s_oT.up(last)

        def pe_run(pe, n, tail=True, front=True):
            pe_second(pe, n, 0)
            if front:
                if tail:
                    s_st.wait(pe, n - 2, 1)
                pe_front(pe, n + 1)
            pe_second(pe, n, 1)
            pe_second(pe, n, 2)
            if tail:
                pe_back(pe, n - 1, not front)
            pe_second(pe, n, 3)
            if front:
                pe_first(pe, n + 1, 0)
            for w in range(HT - 1):
                pe_third(pe, n, w)
            if front:
                pe_first(pe, n + 1, 1)
            pe_third(pe, n, HT - 1)
            if front:
                pe_first(pe, n + 1, 2)
            pe_out(pe, n)
            if front:
                pe_first(pe, n + 1, 3)

        @block.tensor
        def _(pe):
            s_w.wait(pe, 0)
            turner.tensor(pe)
            turner.wait(pe)
            pe_front(pe, 0)
            for j in range(HT):
                pe_first(pe, 0, j)
            pe_run(pe, 0, tail=False)
            pe_run(pe, 1)
            with pe.Fori(2, RUNS - 1) as n:
                pe_run(pe, n)
            pe_run(pe, RUNS - 1, front=False)
            pe_back(pe, RUNS - 1, True)

        def dve_front(dve, n):
            s_xT.wait(dve, n - 1)
            for t in range(T4):
                last = normalise(dve, c, xn[:, t, :], n * T4 + t)
            s_xn.up(last)

        def dve_modulate(dve, n):
            s_xT.wait(dve, n)
            for m in range(S2):
                last = dve.tensor_scalar(hf[:, m * N:(m + 1) * N], pX[:, m * N:(m + 1) * N],
                                         c.mod[:, 1, 4, bass.ds(n * S2 + m, 1)], c.mod[:, 1, 3, bass.ds(n * S2 + m, 1)],
                                         ALU.mult, ALU.add)
            s_hf.up(last)
            s_hf.wait(dve, n)
            s_in.wait(dve, n - 1)
            split(dve, n, hx[:, 0, :], hx[:, 1, :], hf[:, :], s_hh, 1, s_hx)

        s_hh = sig("hh")

        def split(dve, n, hi, lo, x, mid, k, done):
            mid.up(dve.tensor_copy(hi, x))
            mid.wait(dve, n, k)
            done.up(dve.tensor_tensor(lo, x, hi, ALU.subtract))

        def dve_gated(dve, n, j):
            s_th.wait(dve, n, j + 1)
            s_gf.up(dve.scalar_tensor_tensor(gf[:, :], th[:, :], 1.0, pA[:, :], ALU.add, ALU.mult))
            s_gf.wait(dve, n, j + 1)
            if j < 2:
                s_a1.wait(dve, n - 1, HT + j - 1)
            else:
                s_a1.wait(dve, n, j - 1)
            s_uf.up(dve.scalar_tensor_tensor(uf[j % 2][:, :], gf[:, :], s12[:, j:j + 1], pB[:, :], ALU.mult, ALU.mult))

        def dve_parts(dve, n, o, layer):
            ready, mid, done, a, reader = ((s_g2, s_h2, s_a2, a2, s_m3), (s_g3, s_h3, s_a3, a3, s_o))[layer]
            ready.wait(dve, n, o + 1)
            if o == 0:
                reader.wait(dve, n - 1)
            split(dve, n, a[:, o, 0, :], a[:, o, 1, :], ge[o % 3][:, :], mid, o + 1, done)

        def dve_gate(dve, n):
            s_o.wait(dve, n)
            s_oT.wait(dve, n - 1)
            for m in range(S2):
                last = dve.tensor_scalar(og[:, m * N:(m + 1) * N], pD[:, m * N:(m + 1) * N],
                                         gate[:, bass.ds(n * S2 + m, 1)], None, ALU.mult)
            s_og.up(last)

        def dve_add(dve, n):
            s_oT.wait(dve, n)
            xt = x_tiles(c, n * T4, T4)
            s_st.up(dve.tensor_tensor(xt, xt, pX[:, :].rearrange("p (t d) -> p t d", t=T4), ALU.add))

        def dve_run(dve, n, tail=True, front=True):
            if front:
                dve_front(dve, n + 1)
            if tail:
                dve_gate(dve, n - 1)
            if front:
                dve_modulate(dve, n + 1)
            if tail:
                dve_add(dve, n - 1)
            for o in range(HT):
                dve_parts(dve, n, o, 0)
            if front:
                dve_gated(dve, n + 1, 0)
                dve_gated(dve, n + 1, 1)
            for o in range(HT):
                dve_parts(dve, n, o, 1)
            if front:
                dve_gated(dve, n + 1, 2)
                dve_gated(dve, n + 1, 3)

        @block.vector
        def _(dve):
            step = steps.on(dve)
            turner.vector(dve)
            s_w.wait(dve, 0)
            step(dve.tensor_scalar(s1h[:, :], sc["w1"][:, :], 0.5, None, ALU.mult))
            step(dve.tensor_tensor(s12[:, :], s1h[:, :], sc["w2"][:, :], ALU.mult))
            s_c.up(dve.tensor_scalar(gate[:, :], c.mod[:, 1, 5, :], sc3[:, 0:1], None, ALU.mult))
            s_c.wait(dve, 0)
            dve_front(dve, 0)
            dve_modulate(dve, 0)
            for j in range(HT):
                dve_gated(dve, 0, j)
            dve_run(dve, 0, tail=False)
            dve_run(dve, 1)
            with dve.Fori(2, RUNS - 1) as n:
                dve_run(dve, n)
            dve_run(dve, RUNS - 1, front=False)
            dve_gate(dve, RUNS - 1)
            dve_add(dve, RUNS - 1)

        def act_tanh(act, n, j):
            s_in.wait(act, n, j + 1)
            s_gf.wait(act, n - 1 if j == 0 else n, HT if j == 0 else j)
            s_th.up(act.activation(th[:, :], pA[:, :], ACT.Tanh, scale=s1h[:, j:j + 1]))

        def act_hi(act, n, j):
            s_uf.wait(act, n, j + 1)
            if j == 0:
                s_m2.wait(act, n - 1)
            s_uh.up(act.activation(a1[:, j, 0, :], uf[j % 2][:, :], ACT.Copy))

        def act_gelu(act, n, o, layer):
            made, done, key = ((s_m2, s_g2, "h1"), (s_m3, s_g3, "h2"))[layer]
            made.wait(act, n, o + 1)
            u = o - 3
            if u >= 0:
                (s_a2, s_a3)[layer].wait(act, n, u + 1)
            elif layer:
                s_a2.wait(act, n)
            else:
                s_a3.wait(act, n - 1)
            done.up(act.activation(ge[o % 3][:, :], pH[o][:, :], ACT.Gelu, scale=sc[key][:, o:o + 1]))

        def act_run(act, n, tail=True, front=True):
            for o in range(HT):
                act_gelu(act, n, o, 0)
            if front:
                act_tanh(act, n + 1, 0)
                act_hi(act, n + 1, 0)
                act_tanh(act, n + 1, 1)
                act_hi(act, n + 1, 1)
            for o in range(HT):
                act_gelu(act, n, o, 1)
            if front:
                act_tanh(act, n + 1, 2)
                act_hi(act, n + 1, 2)
                act_tanh(act, n + 1, 3)
                act_hi(act, n + 1, 3)

        @block.scalar
        def _(act):
            act.preload_act_table(ACT.Gelu)
            s_c.wait(act, 0)
            for j in range(HT):
                act_tanh(act, 0, j)
                act_hi(act, 0, j)
            act_run(act, 0, tail=False)
            act_run(act, 1)
            with act.Fori(2, RUNS - 1) as n:
                act_run(act, n)
            act_run(act, RUNS - 1, front=False)

        def gp_lo(gp, n, j):
            s_uh.wait(gp, n, j + 1)
            s_a1.up(gp.tensor_tensor(a1[:, j, 1, :], uf[j % 2][:, :], a1[:, j, 0, :], ALU.subtract))

        def gp_run(gp, n):
            for j in range(HT):
                gp_lo(gp, n, j)

        @block.gpsimd
        def _(gp):
            gp_run(gp, 0)
            with gp.Fori(1, RUNS) as n:
                gp_run(gp, n)


def store(nc, c, out):
    with ExitStack() as ctx:
        s_out = Signal(nc, ctx, "out", 16)
        block = ctx.enter_context(nc.Block())

        @block.sync
        def _(sp):
            s_out.up(sp.dma_start(out.rearrange("b (t p) d -> p (b t) d", p=P), c.x[:, :, :]), 16)
            s_out.wait(sp, 0)


def build(nc, ins, out):
    with ExitStack() as ctx:
        c = Core(nc, ctx)
        setup(nc, c, ins)
        attention0(nc, c, ins)
        moe(nc, c, ins)
        attention1(nc, c, ins)
        mlp(nc, c, ins)
        store(nc, c, out)


def kernel(**inputs):
    import numpy as _np
    import concourse.bacc as _bacc
    from concourse.bass_utils import run_bass_kernel_spmd as _run

    nc = _bacc.Bacc("TRN2", target_bir_lowering=False, num_devices=1)
    arrays, ins = {}, {}
    for name, value in {**inputs, "rope": rope_tables()}.items():
        a = _np.ascontiguousarray(value)
        arrays[f"in_{name}_dram"] = a
        ins[name] = nc.dram_tensor(f"in_{name}_dram", a.shape, mybir.dt.from_np(a.dtype), kind="ExternalInput").ap()
    out = nc.dram_tensor("out_0_dram", (B, N, D), F32, kind="ExternalOutput").ap()
    build(nc, ins, out)
    r = _run(nc, [arrays], core_ids=[0])
    return r.results[0]["out_0_dram"]
```

```python
from contextlib import ExitStack

import numpy as np

import concourse.bass as bass
from concourse import mybir

F32 = mybir.dt.float32
F16 = mybir.dt.float16
I32 = mybir.dt.int32
ALU = mybir.AluOpType
ACT = mybir.ActivationFunctionType
AX = mybir.AxisListType

P = 128
B, N, D = 32, 256, 128
TT = N // P
TILES = B * TT
LN_EPS = 1e-5
QH, KH, DH = 16, 8, 64
G2 = QH // KH
HPG = 4
GROUPS = QH // HPG
QW, KW = QH * DH, KH * DH
VC = 96
RMS_EPS = float(np.finfo(np.float32).eps)
SOFTCLAMP = 50.0
E, EI, SI = 16, 64, 256
NG, EG = 4, 4
TOPG, TOPK, ROUTED = 2, 4, 2.5
H1, DC, DR, LAT = 16, 8, 4, 32
DQ = DC + DR
CLIP = 80.0
HID = 512
BANK = 512


class Signal:

    def __init__(self, nc, ctx, name, per=1, runs=None):
        self.sem, self.per, self.runs = ctx.enter_context(nc.semaphore(name)), per, runs

    def up(self, instruction, by=1):
        instruction.then_inc(self.sem, by)

    def wait(self, engine, n, k=None):
        value = n * self.per + (self.per if k is None else k)
        if isinstance(value, int) and self.runs:
            value = min(value, self.runs * self.per)
        if isinstance(value, int) and value <= 0:
            return
        engine.wait_ge(self.sem, value)

    def wait_apart(self, engine, n, k=None):
        self.wait(engine, n, k)
        engine.nop(nofuse=True)


class Chain:

    def __init__(self, nc, ctx, name, per, runs):
        self.raised = Signal(nc, ctx, name, per, runs)

    def take(self, engine, n, steps, lo, hi):
        assert len(steps) == self.raised.per
        for k in range(lo, hi):
            if k:
                self.raised.wait(engine, n, k)
            self.raised.up(steps[k]())


class Weights:

    def __init__(self, nc, ctx, name, **tensors):
        self.tensors = {key: ctx.enter_context(nc.sbuf_tensor(f"{name}_{key}", list(shape), F32))
                        for key, shape in tensors.items()}
        self.sem, self.loads = ctx.enter_context(nc.semaphore(name + "_loaded")), []
        self.halved, self.halves = ctx.enter_context(nc.semaphore(name + "_halved")), []

    def __getitem__(self, key):
        return self.tensors[key]

    def add(self, to, of, **how):
        self.loads.append((to, of, how))

    def load(self, sp):
        for to, of, how in self.loads:
            sp.dma_start(to, of, **how).then_inc(self.sem, 16)

    def wait(self, engine):
        engine.wait_ge(self.sem, 16 * len(self.loads))

    def add_half(self, to, of):
        self.halves.append((to, of))

    def halve(self, act):
        self.wait(act)
        for to, of in self.halves:
            act.activation(to, of, ACT.Copy).then_inc(self.halved, 1)

    def wait_halves(self, engine):
        engine.wait_ge(self.halved, len(self.halves))


FIRST, LAST = -2, 1


def pipeline(engine, plan, count, short=0):
    def run(n, k):
        for shift, stage, *which in plan:
            if not isinstance(n, int) or 0 <= n + shift < count:
                stage(engine, n + shift, (k + shift) % 2, *which)
    pairs = (count - 4) // 2 - short
    for n in range(FIRST, 2):
        run(n, n % 2)
    with engine.Fori(0, pairs) as i:
        for k in range(2):
            run(i * 2 + (2 + k), k)
    for n in range(2 * pairs + 2, count + LAST):
        run(n, n % 2)


class Steps:

    def __init__(self, nc, ctx, name):
        self.sem, self.k = ctx.enter_context(nc.semaphore(name)), 0

    def on(self, engine):
        def step(instruction):
            self.k += 1
            instruction.then_inc(self.sem, 1)
            engine.wait_ge(self.sem, self.k)
        return step


RSQRT_STEPS = 12


def rsqrt(dve, y, v, tmp, half):
    newton = [lambda: dve.tensor_tensor(tmp, y, y, ALU.mult),
              lambda: dve.tensor_tensor(tmp, tmp, half, ALU.mult),
              lambda: dve.scalar_tensor_tensor(y, tmp, 1.5, y, ALU.add, ALU.mult)]
    return [lambda: dve.tensor_scalar(tmp.bitcast(I32), v.bitcast(I32), 1, None, ALU.logical_shift_right),
            lambda: dve.tensor_scalar(y.bitcast(I32), tmp.bitcast(I32), -1.0, float(0x5F3759DF), ALU.mult, ALU.add),
            lambda: dve.tensor_scalar(half, v, -0.5, None, ALU.mult)] + 3 * newton


X_LOADS = 8


class Core:

    def __init__(self, nc, ctx):
        def sb(name, shape, dt=F32):
            return ctx.enter_context(nc.sbuf_tensor(name, shape, dt))
        self.x = sb("x", [P, TILES, D])
        self.s_x = [Signal(nc, ctx, f"x{k}", 16) for k in range(X_LOADS)]
        self.mv = sb("mv", [P, TILES, 2])
        self.rs = sb("rs", [P, TILES])
        self.var = sb("var", [P, TILES])
        self.tmp = sb("ln_tmp", [P, TILES])
        self.half = sb("ln_half", [P, TILES])
        self.stat = sb("stat", [P, TT * TT, 6])
        self.agg = sb("agg", [P, TT * TT, 2])
        self.mod = sb("mod", [P, 2, 6, B])
        self.id32 = sb("id32", [P, P])
        self.id16 = sb("id16", [P, P], F16)




def ln_scales(step, dve, c):
    step(dve.tensor_scalar(c.var[:, :], c.mv[:, :, 1], LN_EPS, None, ALU.add))
    for instruction in rsqrt(dve, c.rs[:, :], c.var[:, :], c.tmp[:, :], c.half[:, :]):
        step(instruction())


def normalise(dve, c, out, tile):
    return dve.tensor_scalar(out, c.x[:, bass.ds(tile, 1), :].rearrange("p a d -> p (a d)"),
                             c.mv[:, bass.ds(tile, 1), 0], c.rs[:, bass.ds(tile, 1)],
                             ALU.subtract, ALU.mult)


def x_tiles(c, tile, count):
    return c.x[:, bass.ds(tile, count), :]


ADD_STEPS = 4


def add_to_x(dve, c, s_st, n, tiles, out):
    xt = x_tiles(c, n * tiles, tiles)
    s_st.up(dve.tensor_tensor(xt, xt, out.rearrange("p (t d) -> p t d", t=tiles), ALU.add))


def measure(dve, c, s_st, n, tiles, step):
    if step == 1:
        s_st.wait_apart(dve, n, 1)
        for t in range(tiles):
            last = dve.bn_stats(c.stat[:, t, :], x_tiles(c, n * tiles + t, 1).rearrange("p a d -> p (a d)"))
    elif step == 2:
        s_st.wait_apart(dve, n, 2)
        for t in range(tiles):
            last = dve.bn_aggr(c.agg[:, t, :], c.stat[:, t, :])
    else:
        s_st.wait(dve, n, 3)
        last = dve.tensor_copy(c.mv[:, bass.ds(n * tiles, tiles), :], c.agg[:, 0:tiles, :])
    s_st.up(last)


def setup(nc, c, ins, ahead):
    with ExitStack() as ctx:
        def sb(name, shape, dt=F32):
            return ctx.enter_context(nc.sbuf_tensor(name, shape, dt))
        TC = TILES // X_LOADS
        cin = [sb(f"cin{l}", [B, D]) for l in range(2)]
        sg = [sb(f"sg{l}", [B, D]) for l in range(2)]
        wmod = [sb(f"wmod{l}", [D, 6 * D]) for l in range(2)]
        cT = sb("cT", [D, 2, B])
        sgn, mag = sb("sgn", [P, 2, 2, B]), sb("mag", [P, 2, 2, B])
        psc = ctx.enter_context(nc.psum_tensor("psc", [D, BANK], F32))
        psm = ctx.enter_context(nc.psum_tensor("psm", [D, 2, BANK], F32))
        s_c = [Signal(nc, ctx, f"su_c{l}", 32) for l in range(2)]
        s_id = Signal(nc, ctx, "su_id", 4)
        s_exp = Signal(nc, ctx, "su_exp", 2)
        s_silu = Signal(nc, ctx, "su_silu", 1)
        s_cT = Signal(nc, ctx, "su_cT", 1)
        s_cTs = Signal(nc, ctx, "su_cTs", 1)
        s_mod = Signal(nc, ctx, "su_mod", 1)
        steps = Steps(nc, ctx, "su_dve")
        x_dram = ins["L0_attn_tokens"].rearrange("b (t p) d -> p (b t) d", p=P)
        block = ctx.enter_context(nc.Block())

        @block.sync
        def _(sp):
            for l in range(2):
                s_c[l].up(sp.dma_start(cin[l][:, :], ins[f"L{l}_c"]), 16)
                s_c[l].up(sp.dma_start(wmod[l][:, :], ins[f"L{l}_wmod"]), 16)
            for k in range(X_LOADS):
                c.s_x[k].up(sp.dma_start(c.x[:, k * TC:(k + 1) * TC, :], x_dram[:, k * TC:(k + 1) * TC, :]), 16)
                if k < len(ahead):
                    ahead[k].load(sp)

        @block.gpsimd
        def _(gp):
            s_id.up(gp.memset(c.id32[:, :], 0.0))
            s_id.up(gp.memset(c.id16[:, :], 0.0))
            s_id.wait(gp, 0, 2)
            for m in (c.id32, c.id16):
                s_id.up(gp.affine_select(out=m[:, :], in_=m[:, :], compare_op=ALU.not_equal, fill=1.0,
                                         base=0, pattern=[[-1, P]], channel_multiplier=1))

        @block.scalar
        def _(act):
            for l in range(2):
                s_c[l].wait(act, 0)
                s_exp.up(act.activation(sg[l][:, :], cin[l][:, :], ACT.Exp, scale=-1.0))

        @block.tensor
        def _(pe):
            s_id.wait(pe, 0)
            s_silu.wait(pe, 0)
            for l in range(2):
                last = pe.transpose(psc[:, l * B:(l + 1) * B], sg[l][:, :], c.id32[0:B, 0:B])
            s_cT.up(last)
            s_cTs.wait(pe, 0)
            for l in range(2):
                s_c[l].wait(pe, 0)
                for j in range(6):
                    last = pe.matmul(psm[:, l, j * B:(j + 1) * B], wmod[l][:, j * D:(j + 1) * D],
                                     cT[:, l, :], start=True, stop=True)
            s_mod.up(last)

        @block.vector
        def _(dve):
            step = steps.on(dve)
            for l in range(2):
                s_exp.wait(dve, 0, l + 1)
                step(dve.tensor_scalar(sg[l][:, :], sg[l][:, :], 1.0, None, ALU.add))
                step(dve.reciprocal(sg[l][:, :], sg[l][:, :]))
                last = dve.tensor_tensor(sg[l][:, :], sg[l][:, :], cin[l][:, :], ALU.mult)
                if l == 0:
                    step(last)
            s_silu.up(last)
            s_cT.wait(dve, 0)
            s_cTs.up(dve.tensor_copy(cT[:, :, :].rearrange("p l b -> p (l b)"), psc[:, 0:2 * B]))
            s_mod.wait(dve, 0)
            got = psm[:, :, 0:6 * B].rearrange("p l (h j b) -> p l h j b", h=2, j=3)
            out = c.mod[:, :, :, :].rearrange("p l (h j) b -> p l h j b", h=2)
            dve.tensor_copy(out[:, :, :, 0, :], got[:, :, :, 0, :])
            dve.tensor_scalar(out[:, :, :, 1, :], got[:, :, :, 1, :], 1.0, None, ALU.add)
            dve.tensor_scalar(sgn[:, :, :, :], got[:, :, :, 2, :], 0.0, 2.0, ALU.is_ge, ALU.mult)
            step(dve.tensor_copy(mag[:, :, :, :], got[:, :, :, 2, :]))
            step(dve.scalar_tensor_tensor(mag[:, :, :, :], mag[:, :, :, :], -1.0, mag[:, :, :, :], ALU.mult, ALU.max))
            step(dve.tensor_scalar(mag[:, :, :, :], mag[:, :, :, :], 0.25, None, ALU.max))
            step(dve.scalar_tensor_tensor(out[:, :, :, 2, :], sgn[:, :, :, :], -1.0, mag[:, :, :, :], ALU.add, ALU.mult))


def attention0_weights(nc, ctx, ins):
    w = Weights(nc, ctx, "a", wq=(D, QW), wkv=(D, 2 * KW), wo=(P, KW // P, D), nw=(D, 1),
                gam=(P, QW + KW),
                gk=(P, KW))
    w.add(w["wq"][:, :], ins["L0_attn_Wq"])
    w.add(w["wkv"][:, :], ins["L0_attn_Wkv"])
    w.add(w["wo"][:, :, :], ins["L0_attn_Wout"].rearrange("(j p) n -> p j n", p=P))
    w.add(w["nw"][:, :], ins["L0_attn_norm_w"].rearrange("(p a) -> p a", a=1))
    w.add(w["gam"][:, 0:QW], ins["L0_attn_q_gamma"].rearrange("h d -> (h d)").partition_broadcast(P))
    w.add(w["gk"][:, :], ins["L0_attn_k_gamma"].rearrange("h d -> (h d)").partition_broadcast(P))
    return w


def attention0(nc, c, weights):
    with ExitStack() as ctx:
        def sb(name, shape, dt=F32):
            return ctx.enter_context(nc.sbuf_tensor(name, shape, dt))

        def sig(name, per=1):
            return Signal(nc, ctx, "a_" + name, per, B)
        wq, wkv, wo, nw, gam, gk = (
            weights["wq"], weights["wkv"], weights["wo"], weights["nw"], weights["gam"], weights["gk"])
        ones = sb("ones", [P, 1])
        xn, hsq = sb("xn", [P, TT, D]), sb("hsq", [D, N])
        hT = [sb(f"hT{k}", [D, N]) for k in range(2)]
        sq = sb("sq", [P, QW + KW])
        qg = sb("qg", [P, TT, QW + KW])
        heads = QH + KH
        MS = TT * heads
        LN = MS + TT
        ss, rr, rtmp, rhalf = (sb(x, [P, LN + TT]) for x in ("ss", "rr", "rtmp", "rhalf"))
        st, ag = sb("st", [P, 2 * TT, 6]), sb("ag", [P, 2 * TT, 2])
        rlim = sb("rlim", [P, TT])
        rv = sb("rv", [P, TT])
        qp = sb("qp", [P, TT, QH, 2 * DH], F16)
        kp = sb("kp", [P, TT, KH, 3 * DH], F16)
        qs = [sb(f"qs{k}", [P, QH, N], F16) for k in range(2)]
        k1 = [sb(f"k1{k}", [P, KH, N], F16) for k in range(2)]
        k2 = [sb(f"k2{k}", [P, KH, N], F16) for k in range(2)]
        va = [sb(f"va{k}", [P, TT, KH, VC]) for k in range(2)]
        SC = HPG * (N + P)
        th = sb("th", [P, SC])
        pr = [sb(f"pr{k}", [P, SC]) for k in range(2)]
        rl = sb("rl", [P, TT, HPG])
        on = [sb(f"on{k}", [P, TT, HPG, DH]) for k in range(2)]
        as_ = sb("as", [P, TT, KW])
        at = sb("at", [P, KW // P, N])
        og = sb("og", [D, N])
        pS = ctx.enter_context(nc.psum_tensor("a_pS", [P, 3 * BANK], F32))
        pO = ctx.enter_context(nc.psum_tensor("a_pO", [P, TT, BANK], F32))
        pW = ctx.enter_context(nc.psum_tensor("a_pW", [P, 3, BANK], F32))

        s_prep, s_gam = Signal(nc, ctx, "a_prep", 5), Signal(nc, ctx, "a_gam", 5)
        steps = Steps(nc, ctx, "a_steps")
        s_aT, s_at, s_o, s_og, s_oT, s_st = (
            sig(x, p) for x, p in (("aT", TT), ("at", TT), ("o", 1), ("og", 1), ("oT", 1), ("st", ADD_STEPS)))
        s_sc, s_th, s_pr, s_mk, s_pv, s_rl, s_on, s_as = (
            sig(x, GROUPS) for x in ("sc", "th", "pr", "mk", "pv", "rl", "on", "as"))
        BANKS = (1, 2, 0)
        s_xn, s_xT, s_hT, s_hsq, s_ms, s_msv = (sig(x) for x in ("xn", "xT", "hT", "hsq", "ms", "msv"))
        s_qk, s_sq, s_qg = (sig(x, TT * len(BANKS)) for x in ("qk", "sq", "qg"))
        s_ss, s_qn = sig("ss", TT), sig("qn", TT)
        s_hi, s_lo = sig("hi", 2 * TT), sig("lo", 2 * TT)
        s_tr, s_trv = sig("tr", 8), sig("trv", 4)
        s_trk = sig("trk", 4)
        s_v, s_va = sig("v", TT), sig("va", TT)
        SAMPLES_OF_LOAD = B // X_LOADS
        s_ln, s_rs = Signal(nc, ctx, "a_ln", 4, B - 2), Signal(nc, ctx, "a_lns", 1, B - 2)
        chain = Chain(nc, ctx, "a_rs", RSQRT_STEPS + 2 + TT, B)

        block = ctx.enter_context(nc.Block())

        def pe_transpose_x(pe, n, k):
            s_xn.wait(pe, n)
            s_qg.wait(pe, n - 1)
            for t in range(TT):
                last = pe.transpose(pW[:, 0, t * P:(t + 1) * P], xn[:, t, :], c.id32[:, :])
            s_xT.up(last)

        def pe_values(pe, n, k):
            s_qg.wait(pe, n)
            for t in range(TT):
                s_v.up(pe.matmul(pW[:, 1 + t, :], hT[k][:, t * P:(t + 1) * P], wkv[:, KW:2 * KW],
                                 start=True, stop=True))

        def pe_mean_square(pe, n, k):
            s_hsq.wait(pe, n)
            s_hT.wait(pe, n)
            for t in range(TT):
                last = pe.matmul(pW[:, 0, t:t + 1], hsq[:, t * P:(t + 1) * P], ones[:, :], start=True, stop=True)
            s_ms.up(last)

        def pe_out_transposes(pe, n, k):
            s_as.wait(pe, n)
            for t in range(TT):
                s_va.wait(pe, n + 2, t + 1)
                for j in range(KW // P):
                    last = pe.transpose(pW[:, 1 + t, j * P:(j + 1) * P], as_[:, t, j * P:(j + 1) * P], c.id32[:, :])
                s_aT.up(last)

        def pe_split_transpose(pe, n, k, m):
            t, u = m // 4, m % 4
            s_hi.wait(pe, n, 2 * t + 1 + u // 2)
            s_lo.wait(pe, n, 2 * t + 1 + u // 2)
            if m == 0:
                s_qg.wait(pe, n)
                s_msv.wait(pe, n + 1)
            elif m in (1, 2):
                s_va.wait(pe, n, m)
                s_at.wait(pe, n - 2, m)
            elif m == 3:
                s_trv.wait(pe, n, 1)
            elif m == 4:
                s_trk.wait(pe, n, 2)
            elif m == 5:
                s_trv.wait(pe, n, 2)
                s_og.wait(pe, n - 2)
            elif m == 6:
                s_trk.wait(pe, n, 1)
                if not isinstance(n, int) or n >= 2:
                    s_st.wait(pe, n - 2, 1)
            else:
                s_trv.wait(pe, n, 3)
            bank = pW[:, (0, 1, 2, 0)[u], :].bitcast(F16)
            for j in range(8):
                src = (qp[:, t, 8 * u + j, :] if u < 2 else
                       kp[:, t, j, (u - 2) * DH:(u - 2) * DH + 2 * DH])
                last = pe.transpose(bank[:, j * P:(j + 1) * P], src, c.id16[:, :])
            s_tr.up(last)

        def pe_out_project(pe, n, k):
            s_at.wait(pe, n)
            s_trv.wait(pe, n + 2, 2)
            for j in range(KW // P):
                last = pe.matmul(pW[:, 1, 0:N], wo[:, j, :], at[:, j, :], start=j == 0, stop=j == KW // P - 1)
            s_o.up(last)

        def pe_out_back(pe, n, k):
            s_og.wait(pe, n)
            s_trk.wait(pe, n + 2, 1)
            for t in range(TT):
                last = pe.transpose(pW[:, 2, t * P:(t + 1) * P], og[:, t * P:(t + 1) * P], c.id32[:, :])
            s_oT.up(last)

        def pe_project_qk(pe, n, k, m):
            t, j = m // len(BANKS), m % len(BANKS)
            b = BANKS[j]
            if m == 0:
                s_hT.wait(pe, n)
                s_msv.wait(pe, n)
                s_trv.wait(pe, n - 1, 4)
                s_trk.wait(pe, n - 1, 4)
            elif t:
                s_qg.wait(pe, n, m - len(BANKS) + 1)
            w = wkv[:, 0:KW] if b == 2 else wq[:, b * BANK:(b + 1) * BANK]
            s_qk.up(pe.matmul(pW[:, b, :], hT[k][:, t * P:(t + 1) * P], w, start=True, stop=True))

        def pe_scores(pe, n, k, g):
            if g == 0:
                s_trv.wait(pe, n)
                s_trk.wait(pe, n)
            s_th.wait(pe, n - 1 if g == 0 else n, GROUPS if g == 0 else g)
            for hh in range(0, HPG, G2):
                h = g * HPG + hh
                for out, keys in ((pS[:, hh * N:(hh + G2) * N], 0),
                                  (pS[:, HPG * N + hh * P:HPG * N + (hh + G2) * P], 1)):
                    for first, kk in ((True, k1[k]), (False, k2[k])):
                        last = pe.matmul(out, kk[:, h // G2, keys * P:(keys + 1) * P],
                                         qs[k][:, h:h + G2, keys * P:N], start=first, stop=not first)
            s_sc.up(last)

        def pe_weighted_values(pe, n, k, g):
            if g == 0:
                s_va.wait(pe, n)
            s_mk.wait(pe, n, g + 1)
            s_on.wait(pe, n - 1 if g == 0 else n, GROUPS if g == 0 else g)
            p = pr[g % 2]
            for hh in range(HPG):
                v = (g * HPG + hh) // G2
                for t in range(TT):
                    out = pO[:, t, hh * VC:(hh + 1) * VC]
                    pe.matmul(out, p[:, hh * N + t * P:hh * N + (t + 1) * P], va[k][:, 0, v, :],
                              start=True, stop=t == 0)
                last = pe.matmul(out, p[:, HPG * N + hh * P:HPG * N + (hh + 1) * P], va[k][:, 1, v, :],
                                 start=False, stop=True)
            s_pv.up(last)

        PE = ((1, pe_project_qk, 5), (-1, pe_weighted_values, 3), (0, pe_scores, 1), (1, pe_values),
              (0, pe_weighted_values, 0), (2, pe_transpose_x), (0, pe_scores, 2), (-1, pe_out_transposes),
              (0, pe_weighted_values, 1), (2, pe_mean_square), (0, pe_scores, 3), (1, pe_split_transpose, 0),
              (1, pe_split_transpose, 1), (1, pe_split_transpose, 2), (1, pe_split_transpose, 3),
              (-1, pe_out_project), (-1, pe_out_back), (1, pe_split_transpose, 4), (1, pe_split_transpose, 5),
              (1, pe_split_transpose, 6), (1, pe_split_transpose, 7), (0, pe_weighted_values, 2),
              (2, pe_project_qk, 0), (2, pe_project_qk, 1), (2, pe_project_qk, 2), (2, pe_project_qk, 3),
              (2, pe_project_qk, 4), (1, pe_scores, 0))

        @block.tensor
        def _(pe):
            s_prep.wait(pe, 0)
            pipeline(pe, PE, B)

        def dve_ln(dve, n, k, step):
            if isinstance(n, int) and n + 2 >= B:
                return
            tiles = bass.ds((n + 2) * TT, TT)
            if step == 0:
                if isinstance(n, int):
                    part = (n + 2) // SAMPLES_OF_LOAD
                    for loaded in c.s_x[part:] if n == 2 else c.s_x[part:part + 1]:
                        loaded.wait(dve, 0)
                s_ln.wait_apart(dve, n - 1, 2)
                for t in range(TT):
                    last = dve.bn_stats(st[:, t, :], x_tiles(c, (n + 2) * TT + t, 1).rearrange("p a d -> p (a d)"))
            elif step == 1:
                s_ln.wait(dve, n - 1)
                s_ln.wait_apart(dve, n, 1)
                for t in range(TT):
                    last = dve.bn_aggr(ag[:, t, :], st[:, t, :])
            elif step == 2:
                s_ln.wait(dve, n, 2)
                chain.raised.wait(dve, n - 1)
                last = dve.tensor_scalar(ss[:, LN:], ag[:, 0:TT, 1], LN_EPS, None, ALU.add)
            else:
                last = dve.tensor_copy(c.mv[:, tiles, :], ag[:, 0:TT, :])
            s_ln.up(last)

        def dve_ln_scale(dve, n, k):
            if isinstance(n, int) and n + 2 >= B:
                return
            chain.raised.wait(dve, n, RSQRT_STEPS)
            s_rs.up(dve.tensor_copy(c.rs[:, bass.ds((n + 2) * TT, TT)], rr[:, LN:]))

        def dve_normalise(dve, n, k):
            s_rs.wait(dve, n - 2)
            s_xT.wait(dve, n - 1)
            for t in range(TT):
                last = normalise(dve, c, xn[:, t, :], n * TT + t)
            s_xn.up(last)

        def dve_modulate(dve, n, k):
            s_xT.wait(dve, n)
            s_v.wait(dve, n - 2)
            s_hT.up(dve.tensor_scalar(hT[k][:, :], pW[:, 0, 0:N], c.mod[:, 0, 1, bass.ds(n, 1)],
                                      c.mod[:, 0, 0, bass.ds(n, 1)], ALU.mult, ALU.add))

        def dve_mean_square(dve, n, k):
            s_ms.wait(dve, n)
            chain.raised.wait(dve, n - 1)
            s_msv.up(dve.tensor_scalar(ss[:, MS:LN], pW[:, 0, 0:TT], RMS_EPS, None, ALU.add))

        def dve_gain(dve, n, k, m):
            if m == 0:
                if isinstance(n, int) and n == 0:
                    s_gam.wait(dve, 0)
                s_hi.wait(dve, n - 1)
                s_lo.wait(dve, n - 1)
            s_sq.wait(dve, n, m + 1)
            t, b = m // len(BANKS), BANKS[m % len(BANKS)]
            cols = slice(b * BANK, (b + 1) * BANK)
            s_qg.up(dve.tensor_tensor(qg[:, t, cols], pW[:, b, :], gam[:, cols], ALU.mult))

        def dve_sums(dve, n, k, t):
            s_sq.wait(dve, n, (t + 1) * len(BANKS))
            if t == 0:
                chain.raised.wait(dve, n - 1)
            s_ss.up(dve.tensor_reduce(ss[:, t * heads:(t + 1) * heads],
                                      sq[:, :].rearrange("p (h d) -> p h d", d=DH), AX.X, ALU.add))

        def factor_steps(dve):
            def limit(t):
                r = rr[:, t * heads:(t + 1) * heads]
                return dve.tensor_scalar(r, r, rlim[:, t:t + 1], None, ALU.min)
            return rsqrt(dve, rr[:, :], ss[:, :], rtmp[:, :], rhalf[:, :]) + [
                lambda: dve.tensor_copy(rv[:, :], rr[:, MS:LN]),
                lambda: dve.tensor_scalar(rlim[:, :], rr[:, MS:LN], 1e12, None, ALU.mult),
                lambda: limit(0), lambda: limit(1)]

        def dve_factors(dve, n, k, lo, hi):
            if lo == 0:
                s_ss.wait(dve, n)
                s_ln.wait(dve, n)
                s_rs.wait(dve, n - 1)
                s_msv.wait(dve, n)
                s_va.wait(dve, n - 1)
                s_qn.wait(dve, n - 1)
            chain.take(dve, n, factor_steps(dve), lo, hi)

        def dve_norm(dve, n, k, t):
            if t == 0:
                chain.raised.wait(dve, n)
                s_qg.wait(dve, n)
            r = rr[:, t * heads:(t + 1) * heads].unsqueeze(2).broadcast_to((P, heads, DH))
            q = qg[:, t, :].rearrange("p (h d) -> p h d", d=DH)
            s_qn.up(dve.tensor_tensor(q, q, r, ALU.mult))

        def dve_outputs(dve, n, k, g):
            s_pv.wait(dve, n, g + 1)
            s_as.wait(dve, n - 1 if g < 2 else n, GROUPS + g - 1 if g < 2 else g - 1)
            o = pO[:, :, 0:HPG * VC].rearrange("p t (h w) -> p t h w", w=VC)
            s_rl.up(dve.reciprocal(rl[:, :, :], o[:, :, :, DH]))
            s_rl.wait(dve, n, g + 1)
            for t in range(TT):
                last = dve.tensor_tensor(on[g % 2][:, t, :, :], o[:, t, :, 0:DH],
                                         rl[:, t, :].unsqueeze(2).broadcast_to((P, HPG, DH)), ALU.mult)
            s_on.up(last)

        def dve_take_q(dve, n, k, m):
            if m == 0:
                s_sc.wait(dve, n - 2)
            t, u = m // 4, m % 4
            s_tr.wait(dve, n, m + 1)
            s_trv.up(dve.tensor_copy(qs[k][:, 8 * u:8 * u + 8, t * P:(t + 1) * P],
                                     pW[:, u, :].bitcast(F16).rearrange("p (h i) -> p h i", i=P)))

        def dve_gate(dve, n, k):
            s_o.wait(dve, n)
            s_oT.wait(dve, n - 1)
            s_og.up(dve.tensor_scalar(og[:, :], pW[:, 1, 0:N], c.mod[:, 0, 2, bass.ds(n, 1)], None, ALU.mult))

        def dve_add(dve, n, k):
            s_oT.wait(dve, n)
            add_to_x(dve, c, s_st, n, TT, pW[:, 2, 0:N])

        def dve_measure(dve, n, k, step):
            measure(dve, c, s_st, n, TT, step)

        DVE = ((1, dve_gain, 5), (1, dve_factors, 0, 4), (1, dve_factors, 4, 8), (-1, dve_outputs, 3),
               (2, dve_normalise), (1, dve_factors, 8, 12), (1, dve_factors, 12, 16), (1, dve_norm, 0),
               (0, dve_outputs, 0), (2, dve_ln, 0), (2, dve_modulate), (2, dve_ln, 1), (1, dve_norm, 1),
               (1, dve_ln_scale), (0, dve_outputs, 1), (2, dve_mean_square), (1, dve_take_q, 0), (2, dve_ln, 2),
               (1, dve_take_q, 1), (-1, dve_gate), (-1, dve_add), (1, dve_take_q, 4), (-1, dve_measure, 1),
               (1, dve_take_q, 5), (0, dve_outputs, 2), (-1, dve_measure, 2), (2, dve_gain, 0), (2, dve_ln, 3),
               (2, dve_gain, 1), (-1, dve_measure, 3), (2, dve_gain, 2), (2, dve_sums, 0), (2, dve_gain, 3),
               (2, dve_gain, 4), (2, dve_sums, 1))

        @block.vector
        def _(dve):
            step = steps.on(dve)
            c.s_x[0].wait(dve, 0)
            first = slice(0, 2 * TT)
            for t in range(2 * TT):
                last = dve.bn_stats(st[:, t, :], c.x[:, t, :])
            step(last)
            for t in range(2 * TT):
                last = dve.bn_aggr(ag[:, t, :], st[:, t, :])
            step(last)
            step(dve.tensor_copy(c.mv[:, first, :], ag[:, :, :]))
            step(dve.tensor_scalar(c.var[:, first], ag[:, :, 1], LN_EPS, None, ALU.add))
            for instruction in rsqrt(dve, *(x[:, first] for x in (c.rs, c.var, c.tmp, c.half))):
                step(instruction())
            pipeline(dve, DVE, B, short=1)
            s_st.wait(dve, B - 1)
            ln_scales(step, dve, c)

        def act_square_qk(act, n, k, m):
            t, j = m // len(BANKS), m % len(BANKS)
            s_qk.wait(act, n, m + 1)
            if j == 0:
                s_ss.wait(act, n - 1 if t == 0 else n, TT if t == 0 else t)
            b = BANKS[j]
            s_sq.up(act.activation(sq[:, b * BANK:(b + 1) * BANK], pW[:, b, :], ACT.Square))

        def act_hi(act, n, k, t, u):
            s_qn.wait(act, n, t + 1)
            s_tr.wait(act, n - 1, 4 * t + 2 * u + 2)
            if u == 0:
                last = act.activation(qp[:, t, :, 0:DH], qg[:, t, 0:QW].rearrange("p (h d) -> p h d", d=DH), ACT.Copy)
            else:
                x = qg[:, t, QW:].rearrange("p (h d) -> p h d", d=DH)
                act.activation(kp[:, t, :, 0:DH], x, ACT.Copy)
                last = act.activation(kp[:, t, :, 2 * DH:3 * DH], x, ACT.Copy)
            s_hi.up(last)

        def act_softmax(act, n, k, g):
            s_sc.wait(act, n, g + 1)
            s_pr.wait(act, n - 1 if g == 0 else n, GROUPS if g == 0 else g)
            s_th.up(act.activation(th[:, :], pS[:, :], ACT.Tanh, scale=1.0 / SOFTCLAMP))
            s_th.wait(act, n, g + 1)
            s_pv.wait(act, n - 1 if g < 2 else n, GROUPS + g - 1 if g < 2 else g - 1)
            s_pr.up(act.activation(pr[g % 2][:, :], th[:, :], ACT.Exp, scale=SOFTCLAMP * DH ** -0.5))

        def act_take_heads(act, n, k):
            s_o.wait(act, n - 1)
            for t in range(TT):
                s_aT.wait(act, n, t + 1)
                s_at.up(act.activation(at[:, :, t * P:(t + 1) * P],
                                       pW[:, 1 + t, :].rearrange("p (j i) -> p j i", i=P), ACT.Copy))

        def act_take_k(act, n, k, m):
            if m == 2:
                s_sc.wait(act, n - 2)
            t, u = m // 4, m % 4 - 2
            s_tr.wait(act, n, m + 1)
            s_trk.up(act.activation((k1, k2)[u][k][:, :, t * P:(t + 1) * P],
                                    pW[:, 2 - 2 * u, :].bitcast(F16).rearrange("p (h i) -> p h i", i=P), ACT.Copy))

        def act_take_values(act, n, k):
            s_pv.wait(act, n - 2)
            chain.raised.wait(act, n, RSQRT_STEPS + 1)
            for t in range(TT):
                s_v.wait(act, n, t + 1)
                s_va.up(act.activation(va[k][:, t, :, 0:DH], pW[:, 1 + t, :].rearrange("p (h d) -> p h d", d=DH),
                                       ACT.Copy, scale=rv[:, t:t + 1]))

        ACTS = ((1, act_square_qk, 0), (1, act_square_qk, 1), (1, act_square_qk, 2), (1, act_square_qk, 3),
                (1, act_square_qk, 4), (1, act_square_qk, 5), (0, act_softmax, 0), (0, act_softmax, 1),
                (1, act_take_values), (1, act_hi, 0, 0), (1, act_hi, 0, 1), (0, act_softmax, 2),
                (-1, act_take_heads), (1, act_hi, 1, 0), (1, act_hi, 1, 1), (1, act_take_k, 2),
                (1, act_take_k, 3), (0, act_softmax, 3), (1, act_take_k, 6), (1, act_take_k, 7))

        @block.scalar
        def _(act):
            weights.wait(act)
            for w in (wq, wkv):
                s_prep.up(act.activation(w[:, :], w[:, :], ACT.Copy, scale=nw[:, 0:1]))
            pipeline(act, ACTS, B)

        def gp_square_h(gp, n, k):
            s_hT.wait(gp, n)
            s_ms.wait(gp, n - 1)
            s_hsq.up(gp.tensor_tensor(hsq[:, :], hT[k][:, :], hT[k][:, :], ALU.mult))

        def gp_lo(gp, n, k, t, u):
            s_hi.wait(gp, n, 2 * t + 1 + u)
            to, x = ((qp, qg[:, t, 0:QW]), (kp, qg[:, t, QW:]))[u]
            s_lo.up(gp.tensor_tensor(to[:, t, :, DH:2 * DH], x.rearrange("p (h d) -> p h d", d=DH),
                                     to[:, t, :, 0:DH], ALU.subtract))

        def gp_mask(gp, n, k, g):
            s_pr.wait_apart(gp, n, g + 1)
            p = pr[g % 2]
            for part in (p[:, 0:HPG * N].rearrange("p (h i) -> p h i", i=N)[:, :, 0:P],
                         p[:, HPG * N:].rearrange("p (h i) -> p h i", i=P)):
                last = gp.affine_select(out=part, in_=part, compare_op=ALU.is_ge, fill=0.0, base=0,
                                        pattern=[[0, HPG], [1, P]], channel_multiplier=-1)
            s_mk.up(last)

        def gp_sum(gp, n, k, g):
            s_on.wait(gp, n, g + 1)
            if g == 0:
                s_aT.wait(gp, n - 1)
            o = on[g % 2][:, :, :, :].rearrange("p t (h g) d -> p t h g d", g=G2)
            w = HPG // G2 * DH
            for t in range(TT):
                last = gp.tensor_tensor(as_[:, t, g * w:(g + 1) * w].rearrange("p (h d) -> p h d", d=DH),
                                        o[:, t, :, 0, :], o[:, t, :, 1, :], ALU.add)
            s_as.up(last)

        GP = ((-1, gp_sum, 2), (-1, gp_sum, 3), (2, gp_square_h), (1, gp_lo, 0, 0), (1, gp_lo, 0, 1),
              (0, gp_mask, 2), (1, gp_lo, 1, 0), (1, gp_lo, 1, 1), (0, gp_sum, 0), (0, gp_sum, 1),
              (0, gp_mask, 3), (1, gp_mask, 0), (1, gp_mask, 1))

        @block.gpsimd
        def _(gp):
            s_prep.up(gp.memset(ones[:, :], 1.0 / D))
            for v in va:
                s_prep.up(gp.memset(v[:, :, :, DH:VC], 1.0))
            weights.wait(gp)
            s_gam.up(gp.tensor_scalar(gam[:, 0:QW], gam[:, 0:QW], 1.0, float(DH) ** 0.5, ALU.add, ALU.mult))
            s_gam.up(gp.tensor_scalar(gk[:, :], gk[:, :], 1.0, None, ALU.add))
            s_gam.up(gp.memset(gam[:, QW:], float(DH) ** 0.5))
            s_gam.wait(gp, 0, 3)
            gq = gam[:, 0:QW].rearrange("p (h g d) -> p h g d", g=G2, d=DH)
            for g in range(G2):
                s_gam.up(gp.tensor_tensor(gq[:, :, g, :], gq[:, :, g, :],
                                          gk[:, :].rearrange("p (h d) -> p h d", d=DH), ALU.mult))
            pipeline(gp, GP, B)


class Turner:

    def __init__(self, nc, ctx, c, name, banks, dt=F32):
        self.identity = c.id16 if dt == F16 else c.id32
        self.banks, self.groups = [b[:, :].bitcast(dt) if dt == F16 else b[:, :] for b in banks], []
        self.turned = Signal(nc, ctx, name + "_turned", 1)
        self.taken = Signal(nc, ctx, name + "_taken", 1)

    def add(self, out, blocks):
        self.groups.append((out, blocks))

    def tensor(self, pe):
        nb = len(self.banks)
        for m, (_, blocks) in enumerate(self.groups):
            self.taken.wait(pe, m - nb)
            at = 0
            for b in blocks:
                rows, cols = b.shape
                last = pe.transpose(self.banks[m % nb][0:cols, at:at + rows], b, self.identity[0:rows, 0:rows])
                at += rows
            self.turned.up(last)

    def vector(self, dve):
        for m, (out, blocks) in enumerate(self.groups):
            self.turned.wait(dve, m)
            rows, cols = sum(b.shape[0] for b in blocks), blocks[0].shape[1]
            self.taken.up(dve.tensor_copy(out, self.banks[m % len(self.banks)][0:cols, 0:rows]))

    def wait(self, engine):
        self.taken.wait(engine, len(self.groups) - 1)


def moe_weights(nc, ctx, ins):
    RT, ST = E * EI // P, SI // P
    w = Weights(nc, ctx, "b", un=(P, RT + ST, D), dn=(D, (RT + ST) * P), gn=(E, D), bias=(P, E))
    w.add(w["un"][:, 0:RT, :], ins["L0_ffn_up_w"].rearrange("e i d -> (e i) d").rearrange("(t p) d -> p t d", p=P))
    w.add(w["un"][:, RT:, :], ins["L0_ffn_shared_up"].rearrange("(t p) d -> p t d", p=P))
    w.add(w["dn"][:, 0:RT * P].rearrange("p (e i) -> p e i", i=EI), ins["L0_ffn_down_w"].rearrange("e d i -> d e i"))
    w.add(w["dn"][:, RT * P:], ins["L0_ffn_shared_down"])
    w.add(w["gn"][:, :], ins["L0_ffn_gate_w"])
    w.add(w["bias"][:, :], ins["L0_ffn_bias_e"].partition_broadcast(P))
    return w


def moe(nc, c, weights, ahead):
    with ExitStack() as ctx:
        def sb(name, shape, dt=F32):
            return ctx.enter_context(nc.sbuf_tensor("b_" + name, shape, dt))

        def sig(name, per=1):
            return Signal(nc, ctx, "b_" + name, per, B // 2)
        S2 = 2
        RUNS = B // S2
        T4, W = S2 * TT, S2 * N
        RT, ST = E * EI // P, SI // P
        IT = RT + ST
        un, dn, gn, bias = weights["un"], weights["dn"], weights["gn"], weights["bias"]
        uT, dT, gT = sb("uT", [D, IT * P]), sb("dT", [P, IT * D]), sb("gT", [D, E])
        sel = sb("sel", [2 * E, RT, P], F16)
        lt4, lt16 = sb("lt4", [P, NG, NG]), sb("lt16", [P, E, E], F16)
        xn = sb("xn", [P, T4, D])
        hT = [sb(f"hT{k}", [D, W]) for k in range(2)]
        s, sc, mk, cw, rank = (sb(x, [P, T4, E]) for x in ("s", "sc", "mk", "cw", "rank"))
        pm, qm = sb("pm", [P, T4 * NG, 2]), sb("qm", [P, T4 * NG, 2])
        m1, m2, m3, gs, gr = (sb(x, [P, T4 * NG]) for x in ("m1", "m2", "m3", "gs", "gr"))
        gt4, eq4 = sb("gt4", [P, T4, NG, NG]), sb("eq4", [P, T4, NG, NG])
        gt16, eq16 = sb("gt16", [P, T4, E, E], F16), sb("eq16", [P, T4, E, E], F16)
        tot = sb("tot", [P, T4])
        cwp = sb("cwp", [P, T4, 2 * E], F16)
        cwT = [sb(f"cwT{k}", [2 * E, W], F16) for k in range(2)]
        r, rc, a = ([sb(f"{x}{k}", [P, W]) for k in range(4)] for x in ("r", "rc", "a"))
        og = sb("og", [D, W])
        pX, pR, pD, pB = (ctx.enter_context(nc.psum_tensor("b_p" + x, [P, BANK], F32)) for x in "XRDB")
        pU = [ctx.enter_context(nc.psum_tensor(f"b_pU{k}", [P, BANK], F32)) for k in range(2)]
        pC = [ctx.enter_context(nc.psum_tensor(f"b_pC{k}", [P, BANK], F32)) for k in range(2)]

        s_k, s_km = Signal(nc, ctx, "b_k", 5), Signal(nc, ctx, "b_km")
        steps = Steps(nc, ctx, "b_steps")
        turner = Turner(nc, ctx, c, "b", [pU[0], pU[1], pC[0], pC[1]])
        s_xn, s_xT, s_hT, s_lg, s_ex, s_cT, s_cw = (
            sig(x, p) for x, p in (("xn", 1), ("xT", 1), ("hT", 1), ("lg", 1), ("ex", 1), ("cT", 1), ("cw", 1)))
        s_up, s_r, s_dn, s_a = (sig(x, IT) for x in ("up", "r", "dn", "a"))
        s_cb, s_rc = sig("cb", RT), sig("rc", RT)
        s_og, s_oT, s_st = sig("og"), sig("oT"), sig("st", ADD_STEPS)
        for lo in range(0, IT, 4):
            hi = min(lo + 4, IT)
            turner.add(uT[:, lo * P:hi * P], [un[:, t, :] for t in range(lo, hi)])
        for lo in range(0, IT, 4):
            hi = min(lo + 4, IT)
            turner.add(dT[:, lo * D:hi * D], [dn[:, t * P:(t + 1) * P] for t in range(lo, hi)])
        turner.add(gT[:, :], [gn[:, :]])

        block = ctx.enter_context(nc.Block())

        @block.sync
        def _(sp):
            for w in ahead:
                w.load(sp)

        chain = Chain(nc, ctx, "b_rt", 29, RUNS)

        def slot(t, k):
            return (IT * k + t) % 4

        def tile_wait(engine, signal, count):
            if not isinstance(count, int) or count >= 0:
                engine.wait_ge(signal.sem, count + 1)

        def pe_front(pe, n, k):
            s_xn.wait(pe, n)
            s_hT.wait(pe, n - 1)
            for t in range(T4):
                last = pe.transpose(pX[:, t * P:(t + 1) * P], xn[:, t, :], c.id32[:, :])
            s_xT.up(last)

        def pe_route(pe, n, k):
            s_hT.wait(pe, n)
            s_cw.wait(pe, n - 1)
            for t in range(T4):
                last = pe.matmul(pR[:, t * E:(t + 1) * E], hT[k][:, t * P:(t + 1) * P], gT[:, :], start=True, stop=True)
            s_lg.up(last)

        def pe_turn_weights(pe, n, k):
            chain.raised.wait(pe, n)
            out = pR[0:2 * E, BANK // 2:BANK].bitcast(F16)
            for t in range(T4):
                last = pe.transpose(out[:, t * P:(t + 1) * P], cwp[:, t, :], c.id16[:, :])
            s_cT.up(last)

        def pe_up(pe, n, k, t):
            if t == 0:
                s_hT.wait(pe, n)
            tile_wait(pe, s_r, n * IT + t - 2)
            s_up.up(pe.matmul(pU[t % 2][:, :], uT[:, t * P:(t + 1) * P], hT[k][:, :], start=True, stop=True))

        def pe_spread(pe, n, k, t):
            if t == 0:
                s_cw.wait(pe, n)
            tile_wait(pe, s_rc, n * RT + t - 2)
            s_cb.up(pe.matmul(pC[t % 2][:, :], sel[:, t, :], cwT[k][:, :], start=True, stop=True))

        def pe_down(pe, n, k, t):
            s_a.wait(pe, n, t + 1)
            if t == 0:
                s_og.wait(pe, n - 1)
            s_dn.up(pe.matmul(pD[:, :], dT[:, t * D:(t + 1) * D], a[slot(t, k)][:, :], start=t == 0, stop=t == IT - 1))

        def pe_back(pe, n, k):
            s_og.wait(pe, n)
            if not isinstance(n, int) or n >= 1:
                s_st.wait(pe, n - 1, 1)
            for t in range(T4):
                last = pe.transpose(pB[:, t * P:(t + 1) * P], og[:, t * P:(t + 1) * P], c.id32[:, :])
            s_oT.up(last)

        PE = ((1, pe_front), (0, pe_up, 1), (0, pe_spread, 0), (0, pe_spread, 1), (1, pe_route), (0, pe_up, 2),
              (-1, pe_down, 8), (-1, pe_down, 9), (0, pe_spread, 2), (0, pe_up, 3), (0, pe_spread, 3),
              (-1, pe_back), (0, pe_down, 0), (0, pe_up, 4), (0, pe_down, 1), (0, pe_up, 5), (0, pe_spread, 4),
              (0, pe_spread, 5), (0, pe_up, 6), (0, pe_up, 7), (0, pe_down, 2), (0, pe_spread, 6),
              (0, pe_up, 8), (0, pe_spread, 7), (0, pe_down, 3), (0, pe_down, 4), (0, pe_down, 5),
              (0, pe_up, 9), (0, pe_down, 6), (0, pe_down, 7), (1, pe_turn_weights), (1, pe_up, 0))

        @block.tensor
        def _(pe):
            weights.wait(pe)
            turner.tensor(pe)
            turner.wait(pe)
            s_k.wait(pe, 0)
            s_km.wait(pe, 0)
            pipeline(pe, PE, RUNS)

        def dve_normalise(dve, n, k):
            s_xT.wait(dve, n - 1)
            for t in range(T4):
                last = normalise(dve, c, xn[:, t, :], n * T4 + t)
            s_xn.up(last)

        def routing(dve, n):
            tt, ts, stt = dve.tensor_tensor, dve.tensor_scalar, dve.scalar_tensor_tensor

            def rows(x):
                return x[:, :, :].rearrange("p t (g e) -> p (t g) e", e=EG)
            pairs = rows(sc).rearrange("p a (x y) -> p a x y", y=2)
            g3 = gs[:, :].rearrange("p (t g) -> p t g", g=NG)
            s4, s16 = (P, T4, NG, NG), (P, T4, E, E)
            a4, b4 = g3.unsqueeze(2).broadcast_to(s4), g3.unsqueeze(3).broadcast_to(s4)
            a16, b16 = mk[:, :, :].unsqueeze(2).broadcast_to(s16), mk[:, :, :].unsqueeze(3).broadcast_to(s16)
            return [
                lambda: (s_ex.wait(dve, n), ts(s[:, :, :], s[:, :, :], 1.0, None, ALU.add))[1],
                lambda: dve.reciprocal(s[:, :, :], s[:, :, :]),
                lambda: tt(sc[:, :, :], s[:, :, :], bias[:, :].unsqueeze(1).broadcast_to((P, T4, E)), ALU.add),
                lambda: tt(pm[:, :, :], pairs[:, :, :, 0], pairs[:, :, :, 1], ALU.max),
                lambda: tt(qm[:, :, :], pairs[:, :, :, 0], pairs[:, :, :, 1], ALU.min),
                lambda: tt(m1[:, :], pm[:, :, 0], pm[:, :, 1], ALU.max),
                lambda: tt(m2[:, :], pm[:, :, 0], pm[:, :, 1], ALU.min),
                lambda: tt(m3[:, :], qm[:, :, 0], qm[:, :, 1], ALU.max),
                lambda: tt(m2[:, :], m2[:, :], m3[:, :], ALU.max),
                lambda: tt(gs[:, :], m1[:, :], m2[:, :], ALU.add),
                lambda: tt(gt4[:, :, :, :], a4, b4, ALU.is_gt),
                lambda: tt(eq4[:, :, :, :], a4, b4, ALU.is_equal),
                lambda: tt(eq4[:, :, :, :], eq4[:, :, :, :], lt4[:, :, :].unsqueeze(1).broadcast_to(s4), ALU.mult),
                lambda: tt(gt4[:, :, :, :], gt4[:, :, :, :], eq4[:, :, :, :], ALU.add),
                lambda: dve.tensor_reduce(gr[:, :], gt4[:, :, :, :].rearrange("p t a b -> p (t a) b"), AX.X, ALU.add),
                lambda: ts(gr[:, :], gr[:, :], float(TOPG), None, ALU.is_lt),
                lambda: tt(rows(mk), rows(sc), gr[:, :].unsqueeze(2).broadcast_to((P, T4 * NG, EG)), ALU.mult),
                lambda: tt(gt16[:, :, :, :], a16, b16, ALU.is_gt),
                lambda: tt(eq16[:, :, :, :], a16, b16, ALU.is_equal),
                lambda: tt(eq16[:, :, :, :], eq16[:, :, :, :], lt16[:, :, :].unsqueeze(1).broadcast_to(s16), ALU.mult),
                lambda: tt(gt16[:, :, :, :], gt16[:, :, :, :], eq16[:, :, :, :], ALU.add),
                lambda: dve.tensor_reduce(rank[:, :, :], gt16[:, :, :, :], AX.X, ALU.add),
                lambda: stt(cw[:, :, :], rank[:, :, :], float(TOPK), s[:, :, :], ALU.is_lt, ALU.mult),
                lambda: dve.tensor_reduce(tot[:, :], cw[:, :, :], AX.X, ALU.add),
                lambda: ts(tot[:, :], tot[:, :], 1e-20, None, ALU.add),
                lambda: dve.reciprocal(tot[:, :], tot[:, :]),
                lambda: stt(cw[:, :, :], cw[:, :, :], ROUTED, tot[:, :].unsqueeze(2).broadcast_to((P, T4, E)),
                            ALU.mult, ALU.mult),
                lambda: (s_cT.wait(dve, n - 1), dve.tensor_copy(cwp[:, :, 0:E], cw[:, :, :]))[1],
                lambda: tt(cwp[:, :, E:2 * E], cw[:, :, :], cwp[:, :, 0:E], ALU.subtract),
            ]

        def dve_routing(dve, n, k, lo, hi):
            if lo == 0:
                chain.raised.wait(dve, n - 1)
            chain.take(dve, n, routing(dve, n), lo, hi)

        def dve_weigh(dve, n, k, t):
            s_r.wait(dve, n, t + 1)
            s_cb.wait(dve, n, t + 1)
            tile_wait(dve, s_a, n * IT + t - 4)
            i = slot(t, k)
            s_rc.up(dve.tensor_tensor(rc[i][:, :], r[i][:, :], pC[t % 2][:, :], ALU.mult))

        def dve_add(dve, n, k):
            s_oT.wait(dve, n)
            add_to_x(dve, c, s_st, n, T4, pB[:, :])

        def dve_measure(dve, n, k, step):
            measure(dve, c, s_st, n, T4, step)

        DVE = ((1, dve_routing, 0, 2), (1, dve_routing, 2, 6), (1, dve_routing, 6, 11), (0, dve_weigh, 2),
               (1, dve_routing, 11, 15), (-1, dve_add), (0, dve_weigh, 3), (1, dve_routing, 15, 18),
               (-1, dve_measure, 1), (0, dve_weigh, 4), (0, dve_weigh, 5), (-1, dve_measure, 2),
               (1, dve_routing, 18, 20), (0, dve_weigh, 6), (-1, dve_measure, 3), (0, dve_weigh, 7),
               (1, dve_routing, 20, 22), (1, dve_routing, 22, 25), (1, dve_routing, 25, 29), (2, dve_normalise),
               (1, dve_weigh, 0), (1, dve_weigh, 1))

        @block.vector
        def _(dve):
            turner.vector(dve)
            weights.wait(dve)
            s_km.wait(dve, 0)
            pipeline(dve, DVE, RUNS)
            s_st.wait(dve, RUNS - 1)
            ln_scales(steps.on(dve), dve, c)

        def act_modulate(act, n, k):
            s_up.wait(act, n - 2)
            s_xT.wait_apart(act, n)
            for m in range(S2):
                last = act.activation(hT[k][:, m * N:(m + 1) * N], pX[:, m * N:(m + 1) * N], ACT.Identity,
                                      scale=c.mod[:, 0, 4, bass.ds(n * S2 + m, 1)],
                                      bias=c.mod[:, 0, 3, bass.ds(n * S2 + m, 1)])
            s_hT.up(last)

        def act_exp(act, n, k):
            s_lg.wait(act, n)
            chain.raised.wait(act, n - 1, 23)
            s_ex.up(act.activation(s[:, :, :].rearrange("p t e -> p (t e)"), pR[:, 0:T4 * E], ACT.Exp, scale=-1.0))

        def act_relu(act, n, k, t):
            s_up.wait(act, n, t + 1)
            tile_wait(act, s_a, n * IT + t - 4)
            s_r.up(act.activation(r[slot(t, k)][:, :], pU[t % 2][:, :], ACT.Relu))

        def act_take_weights(act, n, k):
            s_cT.wait(act, n)
            s_cb.wait(act, n - 2)
            s_cw.up(act.activation(cwT[k][:, :], pR[0:2 * E, BANK // 2:BANK].bitcast(F16), ACT.Copy))

        def act_gate(act, n, k):
            s_oT.wait(act, n - 1)
            s_dn.wait_apart(act, n)
            for m in range(S2):
                last = act.activation(og[:, m * N:(m + 1) * N], pD[:, m * N:(m + 1) * N], ACT.Copy,
                                      scale=c.mod[:, 0, 5, bass.ds(n * S2 + m, 1)])
            s_og.up(last)

        ACTS = ((-1, act_relu, 7), (-1, act_relu, 8), (-1, act_relu, 9), (0, act_take_weights),
                (0, act_relu, 0), (1, act_modulate), (0, act_relu, 1), (1, act_exp), (0, act_relu, 2),
                (-1, act_gate), (0, act_relu, 3), (0, act_relu, 4), (0, act_relu, 5), (0, act_relu, 6))

        @block.scalar
        def _(act):
            pipeline(act, ACTS, RUNS)

        def gp_square(gp, n, k, t):
            if t < RT:
                s_rc.wait(gp, n, t + 1)
            else:
                s_r.wait(gp, n, t + 1)
            tile_wait(gp, s_dn, n * IT + t - 4)
            i = slot(t, k)
            other = rc[i] if t < RT else r[i]
            s_a.up(gp.tensor_tensor(a[i][:, :], r[i][:, :], other[:, :], ALU.mult))

        GP = ((-1, gp_square, 1), (-1, gp_square, 2), (-1, gp_square, 3), (-1, gp_square, 4),
              (-1, gp_square, 5), (-1, gp_square, 6), (-1, gp_square, 7), (-1, gp_square, 8),
              (-1, gp_square, 9), (0, gp_square, 0))

        @block.gpsimd
        def _(gp):
            s_k.up(gp.memset(sel[:, :, :], 0.0))
            s_k.up(gp.memset(lt4[:, :, :], 1.0))
            s_k.up(gp.memset(lt16[:, :, :], 1.0))
            for k in range(2):
                s_k.wait(gp, 0, 3 + k)
                m = sel[:, :, :].rearrange("r t (x i) -> r t x i", i=EI)
                s_k.up(gp.affine_select(out=m, in_=m, compare_op=ALU.not_equal, fill=1.0, base=k * E,
                                        pattern=[[2, RT], [1, 2], [0, EI]], channel_multiplier=-1))
            for m, w in ((lt4, NG), (lt16, E)):
                last = gp.affine_select(out=m[:, :, :], in_=m[:, :, :], compare_op=ALU.is_gt, fill=0.0, base=0,
                                        pattern=[[1, w], [-1, w]], channel_multiplier=0)
            s_km.up(last)
            pipeline(gp, GP, RUNS)


def rope_tables():
    inverse = np.float32(10000.0) ** (-np.arange(0, DR, 2, dtype=np.float32) / np.float32(DR))
    angle = np.arange(N, dtype=np.float32)[:, None] * inverse
    both = [f(angle).astype(np.float32).reshape(TT, P, DR // 2).transpose(1, 0, 2) for f in (np.cos, np.sin)]
    return np.ascontiguousarray(np.stack(both, axis=1))


def attention1_weights(nc, ctx, ins):
    HD = H1 * DC
    w = Weights(nc, ctx, "c", dq=(D, LAT), dkv=(D, LAT), up=(LAT, 3 * HD + H1 * DR), kr=(D, DR), wo=(HD, D),
                tab=(P, 2, TT, DR // 2))
    w.add(w["dq"][:, :], ins["L1_attn_W_DQ"])
    w.add(w["dkv"][:, :], ins["L1_attn_W_DKV"])
    for j, key in enumerate(("W_UQ", "W_UK", "W_UV")):
        w.add(w["up"][:, j * HD:(j + 1) * HD], ins["L1_attn_" + key])
    w.add(w["up"][:, 3 * HD:], ins["L1_attn_W_QR"])
    w.add(w["kr"][:, :], ins["L1_attn_W_KR"])
    w.add(w["wo"][:, :], ins["L1_attn_W_O"])
    w.add(w["tab"][:, :, :, :], ins["rope"])
    return w


def attention1(nc, c, weights, ahead):
    with ExitStack() as ctx:
        def sb(name, shape, dt=F32):
            return ctx.enter_context(nc.sbuf_tensor("c_" + name, shape, dt))

        def sig(name, per=1):
            return Signal(nc, ctx, "c_" + name, per, B)
        HD = H1 * DC
        QA = (H1 + 1) * DQ
        KA, VA_ = QA, QA + HD
        COLS = VA_ + HD
        SW = 64
        VW = 32
        SC = HPG * (N + P)
        groups = H1 // HPG
        lim = float(CLIP / np.sqrt(np.float32(DQ)))
        most, least = float(np.float32(np.exp(lim))), float(np.float32(np.exp(-lim)))
        dq_, dkv, kr, wo, tab = weights["dq"], weights["dkv"], weights["kr"], weights["wo"], weights["tab"]
        up = weights["up"]
        dT = sb("dT", [LAT, 2, D])
        wa = sb("wa", [D, COLS])
        xn, hT = sb("xn", [P, TT, D]), sb("hT", [D, N])
        rt = [sb(f"rt{k}", [P, TT, H1 + 1, DR // 2]) for k in range(4)]
        qf, kf = sb("qf", [P, TT, H1 + 1, DQ]), sb("kf", [P, TT, H1, DQ])
        qp, kp = sb("qp", [P, TT, H1, SW], F16), sb("kp", [P, TT, H1, SW], F16)
        qs = [sb(f"qs{k}", [P, H1 // 2, N], F16) for k in range(2)]
        ks = [sb(f"ks{k}", [P, H1, N], F16) for k in range(2)]
        vs = sb("vs", [P, TT, HD])
        va = [sb(f"va{k}", [P, TT, H1, VW]) for k in range(2)]
        pr = [sb(f"pr{g}", [P, SC]) for g in range(groups)]
        vu = sb("vu", [P, groups, N])
        rl = sb("rl", [P, TT, H1])
        an, at, og = sb("an", [P, TT, H1, DC]), sb("at", [HD, N]), sb("og", [D, N])
        pS = ctx.enter_context(nc.psum_tensor("c_pS", [P, 3 * BANK], F32))
        pV = [ctx.enter_context(nc.psum_tensor(f"c_pV{k}", [P, BANK], F32)) for k in range(2)]
        pW = ctx.enter_context(nc.psum_tensor("c_pW", [P, 3, BANK], F32))

        s_wm, s_wr, s_z = (Signal(nc, ctx, "c_" + x) for x in ("wm", "wr", "z"))
        steps = Steps(nc, ctx, "c_steps")
        turner = Turner(nc, ctx, c, "c", [pV[0], pV[1]])
        turner.add(dT[:, 0, :], [dq_[:, :]])
        turner.add(dT[:, 1, :], [dkv[:, :]])
        s_sc, s_ex, s_cl, s_mk, s_pv, s_vu = (sig(x, groups) for x in ("sc", "ex", "cl", "mk", "pv", "vu"))
        s_xn, s_xT, s_hT = sig("xn"), sig("xT"), sig("hT")
        s_pj, s_f, s_rd = sig("pj"), sig("f"), sig("rd")
        s_va, s_rope = sig("va"), sig("rope", 2)
        s_hi, s_lo = sig("hi", TT), sig("lo", TT)
        s_tr, s_ev, s_evk = sig("tr", 2 * TT), sig("ev", 3), sig("evk")
        s_aT, s_nm, s_bT, s_at, s_o, s_og, s_oT, s_st = (
            sig(x, p) for x, p in (("aT", TT), ("nm", TT), ("bT", 1), ("at", 1), ("o", 1), ("og", 1), ("oT", 1), ("st", ADD_STEPS)))
        s_rl = sig("rl", TT)
        block = ctx.enter_context(nc.Block())

        def pe_front(pe, n, k):
            s_xn.wait(pe, n)
            s_ev.wait(pe, n - 1)
            for t in range(TT):
                last = pe.transpose(pW[:, 0, t * P:(t + 1) * P], xn[:, t, :], c.id32[:, :])
            s_xT.up(last)

        def pe_project(pe, n, k):
            s_hT.wait(pe, n)
            s_evk.wait(pe, n - 1)
            s_nm.wait(pe, n - 3, 1)
            for t in range(TT):
                last = pe.matmul(pW[:, t, 0:COLS], hT[:, t * P:(t + 1) * P], wa[:, :], start=True, stop=True)
            s_pj.up(last)

        def pe_stack(pe, n, k, m):
            t, u = m // 2, m % 2
            s_hi.wait(pe, n, t + 1)
            s_lo.wait(pe, n, t + 1)
            if t == 0:
                s_rd.wait(pe, n)
            else:
                s_ev.wait(pe, n, u + 1)
            bank, src = pW[:, u, :].bitcast(F16), (qp, kp)[u]
            for j in range(H1 // 2):
                last = pe.transpose(bank[:, j * P:(j + 1) * P],
                                    src[:, t, 2 * j:2 * j + 2, :].rearrange("p h w -> p (h w)"), c.id16[:, :])
            s_tr.up(last)

        def pe_scores(pe, n, k, g):
            if g == 0:
                s_ev.wait(pe, n)
                s_evk.wait(pe, n)
            s_ex.wait(pe, n - 1 if g == 0 else n, groups if g == 0 else g)
            for hh in range(HPG):
                h = g * HPG + hh
                pe.matmul(pS[:, hh * N:(hh + 1) * N], ks[k][:, h, 0:P], qs[k][:, h // 2, :], start=True, stop=True)
                last = pe.matmul(pS[:, HPG * N + hh * P:HPG * N + (hh + 1) * P], ks[k][:, h, P:N], qs[k][:, h // 2, P:N],
                                 start=True, stop=True)
            s_sc.up(last)

        def pe_weighted_values(pe, n, k, g):
            if g == 0:
                s_va.wait(pe, n)
            s_mk.wait(pe, n, g + 1)
            s_vu.wait(pe, n - 1 if g < 2 else n, groups + g - 1 if g < 2 else g - 1)
            for keys in range(TT):
                for hh in range(HPG):
                    rows = slice(hh * VW, (hh + 1) * VW)
                    rhs = (pr[g][:, hh * N:(hh + 1) * N] if keys == 0 else
                           pr[g][:, HPG * N + hh * P:HPG * N + (hh + 1) * P])
                    last = pe.matmul(pV[g % 2][rows, keys * P:N], va[k][:, keys, g * HPG + hh, :], rhs,
                                     start=keys == 0, stop=keys == TT - 1, skip_group_check=True)
            s_pv.up(last)

        def pe_heads_back(pe, n, k):
            s_vu.wait(pe, n)
            s_evk.wait(pe, n + 2)
            if not isinstance(n, int) or n >= 1:
                s_st.wait(pe, n - 1, 1)
            for t in range(TT):
                for g in range(groups):
                    last = pe.transpose(pW[:, 1 + t, g * P:(g + 1) * P], vu[:, g, t * P:(t + 1) * P], c.id32[:, :])
                s_aT.up(last)

        def pe_heads_turned(pe, n, k):
            s_nm.wait(pe, n)
            for t in range(TT):
                last = pe.transpose(pW[:, 2, t * P:(t + 1) * P], an[:, t, :, :].rearrange("p h d -> p (h d)"), c.id32[:, :])
            s_bT.up(last)

        def pe_out_project(pe, n, k):
            s_at.wait(pe, n)
            s_o.up(pe.matmul(pW[:, 2, 0:N], wo[:, :], at[:, :], start=True, stop=True))

        def pe_out_back(pe, n, k):
            s_og.wait(pe, n)
            for t in range(TT):
                last = pe.transpose(pW[:, 2, t * P:(t + 1) * P], og[:, t * P:(t + 1) * P], c.id32[:, :])
            s_oT.up(last)

        PE = ((-1, pe_weighted_values, 1), (-1, pe_weighted_values, 2), (1, pe_stack, 0), (1, pe_stack, 1),
              (-1, pe_weighted_values, 3), (0, pe_scores, 1), (1, pe_stack, 2), (1, pe_stack, 3),
              (0, pe_weighted_values, 0), (2, pe_front), (0, pe_scores, 2), (-1, pe_heads_back),
              (2, pe_project), (-1, pe_heads_turned), (0, pe_scores, 3), (-1, pe_out_project),
              (1, pe_scores, 0), (-1, pe_out_back))

        @block.tensor
        def _(pe):
            weights.wait(pe)
            turner.tensor(pe)
            turner.wait(pe)
            for j, (a, u) in enumerate(((0, 0), (1, 1), (1, 2), (0, 3))):
                w = HD if j < 3 else H1 * DR
                last = pe.matmul(pW[:, 0, j * HD:j * HD + w], dT[:, a, :], up[:, u * HD:u * HD + w], start=True, stop=True)
            s_wm.up(last)
            s_wr.wait(pe, 0)
            s_z.wait(pe, 0)
            pipeline(pe, PE, B)

        def dve_front(dve, n, k):
            s_xT.wait(dve, n - 1)
            for t in range(TT):
                last = normalise(dve, c, xn[:, t, :], n * TT + t)
            s_xn.up(last)

        def dve_modulate(dve, n, k):
            s_xT.wait(dve, n)
            s_pj.wait(dve, n - 1)
            s_hT.up(dve.tensor_scalar(hT[:, :], pW[:, 0, 0:N], c.mod[:, 1, 1, bass.ds(n, 1)],
                                      c.mod[:, 1, 0, bass.ds(n, 1)], ALU.mult, ALU.add))

        def dve_rope(dve, n, k, step):
            q = pW[:, 0:TT, 0:QA].rearrange("p t (h d) -> p t h d", d=DQ)
            if step == 0:
                s_pj.wait(dve, n)
                x1, x2 = q[:, :, :, DC::2], q[:, :, :, DC + 1::2]
                cos, sin = (tab[:, j, :, :].unsqueeze(2).broadcast_to((P, TT, H1 + 1, DR // 2)) for j in range(2))
                s_rope.wait(dve, n - 1)
                for to, x, by in ((rt[0], x1, cos), (rt[1], x2, sin), (rt[2], x1, sin), (rt[3], x2, cos)):
                    last = dve.tensor_tensor(to[:, :, :, :], x, by, ALU.mult)
            elif step == 1:
                s_rope.wait(dve, n, 1)
                s_f.wait(dve, n - 1)
                s_hi.wait(dve, n - 1)
                s_lo.wait(dve, n - 1)
                for t in range(TT):
                    dve.tensor_copy(qf[:, t, 0:H1, 0:DC], q[:, t, 0:H1, 0:DC])
                    dve.tensor_copy(kf[:, t, :, 0:DC], pW[:, t, KA:KA + HD].rearrange("p (h d) -> p h d", d=DC))
                dve.tensor_tensor(qf[:, :, :, DC::2], rt[0][:, :, :, :], rt[1][:, :, :, :], ALU.subtract)
                last = dve.tensor_tensor(qf[:, :, :, DC + 1::2], rt[2][:, :, :, :], rt[3][:, :, :, :], ALU.add)
            else:
                s_rope.wait(dve, n, 2)
                for t in range(TT):
                    last = dve.tensor_copy(kf[:, t, :, DC:DQ], qf[:, t, H1, DC:DQ].unsqueeze(1).broadcast_to((P, H1, DR)))
            (s_f if step == 2 else s_rope).up(last)

        def dve_stage_values(dve, n, k):
            s_f.wait(dve, n)
            s_va.wait(dve, n - 1)
            s_rd.up(dve.tensor_copy(vs[:, :, :], pW[:, 0:TT, VA_:VA_ + HD]))

        def take_k(engine_copy, n, k, t):
            i = slice(t * P, (t + 1) * P)
            x = pW[:, 1, :].bitcast(F16).rearrange("p (h i) -> p h i", i=P)
            engine_copy(ks[k][0:SW, 0::2, i], x[0:SW, :, :])
            return engine_copy(ks[k][SW:P, 1::2, i], x[SW:P, :, :])

        def dve_stack(dve, n, k, m):
            if m == 0:
                s_sc.wait(dve, n - 2)
            s_tr.wait(dve, n, m + 1)
            if m == 1:
                s_ev.up(take_k(dve.tensor_copy, n, k, 0))
            else:
                i = slice(m // 2 * P, (m // 2 + 1) * P)
                s_ev.up(dve.tensor_copy(qs[k][:, :, i], pW[:, 0, :].bitcast(F16).rearrange("p (h i) -> p h i", i=P)))

        def dve_clip(dve, n, k, g):
            s_ex.wait(dve, n, g + 1)
            p = pr[g][:, :]
            s_cl.up(dve.tensor_scalar(p, p, most, least, ALU.min, ALU.max))

        def dve_sums(dve, n, k, t):
            s_aT.wait(dve, n, t + 1)
            s_nm.wait(dve, n - 1)
            heads = pW[:, 1 + t, :].rearrange("p (h w) -> p h w", w=VW)
            s_rl.up(dve.reciprocal(rl[:, t, :], heads[:, :, DC]))

        def dve_normalise(dve, n, k, t):
            s_rl.wait(dve, n, t + 1)
            s_bT.wait(dve, n - 1)
            heads = pW[:, 1 + t, :].rearrange("p (h w) -> p h w", w=VW)
            s_nm.up(dve.tensor_tensor(an[:, t, :, :], heads[:, :, 0:DC],
                                      rl[:, t, :].unsqueeze(2).broadcast_to((P, H1, DC)), ALU.mult))

        def dve_add(dve, n, k):
            s_oT.wait(dve, n)
            add_to_x(dve, c, s_st, n, TT, pW[:, 2, 0:N])

        def dve_measure(dve, n, k, step):
            measure(dve, c, s_st, n, TT, step)

        DVE = ((0, dve_clip, 0), (1, dve_stack, 0), (1, dve_stack, 1), (2, dve_front), (1, dve_stack, 2),
               (2, dve_modulate), (-1, dve_sums, 0), (-1, dve_normalise, 0), (-1, dve_sums, 1),
               (-1, dve_normalise, 1), (0, dve_clip, 1), (0, dve_clip, 2), (2, dve_rope, 0), (2, dve_rope, 1),
               (2, dve_rope, 2), (0, dve_clip, 3), (-1, dve_add), (2, dve_stage_values), (-1, dve_measure, 1),
               (-1, dve_measure, 2), (-1, dve_measure, 3))

        @block.vector
        def _(dve):
            turner.vector(dve)
            step = steps.on(dve)
            step(dve.memset(wa[:, :], 0.0))
            s_wm.wait(dve, 0)
            q = wa[:, 0:QA].rearrange("p (h d) -> p h d", d=DQ)
            dve.tensor_copy(q[:, 0:H1, 0:DC], pW[:, 0, 0:HD].rearrange("p (h d) -> p h d", d=DC))
            dve.tensor_copy(q[:, 0:H1, DC:DQ], pW[:, 0, 3 * HD:3 * HD + H1 * DR].rearrange("p (h d) -> p h d", d=DR))
            dve.tensor_copy(q[:, H1, DC:DQ], kr[:, :])
            step(dve.tensor_copy(wa[:, KA:COLS], pW[:, 0, HD:3 * HD]))
            s_wr.up(dve.memset(qf[:, :, H1, 0:DC], 0.0))
            s_z.wait(dve, 0)
            pipeline(dve, DVE, B)
            s_st.wait(dve, B - 1)
            ln_scales(step, dve, c)

        def parts(x, t, first, gap):
            return x[:, t, :, 0:4 * DQ].rearrange("p h (k d) -> p h k d", d=DQ)[:, :, first:first + gap + 1:gap, :]

        def twice(x, t):
            return x[:, t, 0:H1, :].unsqueeze(2).broadcast_to((P, H1, 2, DQ))

        def act_hi(act, n, k, t):
            s_f.wait(act, n)
            s_tr.wait(act, n - 1)
            act.activation(parts(qp, t, 0, 1), twice(qf, t), ACT.Copy)
            s_hi.up(act.activation(parts(kp, t, 0, 2), twice(kf, t), ACT.Copy))

        def act_exp(act, n, k, g):
            s_sc.wait(act, n, g + 1)
            s_pv.wait(act, n - 1, g + 1)
            s_ex.up(act.activation(pr[g][:, :], pS[:, :], ACT.Exp, scale=float(1.0 / np.sqrt(np.float32(DQ)))))

        def act_take_values(act, n, k, g):
            s_pv.wait(act, n, g + 1)
            if g == 0:
                s_aT.wait(act, n - 1)
            s_vu.up(act.activation(vu[:, g, :], pV[g % 2][:, 0:N], ACT.Copy))

        def act_take_heads(act, n, k):
            s_bT.wait(act, n)
            s_o.wait(act, n - 1)
            s_at.up(act.activation(at[:, :], pW[:, 2, 0:N], ACT.Copy))

        def act_place_values(act, n, k):
            s_rd.wait(act, n)
            s_pv.wait(act, n - 2)
            s_va.up(act.activation(va[k][:, :, :, 0:DC].rearrange("p t h d -> p (t h) d"),
                                   vs[:, :, :].rearrange("p t (h d) -> p (t h) d", d=DC), ACT.Copy))

        def act_stack(act, n, k):
            s_sc.wait(act, n - 2)
            s_tr.wait(act, n)
            s_evk.up(take_k(lambda out, x: act.activation(out, x, ACT.Copy), n, k, 1))

        def act_gate(act, n, k):
            s_oT.wait(act, n - 1)
            s_o.wait_apart(act, n)
            s_og.up(act.activation(og[:, :], pW[:, 2, 0:N], ACT.Copy, scale=c.mod[:, 1, 2, bass.ds(n, 1)]))

        ACTS = ((0, act_exp, 0), (-1, act_take_values, 1), (-1, act_take_values, 2), (1, act_hi, 1),
                (-1, act_take_values, 3), (1, act_place_values), (0, act_exp, 1), (1, act_stack),
                (0, act_exp, 2), (-1, act_take_heads), (0, act_take_values, 0), (0, act_exp, 3), (-1, act_gate),
                (2, act_hi, 0))

        @block.scalar
        def _(act):
            for w in ahead:
                w.halve(act)
            s_z.wait(act, 0)
            pipeline(act, ACTS, B)

        def gp_lo(gp, n, k, t):
            s_hi.wait(gp, n, t + 1)
            gp.tensor_tensor(parts(qp, t, 2, 1), twice(qf, t), parts(qp, t, 0, 1), ALU.subtract)
            s_lo.up(gp.tensor_tensor(parts(kp, t, 1, 2), twice(kf, t), parts(kp, t, 0, 2), ALU.subtract))

        def gp_mask(gp, n, k, g):
            s_cl.wait_apart(gp, n, g + 1)
            p = pr[g]
            for part in (p[:, 0:HPG * N].rearrange("p (h i) -> p h i", i=N)[:, :, 0:P],
                         p[:, HPG * N:].rearrange("p (h i) -> p h i", i=P)):
                last = gp.affine_select(out=part, in_=part, compare_op=ALU.is_ge, fill=0.0, base=0,
                                        pattern=[[0, HPG], [1, P]], channel_multiplier=-1)
            s_mk.up(last)

        GP = ((0, gp_mask, 1), (0, gp_mask, 2), (2, gp_lo, 0), (0, gp_mask, 3), (2, gp_lo, 1), (1, gp_mask, 0))

        @block.gpsimd
        def _(gp):
            gp.memset(qp[:, :, :, 4 * DQ:], 0.0)
            gp.memset(kp[:, :, :, 4 * DQ:], 0.0)
            for k in range(2):
                gp.memset(ks[k][:, :, :], 0.0)
                gp.memset(va[k][:, :, :, DC + 1:], 0.0)
                last = gp.memset(va[k][:, :, :, DC:DC + 1], 1.0)
            s_z.up(last)
            pipeline(gp, GP, B)


def mlp_weights(nc, ctx, ins):
    HT = HID // P
    w = Weights(nc, ctx, "d", w1=(P, HT, D), w2=(P, HT, D), h1=(P, HT, HID), h2=(P, HT, HID), w3=(P, HID),
                w1s=(P, HT), w2s=(P, HT), h1s=(P, HT), h2s=(P, HT), w3s=(D, 1))
    for key in ("w1", "w2", "h1", "h2"):
        to, scale = w[key], w[key + "s"]
        w.add(to[:, :, :], ins[f"L1_ffn_{key}_w"].rearrange("(j p) d -> p j d", p=P))
        w.add(scale[:, :], ins[f"L1_ffn_{key}_s"].rearrange("(j p) -> p j", p=P), allow_slow_non_contiguous=True)
    w.add(w["w3"][:, :], ins["L1_ffn_w3_w"])
    for key in ("w1", "w2", "h1", "h2", "w3"):
        of = w[key]
        to = w.tensors[key + "16"] = ctx.enter_context(nc.sbuf_tensor(f"d_{key}16", list(of.shape), F16))
        w.add_half(*(x[:, :] if key == "w3" else x[:, :, :] for x in (to, of)))
    w.add(w["w3s"][:, :], ins["L1_ffn_w3_s"].rearrange("(p a) -> p a", a=1))
    return w


def mlp(nc, c, weights, out):
    with ExitStack() as ctx:
        def sb(name, shape, dt=F32):
            return ctx.enter_context(nc.sbuf_tensor("d_" + name, shape, dt))

        def sig(name, per=1):
            return Signal(nc, ctx, "d_" + name, per, B // 2)
        S2 = 2
        RUNS = B // S2
        T4, W = S2 * TT, S2 * N
        HT = HID // P
        wave = [[(i, o) for o in range(HT) for i in range(HT) if max(i, o) == w] for w in range(HT)]
        wave[-1].sort(key=lambda x: (x[1], x[0]))
        nat = {key: weights[key + "16"] for key in ("w1", "w2", "h1", "h2", "w3")}
        w1T, w2T, w3T = (sb(x, [P, HID], F16) for x in ("w1T", "w2T", "w3T"))
        h1T, h2T = (sb(x, [P, HT, HID], F16) for x in ("h1T", "h2T"))
        sc = {"w1": weights["w1s"], "w2": weights["w2s"], "h1": weights["h1s"], "h2": weights["h2s"]}
        sc3 = weights["w3s"]
        s12, s1h = sb("s12", [P, HT]), sb("s1h", [P, HT])
        gate = sb("gate", [D, B])
        xn, hf = sb("xn", [P, T4, D]), sb("hf", [D, W])
        hx = sb("hx", [D, 2, W], F16)
        th, gf, uf = sb("th", [P, W]), sb("gf", [P, W]), [sb(f"uf{k}", [P, W]) for k in range(2)]
        a1, a2, a3 = (sb(x, [P, HT, 2, W], F16) for x in ("a1", "a2", "a3"))
        ge = [sb(f"ge{k}", [P, W]) for k in range(3)]
        og = sb("og", [D, W])
        pH = [ctx.enter_context(nc.psum_tensor(f"d_pH{k}", [P, BANK], F32)) for k in range(HT)]
        pA, pB, pD, pX = (ctx.enter_context(nc.psum_tensor("d_p" + x, [P, BANK], F32)) for x in "ABDX")

        steps = Steps(nc, ctx, "d_steps")
        turner = Turner(nc, ctx, c, "d", pH, F16)
        for k, to in (("w1", w1T), ("w2", w2T)):
            turner.add(to[:, :], [nat[k][:, j, :] for j in range(HT)])
        for k, to in (("h1", h1T), ("h2", h2T)):
            for i in range(HT):
                turner.add(to[:, i, :], [nat[k][:, o, i * P:(i + 1) * P] for o in range(HT)])
        turner.add(w3T[:, :], [nat["w3"][:, i * P:(i + 1) * P] for i in range(HT)])
        s_c = Signal(nc, ctx, "d_c")
        s_xn, s_xT, s_hf, s_hx = sig("xn"), sig("xT"), sig("hf"), sig("hx")
        s_in, s_th, s_gf, s_uf, s_uh, s_a1 = (sig(x, HT) for x in ("in", "th", "gf", "uf", "uh", "a1"))
        s_m2, s_m3, s_g2, s_g3, s_a2, s_a3 = (sig(x, HT) for x in ("m2", "m3", "g2", "g3", "a2", "a3"))
        s_h2, s_h3 = sig("h2", HT), sig("h3", HT)
        s_hh = sig("hh")
        s_o, s_og, s_oT, s_st = sig("o"), sig("og"), sig("oT"), sig("st")
        s_out = sig("out", 16)
        block = ctx.enter_context(nc.Block())

        out_dram = out.rearrange("b (t p) d -> p (b t) d", p=P)

        def sp_store(sp, n, k):
            s_st.wait(sp, n)
            s_out.up(sp.dma_start(out_dram[:, bass.ds(n * T4, T4), :], x_tiles(c, n * T4, T4)), 16)

        @block.sync
        def _(sp):
            pipeline(sp, ((0, sp_store),), RUNS)
            s_out.wait(sp, RUNS - 1)

        def pe_front(pe, n, k):
            s_xn.wait(pe, n)
            if not isinstance(n, int) or n >= 3:
                s_st.wait(pe, n - 3)
            for t in range(T4):
                last = pe.transpose(pX[:, t * P:(t + 1) * P], xn[:, t, :], c.id32[:, :])
            s_xT.up(last)

        def pe_first(pe, n, k, j):
            if j == 0:
                s_hx.wait(pe, n)
            s_uf.wait(pe, n - 1 if j == 0 else n, HT if j == 0 else j)
            for out, w in ((pA, w1T), (pB, w2T)):
                for part in range(2):
                    last = pe.matmul(out[:, :], w[:, j * P:(j + 1) * P], hx[:, part, :], start=part == 0, stop=part == 1)
            s_in.up(last)

        def pe_hidden(pe, n, k, layer, w):
            weights, a, have, done = ((h1T, a1, s_a1, s_m2), (h2T, a2, s_a2, s_m3))[layer]
            for m, (i, o) in enumerate(wave[w]):
                if m == 0:
                    have.wait(pe, n, w + 1)
                    if layer:
                        s_g2.wait(pe, n, w + 1)
                    else:
                        s_g3.wait(pe, n - 1, w + 1)
                for part in range(2):
                    last = pe.matmul(pH[o][:, :], weights[:, i, o * P:(o + 1) * P], a[:, i, part, :],
                                     start=i == 0 and part == 0, stop=i == HT - 1 and part == 1)
                if i == HT - 1:
                    done.up(last)

        def pe_second(pe, n, k, w):
            pe_hidden(pe, n, k, 0, w)

        def pe_third(pe, n, k, w):
            pe_hidden(pe, n, k, 1, w)

        def pe_out(pe, n, k, i):
            if i == 0:
                s_og.wait(pe, n - 1)
            s_a3.wait(pe, n, i + 1)
            for part in range(2):
                last = pe.matmul(pD[:, :], w3T[:, i * P:(i + 1) * P], a3[:, i, part, :],
                                 start=i == 0 and part == 0, stop=i == HT - 1 and part == 1)
            if i == HT - 1:
                s_o.up(last)

        def pe_back(pe, n, k):
            s_og.wait(pe, n)
            s_hf.wait(pe, n + 2)
            for t in range(T4):
                last = pe.transpose(pX[:, t * P:(t + 1) * P], og[:, t * P:(t + 1) * P], c.id32[:, :])
            s_oT.up(last)

        PE = ((-1, pe_out, 2), (-1, pe_out, 3), (1, pe_front), (0, pe_second, 2), (-1, pe_back),
              (0, pe_second, 3), (1, pe_first, 0), (0, pe_third, 0), (0, pe_third, 1), (1, pe_first, 1),
              (0, pe_third, 2), (0, pe_third, 3), (1, pe_first, 2), (1, pe_second, 0), (1, pe_second, 1),
              (0, pe_out, 0), (1, pe_first, 3), (0, pe_out, 1))

        @block.tensor
        def _(pe):
            weights.wait_halves(pe)
            turner.tensor(pe)
            turner.wait(pe)
            pipeline(pe, PE, RUNS)

        def dve_front(dve, n, k):
            s_xT.wait(dve, n - 1)
            for t in range(T4):
                last = normalise(dve, c, xn[:, t, :], n * T4 + t)
            s_xn.up(last)

        def dve_split_h(dve, n, k):
            s_hf.wait(dve, n)
            s_in.wait(dve, n - 1)
            split(dve, n, hx[:, 0, :], hx[:, 1, :], hf[:, :], s_hh, 1, s_hx)

        def split(dve, n, hi, lo, x, mid, k, done):
            mid.up(dve.tensor_copy(hi, x))
            mid.wait(dve, n, k)
            done.up(dve.tensor_tensor(lo, x, hi, ALU.subtract))

        def dve_gated(dve, n, k, j):
            s_th.wait(dve, n, j + 1)
            s_gf.up(dve.scalar_tensor_tensor(gf[:, :], th[:, :], 1.0, pA[:, :], ALU.add, ALU.mult))
            s_gf.wait(dve, n, j + 1)
            if j < 2:
                s_a1.wait(dve, n - 1, HT + j - 1)
            else:
                s_a1.wait(dve, n, j - 1)
            s_uf.up(dve.scalar_tensor_tensor(uf[j % 2][:, :], gf[:, :], s12[:, j:j + 1], pB[:, :], ALU.mult, ALU.mult))

        def dve_parts(dve, n, k, layer, o):
            ready, mid, done, a, reader = ((s_g2, s_h2, s_a2, a2, s_m3), (s_g3, s_h3, s_a3, a3, s_o))[layer]
            ready.wait(dve, n, o + 1)
            if o == 0:
                reader.wait(dve, n - 1)
            split(dve, n, a[:, o, 0, :], a[:, o, 1, :], ge[o % 3][:, :], mid, o + 1, done)

        def dve_add(dve, n, k):
            s_oT.wait(dve, n)
            xt = x_tiles(c, n * T4, T4)
            s_st.up(dve.tensor_tensor(xt, xt, pX[:, :].rearrange("p (t d) -> p t d", t=T4), ALU.add))

        def dve_second(dve, n, k, o):
            dve_parts(dve, n, k, 0, o)

        def dve_third(dve, n, k, o):
            dve_parts(dve, n, k, 1, o)

        DVE = ((1, dve_split_h), (0, dve_second, 0), (0, dve_second, 1), (0, dve_second, 2), (1, dve_gated, 0),
               (0, dve_second, 3), (1, dve_gated, 1), (2, dve_front), (0, dve_third, 0), (0, dve_third, 1),
               (0, dve_third, 2), (1, dve_gated, 2), (-1, dve_add), (0, dve_third, 3), (1, dve_gated, 3))

        @block.vector
        def _(dve):
            step = steps.on(dve)
            turner.vector(dve)
            weights.wait(dve)
            step(dve.tensor_scalar(s1h[:, :], sc["w1"][:, :], 0.5, None, ALU.mult))
            step(dve.tensor_tensor(s12[:, :], s1h[:, :], sc["w2"][:, :], ALU.mult))
            s_c.up(dve.tensor_scalar(gate[:, :], c.mod[:, 1, 5, :], sc3[:, 0:1], None, ALU.mult))
            s_c.wait(dve, 0)
            pipeline(dve, DVE, RUNS)

        def act_modulate(act, n, k):
            s_hh.wait(act, n - 1)
            s_hx.wait(act, n - 1)
            s_xT.wait_apart(act, n)
            for m in range(S2):
                last = act.activation(hf[:, m * N:(m + 1) * N], pX[:, m * N:(m + 1) * N], ACT.Identity,
                                      scale=c.mod[:, 1, 4, bass.ds(n * S2 + m, 1)],
                                      bias=c.mod[:, 1, 3, bass.ds(n * S2 + m, 1)])
            s_hf.up(last)

        def act_gate(act, n, k):
            s_oT.wait(act, n - 1)
            s_o.wait_apart(act, n)
            for m in range(S2):
                last = act.activation(og[:, m * N:(m + 1) * N], pD[:, m * N:(m + 1) * N], ACT.Copy,
                                      scale=gate[:, bass.ds(n * S2 + m, 1)])
            s_og.up(last)

        def act_tanh(act, n, k, j):
            s_in.wait(act, n, j + 1)
            s_gf.wait(act, n - 1 if j == 0 else n, HT if j == 0 else j)
            s_th.up(act.activation(th[:, :], pA[:, :], ACT.Tanh, scale=s1h[:, j:j + 1]))

        def act_hi(act, n, k, j):
            s_uf.wait(act, n, j + 1)
            if j == 0:
                s_m2.wait(act, n - 1)
            s_uh.up(act.activation(a1[:, j, 0, :], uf[j % 2][:, :], ACT.Copy))

        def act_gelu(act, n, k, layer, o):
            made, done, key = ((s_m2, s_g2, "h1"), (s_m3, s_g3, "h2"))[layer]
            made.wait(act, n, o + 1)
            u = o - 3
            if u >= 0:
                (s_a2, s_a3)[layer].wait(act, n, u + 1)
            elif layer:
                s_a2.wait(act, n)
            else:
                s_a3.wait(act, n - 1)
            done.up(act.activation(ge[o % 3][:, :], pH[o][:, :], ACT.Gelu, scale=sc[key][:, o:o + 1]))

        def act_second(act, n, k, o):
            act_gelu(act, n, k, 0, o)

        def act_third(act, n, k, o):
            act_gelu(act, n, k, 1, o)

        ACTS = ((0, act_hi, 3), (1, act_modulate), (0, act_second, 0), (0, act_second, 1), (0, act_second, 2),
                (1, act_tanh, 0), (0, act_second, 3), (1, act_tanh, 1), (1, act_hi, 0), (0, act_third, 0),
                (0, act_third, 1), (1, act_hi, 1), (0, act_third, 2), (1, act_tanh, 2), (0, act_third, 3),
                (1, act_hi, 2), (1, act_tanh, 3), (0, act_gate))

        @block.scalar
        def _(act):
            act.preload_act_table(ACT.Gelu)
            s_c.wait(act, 0)
            pipeline(act, ACTS, RUNS)

        def gp_lo(gp, n, k, j):
            s_uh.wait(gp, n, j + 1)
            s_a1.up(gp.tensor_tensor(a1[:, j, 1, :], uf[j % 2][:, :], a1[:, j, 0, :], ALU.subtract))

        GP = ((-1, gp_lo, 3), (0, gp_lo, 0), (0, gp_lo, 1), (0, gp_lo, 2))

        @block.gpsimd
        def _(gp):
            pipeline(gp, GP, RUNS)


def build(nc, ins, out):
    with ExitStack() as ctx:
        c = Core(nc, ctx)
        w0, w1, w2 = (get(nc, ctx, ins) for get in (attention0_weights, moe_weights, attention1_weights))
        setup(nc, c, ins, (w0, w1, w2))
        attention0(nc, c, w0)
        w3 = mlp_weights(nc, ctx, ins)
        moe(nc, c, w1, ahead=(w3,))
        attention1(nc, c, w2, ahead=(w3,))
        mlp(nc, c, w3, out)


def kernel(**inputs):
    import numpy as _np
    import concourse.bacc as _bacc
    from concourse.bass_utils import run_bass_kernel_spmd as _run

    nc = _bacc.Bacc("TRN2", target_bir_lowering=False, num_devices=1)
    arrays, ins = {}, {}
    for name, value in {**inputs, "rope": rope_tables()}.items():
        a = _np.ascontiguousarray(value)
        arrays[f"in_{name}_dram"] = a
        ins[name] = nc.dram_tensor(f"in_{name}_dram", a.shape, mybir.dt.from_np(a.dtype), kind="ExternalInput").ap()
    out = nc.dram_tensor("out_0_dram", (B, N, D), F32, kind="ExternalOutput").ap()
    build(nc, ins, out)
    r = _run(nc, [arrays], core_ids=[0])
    return r.results[0]["out_0_dram"]
```
